# Optimizing a Trainium2 kernel written in Bass

```python
import numpy as np
import jax
import jax.numpy as jnp

def _softmax(x, axis=-1):
    return jax.nn.softmax(x, axis=axis)

def _gelu(x):
    return jax.nn.gelu(x, approximate=True)

def _silu(x):
    return jax.nn.silu(x)

def _sigmoid(x):
    return jax.nn.sigmoid(x)

def _layernorm(x, axis=-1, eps=1e-05):
    m = jnp.mean(x, axis=axis, keepdims=True)
    v = jnp.var(x, axis=axis, keepdims=True)
    return (x - m) / jnp.sqrt(v + eps)

def _scatter_add(tgt, idx, src, axis=0):
    return tgt.at[idx].add(src)

def _segment_sum(src, seg, n):
    return jax.ops.segment_sum(src, seg, n)
kernel_name = 'mk_gnn_preln_d4_gnn_r32_75fcd3'

def setup_inputs(seed: int=0):
    np.random.seed(seed)
    _w = jnp.asarray

    def _rec_inputs():
        import jax
        import jax.numpy as jnp
        _gk = jax.random.key(seed)
        x = -0.000202 + 1 * jax.random.normal(jax.random.fold_in(_gk, 1), (3125, 128), jnp.float32)
        src = jax.random.randint(jax.random.fold_in(_gk, 2), (100000,), 0, 3125, jnp.int32)
        dst = jnp.minimum((3125 * jax.random.uniform(jax.random.fold_in(_gk, 3), (100000,)) ** 2.0).astype(jnp.int32), 99999)
        _o = jnp.argsort(dst, stable=True)
        src = src[_o]
        dst = dst[_o]
        edge_type_16 = jax.random.randint(jax.random.fold_in(_gk, 13), (100000,), 0, 16, jnp.int32)
        edge_weight = 0.00171547 + 0.999346 * jax.random.normal(jax.random.fold_in(_gk, 14), (100000,), jnp.float32)
        return (x, src, dst, edge_type_16, edge_weight)
    x, src, dst, edge_type_16, edge_weight = _rec_inputs()

    def _L0_gnn_setup():
        import jax, jax.numpy as jnp
        import numpy as np
        N = 50000
        E = 20000
        D = 128
        key = jax.random.key(seed)
        k1, k2, k3, k4 = jax.random.split(key, 4)
        feat = jax.random.normal(k1, (N, D), dtype=jnp.float32)
        edge_weight = jax.random.normal(k2, (E,), dtype=jnp.float32)
        src = jax.random.randint(k3, (E,), 0, N)
        dst = jax.random.randint(k4, (E,), 0, N)
        beta = jnp.ones((1,), dtype=jnp.float32)
        eps = jnp.zeros((1,), dtype=jnp.float32)
        return {'feat': feat, 'edge_weight': edge_weight, 'src': src, 'dst': dst, 'beta': beta, 'eps': eps}
    _L0_gnn_all = _L0_gnn_setup()
    _L0_gnn_in = {k: v for k, v in _L0_gnn_all.items() if k in ('beta', 'eps')}
    del _L0_gnn_all

    def _L1_gnn_setup():
        import jax, jax.numpy as jnp
        import numpy as np
        N_NODES = 3125
        N_EDGES = 50000
        D_FEAT = 128
        HEADS = 4
        C_OUT = 32
        NEG_SLOPE = 0.2

        def _glorot(key, shape):
            fan = shape[0] + shape[-1]
            s = jnp.sqrt(6.0 / fan)
            return jax.random.uniform(key, shape, jnp.float32, -s, s)

        def gat_layer(x, W, att_src, att_dst, bias, src, dst, n):
            H, C = att_src.shape
            h = (x @ W).reshape(n, H, C)
            a_src = jnp.einsum('nhc,hc->nh', h, att_src)
            a_dst = jnp.einsum('nhc,hc->nh', h, att_dst)
            e = jax.nn.leaky_relu(a_src[src] + a_dst[dst], NEG_SLOPE)
            m = jax.ops.segment_max(e, dst, num_segments=n)
            ex = jnp.exp(e - m[dst])
            denom = jax.ops.segment_sum(ex, dst, num_segments=n)
            alpha = ex / denom[dst]
            out = jax.ops.segment_sum(alpha[:, :, None] * h[src], dst, num_segments=n)
            return out.reshape(n, H * C) + bias
        key = jax.random.key(seed)
        ks = jax.random.split(key, 10)
        x = jax.random.normal(ks[0], (N_NODES, D_FEAT), jnp.float32)
        src = jax.random.randint(ks[1], (N_EDGES,), 0, N_NODES)
        off = jax.random.randint(ks[2], (N_EDGES,), 1, N_NODES)
        dst = (src + off) % N_NODES
        edge_index = jnp.stack([src, dst]).astype(jnp.int64)
        HC = HEADS * C_OUT
        params = dict(W1=_glorot(ks[3], (D_FEAT, HC)), att_src1=_glorot(ks[4], (HEADS, C_OUT)), att_dst1=_glorot(ks[5], (HEADS, C_OUT)), b1=jnp.zeros((HC,), jnp.float32), W2=_glorot(ks[6], (HC, HC)), att_src2=_glorot(ks[7], (HEADS, C_OUT)), att_dst2=_glorot(ks[8], (HEADS, C_OUT)), b2=jnp.zeros((HC,), jnp.float32))
        return dict(x=x, edge_index=edge_index, **params)
    _L1_gnn_all = _L1_gnn_setup()
    _L1_gnn_in = {k: v for k, v in _L1_gnn_all.items() if k in ('W1', 'att_src1', 'att_dst1', 'b1', 'W2', 'att_src2', 'att_dst2', 'b2')}
    del _L1_gnn_all

    def _L2_gnn_setup():
        import jax, jax.numpy as jnp
        import numpy as np
        N, D, E, L = (50000, 128, 50000, 3)
        EPS = 1e-05
        key = jax.random.key(seed)
        ks = jax.random.split(key, 6)
        x = jax.random.normal(ks[0], (N, D), dtype=jnp.float32)
        edge_index = jax.random.randint(ks[1], (2, E), 0, N, dtype=jnp.int64)
        edge_weight = jax.random.uniform(ks[2], (E,), dtype=jnp.float32)
        W = jax.random.normal(ks[3], (L, D, D), dtype=jnp.float32) * 0.05
        b = jnp.zeros((L, D), dtype=jnp.float32)
        gamma = jnp.ones((L, D), dtype=jnp.float32)
        beta = jnp.zeros((L, D), dtype=jnp.float32)
        return {'x': x, 'edge_index': edge_index, 'edge_weight': edge_weight, 'W': W, 'b': b, 'gamma': gamma, 'beta': beta}
    _L2_gnn_all = _L2_gnn_setup()
    _L2_gnn_in = {k: v for k, v in _L2_gnn_all.items() if k in ('W', 'b', 'gamma', 'beta')}
    del _L2_gnn_all

    def _L3_gnn_setup():
        import jax, jax.numpy as jnp
        import numpy as np
        N_NODES = 50000
        N_EDGES = 25000
        D_IN = 128
        D_HID = 128
        N_RELS = 16
        key = jax.random.key(seed)
        ks = jax.random.split(key, 7)
        node_feats = jax.random.normal(ks[0], (N_NODES, D_IN), dtype=jnp.float32)
        src = jax.random.randint(ks[1], (N_EDGES,), 0, N_NODES, dtype=jnp.int32)
        dst = jax.random.randint(ks[2], (N_EDGES,), 0, N_NODES, dtype=jnp.int32)
        edge_types = jax.random.randint(ks[3], (N_EDGES,), 0, N_RELS, dtype=jnp.int32)
        rel_weights = jax.random.normal(ks[4], (N_RELS, D_IN, D_HID), dtype=jnp.float32) / np.sqrt(D_IN)
        w_lin = jax.random.normal(ks[5], (D_IN, D_HID), dtype=jnp.float32) / np.sqrt(D_IN)
        b_lin = jax.random.normal(ks[6], (D_HID,), dtype=jnp.float32) * 0.01
        return {'node_feats': node_feats, 'src': src, 'dst': dst, 'edge_types': edge_types, 'rel_weights': rel_weights, 'w_lin': w_lin, 'b_lin': b_lin}
    _L3_gnn_all = _L3_gnn_setup()
    _L3_gnn_in = {k: v for k, v in _L3_gnn_all.items() if k in ('rel_weights', 'w_lin', 'b_lin')}
    del _L3_gnn_all
    return {'x': x, 'src': src, 'dst': dst, 'edge_type_16': edge_type_16, 'edge_weight': edge_weight, 'L0_gnn_beta': _L0_gnn_in['beta'], 'L0_gnn_eps': _L0_gnn_in['eps'], 'L1_gnn_W1': _L1_gnn_in['W1'], 'L1_gnn_att_src1': _L1_gnn_in['att_src1'], 'L1_gnn_att_dst1': _L1_gnn_in['att_dst1'], 'L1_gnn_b1': _L1_gnn_in['b1'], 'L1_gnn_W2': _L1_gnn_in['W2'], 'L1_gnn_att_src2': _L1_gnn_in['att_src2'], 'L1_gnn_att_dst2': _L1_gnn_in['att_dst2'], 'L1_gnn_b2': _L1_gnn_in['b2'], 'L2_gnn_W': _L2_gnn_in['W'], 'L2_gnn_b': _L2_gnn_in['b'], 'L2_gnn_gamma': _L2_gnn_in['gamma'], 'L2_gnn_beta': _L2_gnn_in['beta'], 'L3_gnn_rel_weights': _L3_gnn_in['rel_weights'], 'L3_gnn_w_lin': _L3_gnn_in['w_lin'], 'L3_gnn_b_lin': _L3_gnn_in['b_lin']}

def reference(x, src, dst, edge_type_16, edge_weight, L0_gnn_beta, L0_gnn_eps, L1_gnn_W1, L1_gnn_att_src1, L1_gnn_att_dst1, L1_gnn_b1, L1_gnn_W2, L1_gnn_att_src2, L1_gnn_att_dst2, L1_gnn_b2, L2_gnn_W, L2_gnn_b, L2_gnn_gamma, L2_gnn_beta, L3_gnn_rel_weights, L3_gnn_w_lin, L3_gnn_b_lin):
    import jax
    import jax.numpy as jnp

    def _L0_gnn_ref(feat, edge_weight, src, dst, beta, eps):
        import jax, jax.numpy as jnp
        import numpy as np
        N = 50000
        E = 20000
        D = 128
        n = feat.shape[0]
        norm = jnp.linalg.norm(feat, axis=-1, keepdims=True)
        norm_h = feat / jnp.maximum(norm, 1e-12)
        e = beta[0] * edge_weight
        seg_max = jax.ops.segment_max(e, src, num_segments=n)
        ex = jnp.exp(e - seg_max[src])
        seg_sum = jax.ops.segment_sum(ex, src, num_segments=n)
        p = ex / seg_sum[src]
        msg = norm_h[src] * p[:, None]
        h = jax.ops.segment_sum(msg, dst, num_segments=n)
        return (1.0 + eps[0]) * feat + h

    def _L1_gnn_ref(x, edge_index, W1, att_src1, att_dst1, b1, W2, att_src2, att_dst2, b2):
        import jax, jax.numpy as jnp
        import numpy as np
        N_NODES = 3125
        N_EDGES = 50000
        D_FEAT = 128
        HEADS = 4
        C_OUT = 32
        NEG_SLOPE = 0.2

        def _glorot(key, shape):
            fan = shape[0] + shape[-1]
            s = jnp.sqrt(6.0 / fan)
            return jax.random.uniform(key, shape, jnp.float32, -s, s)

        def gat_layer(x, W, att_src, att_dst, bias, src, dst, n):
            H, C = att_src.shape
            h = (x @ W).reshape(n, H, C)
            a_src = jnp.einsum('nhc,hc->nh', h, att_src)
            a_dst = jnp.einsum('nhc,hc->nh', h, att_dst)
            e = jax.nn.leaky_relu(a_src[src] + a_dst[dst], NEG_SLOPE)
            m = jax.ops.segment_max(e, dst, num_segments=n)
            ex = jnp.exp(e - m[dst])
            denom = jax.ops.segment_sum(ex, dst, num_segments=n)
            alpha = ex / denom[dst]
            out = jax.ops.segment_sum(alpha[:, :, None] * h[src], dst, num_segments=n)
            return out.reshape(n, H * C) + bias
        n = x.shape[0]
        loop = jnp.arange(n, dtype=edge_index.dtype)
        src = jnp.concatenate([edge_index[0], loop])
        dst = jnp.concatenate([edge_index[1], loop])
        h = gat_layer(x, W1, att_src1, att_dst1, b1, src, dst, n)
        h = jax.nn.elu(h)
        h = gat_layer(h, W2, att_src2, att_dst2, b2, src, dst, n)
        h = jax.nn.elu(h)
        return h

    def _L2_gnn_ref(x, edge_index, edge_weight, W, b, gamma, beta):
        import jax, jax.numpy as jnp
        import numpy as np
        N, D, E, L = (50000, 128, 50000, 3)
        EPS = 1e-05
        src, dst = (edge_index[0], edge_index[1])
        n = x.shape[0]
        deg = jax.ops.segment_sum(edge_weight, dst, num_segments=n)
        deg_safe = jnp.where(deg > 0, deg, 1.0)
        dinv = jnp.where(deg > 0, jax.lax.rsqrt(deg_safe), 0.0)
        norm = dinv[src] * edge_weight * dinv[dst]
        h = x
        h_last = None
        for l in range(W.shape[0]):
            xl = h @ W[l]
            msgs = norm[:, None] * xl[src]
            agg = jax.ops.segment_sum(msgs, dst, num_segments=n) + b[l]
            hr = agg if h_last is None else agg + h_last
            h_last = hr
            mean = hr.mean(axis=0)
            var = hr.var(axis=0)
            hn = (hr - mean) * jax.lax.rsqrt(var + EPS) * gamma[l] + beta[l]
            h = jax.nn.relu(hn)
        return h

    def _L3_gnn_ref(node_feats, src, dst, edge_types, rel_weights, w_lin, b_lin):
        import jax, jax.numpy as jnp
        import numpy as np
        N_NODES = 50000
        N_EDGES = 25000
        D_IN = 128
        D_HID = 128
        N_RELS = 16
        n = node_feats.shape[0]
        h_rel = jnp.einsum('ni,rih->rnh', node_feats, rel_weights)
        msg = h_rel[edge_types, src]
        msg_sum = jax.ops.segment_sum(msg, dst, num_segments=n)
        cnt = jax.ops.segment_sum(jnp.ones((msg.shape[0], 1), msg.dtype), dst, num_segments=n)
        node_msg = msg_sum / jnp.maximum(cnt, 1.0)
        return jnp.tanh(node_msg + node_feats @ w_lin + b_lin)
    edge_index = jnp.stack([src, dst])
    h = jnp.maximum(_layernorm(x, axis=-1), 0.0)
    x = x + _L0_gnn_ref(h, edge_weight, src, dst, L0_gnn_beta, L0_gnn_eps)
    h = jnp.maximum(_layernorm(x, axis=-1), 0.0)
    x = x + _L1_gnn_ref(h, edge_index, L1_gnn_W1, L1_gnn_att_src1, L1_gnn_att_dst1, L1_gnn_b1, L1_gnn_W2, L1_gnn_att_src2, L1_gnn_att_dst2, L1_gnn_b2)
    h = jnp.maximum(_layernorm(x, axis=-1), 0.0)
    x = x + _L2_gnn_ref(h, edge_index, edge_weight, L2_gnn_W, L2_gnn_b, L2_gnn_gamma, L2_gnn_beta)
    h = jnp.maximum(_layernorm(x, axis=-1), 0.0)
    x = x + _L3_gnn_ref(h, src, dst, edge_type_16, L3_gnn_rel_weights, L3_gnn_w_lin, L3_gnn_b_lin)
    return x

_drawn_inputs = setup_inputs


def setup_inputs(seed=0):
    import zlib

    import numpy as np

    out = dict(_drawn_inputs(seed))
    spreads = {'L1_gnn_b1': (0.0, 0.1),
     'L1_gnn_b2': (0.0, 0.1),
     'L2_gnn_b': (0.0, 0.8),
     'L2_gnn_gamma': (1.0, 0.2),
     'L2_gnn_beta': (0.0, 0.1)}
    factors = {'L1_gnn_att_dst1': 5.997,
     'L1_gnn_att_src2': 8.0,
     'L1_gnn_att_dst2': 8.0,
     'L3_gnn_b_lin': 8.0}
    for name, (base, spread) in spreads.items():
        noise = np.random.default_rng([zlib.crc32(name.encode()), seed]).standard_normal(out[name].shape)
        drawn = base * np.exp(spread * noise) if base else spread * noise
        out[name] = jnp.asarray(drawn.astype(out[name].dtype))
    for name, factor in factors.items():
        out[name] = (out[name] * factor).astype(out[name].dtype)
    return out
```

```python
from contextlib import ExitStack, contextmanager

import concourse.bass as bass
from concourse import mybir

FP32 = mybir.dt.float32
I32 = mybir.dt.int32
ALU = mybir.AluOpType
ACT = mybir.ActivationFunctionType
AX = mybir.AxisListType

P = 128
N_NODES, D = 3125, 128
N_EDGES = 100000
NT = -(-N_NODES // P)
NPAD = NT * P
LAST_ROWS = N_NODES - (NT - 1) * P
NC_ = -(-N_EDGES // P)
FULL_CHUNKS = N_EDGES // P
TAIL = N_EDGES - FULL_CHUNKS * P
CB = -(-NC_ // P)
NPAIRS = NC_ + NT - 1
U = 8
ITERS = -(-NPAIRS // U)
NPP = CB * P
HALF = U // 2
HEADS, HC = 4, 32
HW = HC + 1
GW = HEADS * HW
GROW = GW + HEADS
N_RELS = 16
EPS = 1e-5
BIG = 1e30
PAD_NODE = NPAD - 1
FAR = 1 << 20


class Chain:

    def __init__(self, eng, sem, base=0):
        self.eng, self.sem, self.n, self.base = eng, sem, 0, base

    def __call__(self, ins):
        self.n += 1
        ins.then_inc(self.sem, 1)
        self.eng.wait_ge(self.sem, self.base + self.n)


@contextmanager
def phase(nc):
    sems = []
    with ExitStack() as ctx:
        def give_back():
            for s in sems:
                nc.sync.sem_clear(s)
                nc.release_semaphore(s)

        ctx.callback(give_back)

        def sb(name, shape, dt=FP32):
            return ctx.enter_context(nc.sbuf_tensor(f"{name}_{nc.next_id()}", shape, dt))

        def ps(name, shape):
            return ctx.enter_context(nc.psum_tensor(f"{name}_{nc.next_id()}", shape, FP32))

        def sem(name, for_pool_dma=False):
            s = nc.alloc_semaphore(f"{name}_{nc.next_id()}")
            if not for_pool_dma:
                sems.append(s)
            return s

        yield sb, ps, sem, (lambda: ctx.enter_context(nc.Block()))


def bc(ap, n):
    return ap.unsqueeze(len(ap.shape)).to_broadcast([*ap.shape, n])


def mid(ap, n):
    return ap.unsqueeze(1).to_broadcast([ap.shape[0], n, ap.shape[1]])


def at(i, n=1):
    return bass.ds(i, n)


def setup(nc, a, m):
    with phase(nc) as (sb, ps, sem, block_):
        raw = [sb(f"raw{k}", [P, CB, P], I32) for k in range(3)]
        w_raw = sb("w_raw", [P, CB, P])
        rec = sb("rec", [P, CB, 4, P])
        ev = sb("ev", [P, CB, P])
        rec_pair = sb("rec_pair", [P, CB, 4 * P])
        ends = sb("ends", [1, NC_ - 1], I32)
        end_tile = sb("end_tile", [1, NC_ - 1], I32)
        keys = sb("keys", [1, NC_ - 1])
        chunk_no = sb("chunk_no", [1, NC_ - 1])
        keys_all = sb("keys_all", [P, NC_ - 1])
        below = sb("below", [P, NC_ - 1])
        jcol = sb("jcol", [P, CB])
        chunk_f = sb("chunk_f", [P, CB])
        chunk_i = sb("chunk_i", [P, CB], I32)
        tile_f = sb("tile_f", [P, CB])
        tile_128 = sb("tile_128", [P, CB])
        tile_cap = sb("tile_cap", [P, CB])
        tile_i = sb("tile_i", [P, CB], I32)
        hi_i = sb("hi_i", [P, NPP], I32)
        psum = ps("tp", [P, 2, 4, P])
        made, loaded, ends_in, cleared = sem("made"), sem("loaded"), sem("ends_in"), sem("cleared")
        keyed, spread = sem("keyed"), sem("spread")
        chunks_known, recs_in, pairs_in = sem("chunks_known"), sem("recs_in", True), sem("pairs_in")
        rec_ready, tile_ready, tile_out, row_in = sem("rec_ready"), sem("tile_ready"), sem("tile_out"), sem("row_in")
        stored, local, turned, taken, d_, b_in = sem("stored"), sem("local"), sem("turned"), sem("taken"), sem("d"), sem("b_in")
        block = block_()
        full = (CB - 1) * P * P
        rest = FULL_CHUNKS - (CB - 1) * P

        @block.gpsimd
        def _(pool):
            kw = dict(allow_small_or_imprecise_dtypes=True)
            nc.gpsimd.iota(m.iota[:, :], [[1, P]], 0, 0, **kw).then_inc(made, 1)
            nc.gpsimd.iota(m.pcol[:, :], [[0, 1]], 0, 1, **kw).then_inc(made, 1)
            nc.gpsimd.iota(m.rev[:, :], [[-1, P]], P, 0, **kw).then_inc(made, 1)
            nc.gpsimd.iota(m.revcol[:, :], [[0, U]], P, -1, **kw).then_inc(made, 1)
            nc.gpsimd.iota(jcol[:, :], [[P, CB]], 0, 1, **kw).then_inc(made, 1)
            nc.gpsimd.iota(chunk_no[:, :], [[1, NC_ - 1]], 0, 0, **kw).then_inc(made, 1)
            pool.wait_ge(keyed, 1)
            nc.gpsimd.partition_broadcast(keys_all[:, :], keys[:, :]).then_inc(spread, 1)
            pool.wait_ge(chunks_known, 1)
            pool.wait_ge(stored, 48)
            for b in range(CB):
                pool.indirect_dma_start(rec_pair[:, b, :], None, m.rec_dram[:, :],
                                        bass.IndirectOffsetOnAxis(ap=chunk_i[:, b:b + 1], axis=0)).then_inc(recs_in, 16)

        @block.sync
        def _(sp):
            with nc.allow_non_contiguous_dma(reason="the last destination of each chunk"):
                sp.dma_start(ends[:, :], a["dst"][0:(NC_ - 1) * P].rearrange("(o c e) -> o c e", o=1, e=P)[:, :, P - 1]).then_inc(ends_in, 16)
                sp.dma_start(m.beta[:, :], a["L0_gnn_beta"].rearrange("(o n) -> o n", o=1).to_broadcast([P, 1])).then_inc(b_in, 16)
                sp.dma_start(m.eps1[:, :], a["L0_gnn_eps"].rearrange("(o n) -> o n", o=1).to_broadcast([P, 1])).then_inc(b_in, 16)
            sp.wait_ge(cleared, 5)
            for name, tile in (("src", raw[0]), ("dst", raw[1]), ("edge_type_16", raw[2]), ("edge_weight", w_raw)):
                v = a[name]
                sp.dma_start(tile[:, 0:CB - 1, :], v[0:full].rearrange("(b c e) -> c b e", c=P, e=P)).then_inc(loaded, 16)
                sp.dma_start(tile[0:rest, CB - 1, :], v[full:FULL_CHUNKS * P].rearrange("(c e) -> c e", e=P)).then_inc(loaded, 16)
                sp.dma_start(tile[rest:rest + 1, CB - 1, 0:TAIL], v[FULL_CHUNKS * P:].rearrange("(c e) -> c e", c=1)).then_inc(loaded, 16)
            sp.dma_start(m.x[:, 0:NT - 1, :], a["x"][0:(NT - 1) * P, :].rearrange("(t p) f -> p t f", p=P)).then_inc(loaded, 16)
            sp.dma_start(m.x[0:LAST_ROWS, NT - 1, :], a["x"][(NT - 1) * P:, :]).then_inc(loaded, 16)
            sp.wait_ge(rec_ready, 1)
            sp.dma_start(m.rec_dram.rearrange("(b c) k -> c b k", c=P), rec[:, :, :, :].rearrange("p b k e -> p b (k e)")).then_inc(stored, 16)
            sp.dma_start(m.src_dram.rearrange("(b c e) -> c b e", c=P, e=P), rec[:, :, 0, :]).then_inc(stored, 16)
            sp.dma_start(m.ev_dram.rearrange("(b c e) -> c b e", c=P, e=P), ev[:, :, :]).then_inc(stored, 16)
            sp.wait_ge(tile_ready, 1)
            with nc.allow_non_contiguous_dma(reason="one number a pair"):
                sp.dma_start(m.tile_dram.rearrange("(b p) -> p b", p=P), tile_i[:, :]).then_inc(tile_out, 16)
            sp.wait_ge(tile_out, 16)
            sp.dma_start(m.tile_row[:, :], m.tile_dram.rearrange("(o j) -> o j", o=1)).then_inc(row_in, 16)
            sp.wait_ge(row_in, 16)
            sp.wait_ge(stored, 48)

        @block.vector
        def _(dve):
            v = nc.vector
            step = Chain(dve, d_)
            v.memset(raw[0][:, CB - 1, :], PAD_NODE).then_inc(cleared, 1)
            v.memset(raw[1][:, CB - 1, :], FAR).then_inc(cleared, 1)
            v.memset(raw[2][:, CB - 1, :], 0).then_inc(cleared, 1)
            v.memset(w_raw[:, CB - 1, :], 0.0).then_inc(cleared, 1)
            v.memset(m.x[:, NT - 1, :], 0.0).then_inc(cleared, 1)
            v.memset(m.w1[:, :, 1:2], 1.0)
            dve.wait_ge(made, 6)
            v.tensor_scalar(m.ident[:, :], m.iota[:, :], m.pcol[:, 0:1], None, ALU.is_equal)
            dve.wait_ge(ends_in, 16)
            step(v.tensor_scalar(end_tile[:, :], ends[:, :], 7, None, ALU.arith_shift_right))
            step(v.tensor_copy(keys[:, :], end_tile[:, :]))
            v.tensor_tensor(keys[:, :], keys[:, :], chunk_no[:, :], ALU.add).then_inc(keyed, 1)
            dve.wait_ge(loaded, 16 * 14)
            dve.wait_ge(b_in, 32)
            step(v.tensor_scalar(m.eps1[:, :], m.eps1[:, :], 1.0, None, ALU.add))
            step(v.tensor_copy(rec[:, :, 0, :], raw[0][:, :, :]))
            step(v.tensor_copy(rec[:, :, 1, :], raw[1][:, :, :]))
            step(v.tensor_copy(rec[:, :, 2, :], w_raw[:, :, :]))
            step(v.tensor_copy(rec[:, :, 3, :], raw[2][:, :, :]))
            step(v.tensor_scalar(ev[:, :, :], w_raw[:, :, :], m.beta[:, 0:1], None, ALU.mult))
            v.scalar_tensor_tensor(rec[:, :, 3, :], rec[:, :, 3, :], float(NPAD), rec[:, :, 0, :], ALU.mult, ALU.add).then_inc(rec_ready, 1)
            dve.wait_ge(spread, 1)
            for b in range(CB):
                step(v.tensor_scalar(below[:, :], keys_all[:, :], jcol[:, b:b + 1], None, ALU.is_lt, ALU.add, accum_out=chunk_f[:, b:b + 1]))
            v.tensor_copy(chunk_i[:, :], chunk_f[:, :]).then_inc(chunks_known, 1)
            step(v.tensor_tensor(tile_f[:, :], jcol[:, :], chunk_f[:, :], ALU.subtract))
            step(v.tensor_scalar(tile_128[:, :], tile_f[:, :], float(P), None, ALU.mult))
            step(v.tensor_scalar(tile_cap[:, :], tile_f[:, :], float(NT - 1), None, ALU.min))
            v.tensor_copy(tile_i[:, :], tile_cap[:, :]).then_inc(tile_ready, 1)
            dve.wait_ge(recs_in, 16 * CB)
            for b in range(CB):
                last = v.tensor_scalar(rec_pair[:, b, P:2 * P], rec_pair[:, b, P:2 * P], tile_128[:, b:b + 1], None, ALU.subtract)
                step(last)
            v.nop().then_inc(local, 1)
            for b in range(CB):
                dve.wait_ge(turned, 2 * b + 1)
                q = psum[:, 0, :, :]
                cols = slice(b * P, b * P + P)
                step(v.tensor_copy(m.src_pair[:, cols], q[:, 0, :]))
                step(v.tensor_copy(m.loc_pair[:, cols], q[:, 1, :]))
                step(v.tensor_copy(m.w1[:, cols, 0], q[:, 2, :]))
                step(v.tensor_copy(m.rel_pair[:, cols], q[:, 3, :]))
                v.tensor_scalar(m.ev_pair[:, cols], q[:, 2, :], m.beta[:, 0:1], None, ALU.mult).then_inc(taken, 1)
                dve.wait_ge(turned, 2 * b + 2)
                step(v.tensor_copy(m.src_col[:, cols], psum[:, 1, 0, :]))
                v.tensor_copy(m.ev_col[:, cols], psum[:, 1, 1, :]).then_inc(taken, 1)
            step(v.tensor_copy(hi_i[:, :], m.src_col[:, :]))
            step(v.tensor_scalar(hi_i[:, :], hi_i[:, :], 7, None, ALU.arith_shift_right))
            step(v.tensor_copy(m.hi_col[:, :], hi_i[:, :]))
            step(v.scalar_tensor_tensor(m.lo_col[:, :], m.hi_col[:, :], -float(P), m.src_col[:, :], ALU.mult, ALU.add))

        @block.tensor
        def _(pe):
            pe.wait_ge(local, 1)
            pe.wait_ge(rec_ready, 1)
            for b in range(CB):
                if b:
                    pe.wait_ge(taken, 2 * b - 1)
                for k in range(4):
                    last = nc.tensor.transpose(psum[:, 0, k, :], rec_pair[:, b, k * P:(k + 1) * P], m.ident[:, :])
                last.then_inc(turned, 1)
                if b:
                    pe.wait_ge(taken, 2 * b)
                nc.tensor.transpose(psum[:, 1, 0, :], rec[:, b, 0, :], m.ident[:, :])
                nc.tensor.transpose(psum[:, 1, 1, :], ev[:, b, :], m.ident[:, :]).then_inc(turned, 1)


def source_softmax(nc, m):
    blocks = -(-NC_ // U)
    blocks += blocks % 2
    with phase(nc) as (sb, ps, sem, block_):
        rows = [[sb(f"rows{b}{k}", [P, U, P]) for k in range(2)] for b in range(2)]
        differ, masked, onehot = sb("differ", [P, U, P]), sb("masked", [P, U, P]), sb("onehot", [P, U, P])
        masked2 = sb("masked2", [P, U, P])
        mx, first, is_first, below, ex = (sb(n, [P, U]) for n in ("mx", "first", "is_first", "below", "ex"))
        hi1 = sb("hi1", [P, U, NT])
        moved = sb("moved", [P, U, 3 * NT])
        chunk_max = sb("chunk_max", [P, U, NT])
        block_max, new_max, block_sum = sb("block_max", [P, NT]), sb("new_max", [P, NT]), sb("block_sum", [P, NT])
        gap, shrink = sb("gap", [P, U + 1, NT]), sb("shrink", [P, U + 1, NT])
        scaled = sb("scaled", [P, U, NT])
        psum = ps("node", [P, U, P])
        row_in = [sem("row_in0"), sem("row_in1")]
        rows_free, d_, gap1, exp1, gap2, exp2, ready, summed = (sem(n) for n in ("rows_free", "d", "gap1", "exp1", "gap2", "exp2", "ready", "summed"))
        block = block_()
        K = 20

        @block.sync
        def _(sp):
            with sp.Fori(0, blocks // 2) as i:
                for b in range(2):
                    blk = i * 2 + b
                    sp.wait_ge(rows_free, blk + 1)
                    sp.nop(nofuse=True)
                    for k, dram in enumerate((m.src_dram, m.ev_dram)):
                        sp.dma_start(rows[b][k][:, :, :].rearrange("p u e -> p (u e)"),
                                     dram[at(blk * (U * P), U * P)].unsqueeze(0).to_broadcast([P, U * P])).then_inc(row_in[b], 16)

        @block.vector
        def _(dve):
            v = nc.vector
            v.memset(m.seg_sum[:, :], 0.0)
            v.memset(m.seg_max[:, :], -BIG).then_inc(d_, 1)
            v.sem_inc(rows_free, 2)
            with dve.Fori(0, blocks // 2) as i:
                for b in range(2):
                    blk = i * 2 + b
                    step = Chain(dve, d_, blk * K + 1)
                    cols = at(blk * U, U)
                    srow, erow = rows[b][0][:, :, :], rows[b][1][:, :, :]
                    dve.wait_ge(row_in[b], i * 32 + 32)
                    step(v.tensor_tensor(differ[:, :, :], srow, bc(m.src_col[:, cols], P), ALU.not_equal))
                    step(v.scalar_tensor_tensor(masked[:, :, :], differ[:, :, :], -BIG, erow, ALU.mult, ALU.add))
                    v.sem_inc(rows_free, 1)
                    step(v.tensor_reduce(mx[:, :], masked[:, :, :], AX.X, ALU.max))
                    v.tensor_tensor(below[:, :], m.ev_col[:, cols], mx[:, :], ALU.subtract).then_inc(gap1, 1)
                    step(v.scalar_tensor_tensor(masked2[:, :, :], differ[:, :, :], -BIG, mid(m.rev[:, :], U), ALU.mult, ALU.add))
                    step(v.tensor_reduce(first[:, :], masked2[:, :, :], AX.X, ALU.max))
                    step(v.tensor_tensor(is_first[:, :], first[:, :], m.revcol[:, :], ALU.is_equal))
                    step(v.tensor_tensor(onehot[:, :, :], mid(m.iota[:, :], U), bc(m.lo_col[:, cols], P), ALU.is_equal))
                    step(v.tensor_tensor(hi1[:, :, :], mid(m.iota[:, 0:NT], U), bc(m.hi_col[:, cols], NT), ALU.is_equal))
                    step(v.tensor_tensor(moved[:, :, 2 * NT:], hi1[:, :, :], bc(is_first[:, :], NT), ALU.mult))
                    step(v.tensor_tensor(moved[:, :, NT:2 * NT], moved[:, :, 2 * NT:], bc(mx[:, :], NT), ALU.mult))
                    dve.wait_ge(exp1, blk + 1)
                    v.tensor_tensor(moved[:, :, 0:NT], hi1[:, :, :], bc(ex[:, :], NT), ALU.mult).then_inc(ready, 1)
                    dve.wait_ge(summed, blk + 1)
                    step(v.tensor_scalar(chunk_max[:, :, :], psum[:, :, 2 * NT:3 * NT], 1.0, BIG, ALU.subtract, ALU.mult))
                    step(v.tensor_tensor(chunk_max[:, :, :], chunk_max[:, :, :], psum[:, :, NT:2 * NT], ALU.add))
                    step(v.tensor_reduce(block_max[:, :], chunk_max[:, :, :].rearrange("p u h -> p h u"), AX.X, ALU.max))
                    step(v.tensor_tensor(new_max[:, :], m.seg_max[:, :], block_max[:, :], ALU.max))
                    step(v.tensor_tensor(gap[:, 0:U, :], chunk_max[:, :, :], mid(new_max[:, :], U), ALU.subtract))
                    v.tensor_tensor(gap[:, U, :], m.seg_max[:, :], new_max[:, :], ALU.subtract).then_inc(gap2, 1)
                    dve.wait_ge(exp2, blk + 1)
                    step(v.tensor_copy(m.seg_max[:, :], new_max[:, :]))
                    step(v.tensor_tensor(scaled[:, :, :], shrink[:, 0:U, :], psum[:, :, 0:NT], ALU.mult))
                    step(v.tensor_reduce(block_sum[:, :], scaled[:, :, :].rearrange("p u h -> p h u"), AX.X, ALU.add))
                    step(v.tensor_tensor(m.seg_sum[:, :], m.seg_sum[:, :], shrink[:, U, :], ALU.mult))
                    step(v.tensor_tensor(m.seg_sum[:, :], m.seg_sum[:, :], block_sum[:, :], ALU.add))
                    assert step.n == K, step.n

        @block.scalar
        def _(act):
            with act.Fori(0, blocks // 2) as i:
                for b in range(2):
                    blk = i * 2 + b
                    act.wait_ge(gap1, blk + 1)
                    nc.scalar.activation(ex[:, :], below[:, :], ACT.Exp).then_inc(exp1, 1)
                    act.wait_ge(gap2, blk + 1)
                    nc.scalar.activation(shrink[:, :, :], gap[:, :, :], ACT.Exp).then_inc(exp2, 1)

        @block.tensor
        def _(pe):
            with pe.Fori(0, blocks // 2) as i:
                for b in range(2):
                    pe.wait_ge(ready, i * 2 + b + 1)
                    for u in range(U):
                        last = nc.tensor.matmul(psum[:, u, 0:3 * NT], onehot[:, u, :], moved[:, u, :], start=True, stop=True)
                    last.then_inc(summed, 1)


def layernorm_relu(nc, m, out):
    with phase(nc) as (sb, ps, sem, block_):
        total, var = sb("total", [P, NT]), sb("var", [P, NT])
        sq = sb("sq", [P, NT, D])
        d_, var_ready, root = sem("d"), sem("var_ready"), sem("root")
        block = block_()

        @block.vector
        def _(dve):
            v = nc.vector
            step = Chain(dve, d_)
            step(v.tensor_reduce(total[:, :], m.x[:, :, :], AX.X, ALU.add))
            step(v.tensor_scalar(total[:, :], total[:, :], 1.0 / D, None, ALU.mult))
            step(v.tensor_tensor(out[:, :, 0:D], m.x[:, :, :], bc(total[:, :], D), ALU.subtract))
            step(v.tensor_tensor(sq[:, :, :], out[:, :, 0:D], out[:, :, 0:D], ALU.mult))
            step(v.tensor_reduce(var[:, :], sq[:, :, :], AX.X, ALU.add))
            v.tensor_scalar(var[:, :], var[:, :], 1.0 / D, EPS, ALU.mult, ALU.add).then_inc(var_ready, 1)
            dve.wait_ge(root, 1)
            step(v.reciprocal(var[:, :], var[:, :]))
            step(v.tensor_tensor(out[:, :, 0:D], out[:, :, 0:D], bc(var[:, :], D), ALU.mult))
            step(v.tensor_scalar(out[:, :, 0:D], out[:, :, 0:D], 0.0, None, ALU.max))

        @block.scalar
        def _(act):
            act.wait_ge(var_ready, 1)
            nc.scalar.activation(var[:, :], var[:, :], ACT.Sqrt).then_inc(root, 1)


def l0_table(nc, m):
    with phase(nc) as (sb, ps, sem, block_):
        sq, rows = sb("sq", [P, NT, D]), sb("rows", [P, NT, L0_ROW])
        norm, den = sb("norm", [P, NT]), sb("den", [P, NT])
        d_, n2, root, ready, out = sem("d"), sem("n2"), sem("root"), sem("ready"), sem("out")
        block = block_()

        @block.vector
        def _(dve):
            v = nc.vector
            step = Chain(dve, d_)
            step(v.tensor_tensor(sq[:, :, :], m.h[:, :, :], m.h[:, :, :], ALU.mult))
            step(v.tensor_reduce(norm[:, :], sq[:, :, :], AX.X, ALU.add))
            v.tensor_scalar(norm[:, :], norm[:, :], 1e-24, None, ALU.max).then_inc(n2, 1)
            step(v.tensor_scalar(den[:, :], m.seg_sum[:, :], 0.5, None, ALU.max))
            dve.wait_ge(root, 1)
            step(v.tensor_tensor(den[:, :], den[:, :], norm[:, :], ALU.mult))
            step(v.reciprocal(den[:, :], den[:, :]))
            step(v.tensor_scalar(rows[:, :, D], m.seg_max[:, :], -1.0, None, ALU.mult))
            step(v.memset(rows[:, :, D + 1:], 0.0))
            v.tensor_tensor(rows[:, :, 0:D], m.h[:, :, :], bc(den[:, :], D), ALU.mult).then_inc(ready, 1)

        @block.scalar
        def _(act):
            act.wait_ge(n2, 1)
            nc.scalar.activation(norm[:, :], norm[:, :], ACT.Sqrt).then_inc(root, 1)

        @block.sync
        def _(sp):
            sp.wait_ge(ready, 1)
            sp.dma_start(m.l0_dram.rearrange("(t p) w -> p t w", p=P), rows[:, :, :]).then_inc(out, 16)
            sp.wait_ge(out, 16)


L0_ROW = D + 2
DEPTH = 4


def gather_rows(nc, pool, m, table, width, ring, staged, fetched, freed):
    with pool.Fori(0, ITERS) as i:
        for u in range(U):
            if u % HALF == 0:
                pool.wait_ge(staged, (i * 2 + u // HALF + 1))
                pool.nop(nofuse=True)
            pool.wait_ge(freed, i * U + u + 1)
            pool.nop(nofuse=True)
            pool.indirect_dma_start(ring[:, u, 0:width], None, table[:, :],
                                    bass.IndirectOffsetOnAxis(ap=m.stage[:, u:u + 1], axis=0)).then_inc(fetched[u], 16)


def edge_sum(nc, m, table, width, index=None, onehot_weight=None, mode="plain"):
    with phase(nc) as (sb, ps, sem, block_):
        ring = sb("ring", [P, U, width])
        out_w = {"plain": D, "source": D + 2, "heads": GW}[mode]
        scaled = ring if mode == "plain" else sb("scaled", [P, U, out_w])
        onehot = sb("onehot", [P, U, P])
        p_src = sb("p_src", [P, U])
        psum = ps("part", [P, DEPTH, 512])
        gathers = mode != "heads"
        fetched = [sem(f"fetched{u}", gathers) for u in range(U)]
        staged, freed, weighed, hot, summed, added, scaled_a = (sem(n) for n in ("staged", "freed", "weighed", "hot", "summed", "added", "scaled_a"))
        block = block_()

        if gathers:
            @block.gpsimd
            def _(pool):
                gather_rows(nc, pool, m, table, width, ring, staged, fetched, freed)
        else:
            @block.sync
            def _(sp):
                with sp.Fori(0, ITERS) as i:
                    for u in range(U):
                        sp.wait_ge(freed, i * U + u + 1)
                        sp.nop(nofuse=True)
                        sp.dma_start(ring[:, u, :], table[at((i * U + u) * P, P), :]).then_inc(fetched[u], 16)

        if mode == "source":
            @block.scalar
            def _(act):
                with act.Fori(0, ITERS) as i:
                    for u in range(U):
                        j = i * U + u
                        act.wait_ge(fetched[u], i * 16 + 16)
                        act.nop(nofuse=True)
                        nc.scalar.activation(p_src[:, u:u + 1], m.ev_pair[:, at(j)], ACT.Exp, bias=ring[:, u, D:D + 1]).then_inc(weighed, 1)
                        act.wait_ge(summed, j + 1)
                        act.nop(nofuse=True)
                        nc.scalar.activation(scaled[:, u, D:D + 2], m.w1[:, at(j), :].rearrange("p o w -> p (o w)"), ACT.Copy)
                        act.wait_ge(weighed, j + 1)
                        act.nop(nofuse=True)
                        nc.scalar.activation(scaled[:, u, 0:D], ring[:, u, 0:D], ACT.Copy, scale=p_src[:, u:u + 1]).then_inc(scaled_a, 1)
                        

        @block.vector
        def _(dve):
            v = nc.vector

            def build(j, u):
                ins = v.tensor_scalar(onehot[:, u, :], m.iota[:, :], m.loc_pair[:, at(j)],
                                      onehot_weight[:, at(j), 0] if onehot_weight is not None else None,
                                      ALU.is_equal, ALU.mult if onehot_weight is not None else ALU.bypass)
                ins.then_inc(hot, 1)

            if gathers:
                for k in range(2):
                    v.tensor_copy(m.stage[:, k * HALF:(k + 1) * HALF], index[:, k * HALF:(k + 1) * HALF]).then_inc(staged, 1)
            v.sem_inc(freed, U)
            v.sem_inc(summed, U)
            v.sem_inc(added, DEPTH)
            for u in range(DEPTH):
                build(u, u)
            with dve.Fori(0, ITERS) as i:
                for u in range(U):
                    j = i * U + u
                    tile = dve.value_load(m.tile_row[0:1, at(j)], min_val=0, max_val=NT - 1)
                    if mode == "heads":
                        dve.wait_ge(fetched[u], i * 16 + 16)
                        dve.wait_ge(summed, j + 1)
                        v.tensor_tensor(scaled[:, u, :].rearrange("p (h c) -> p h c", h=HEADS),
                                        ring[:, u, 0:GW].rearrange("p (h c) -> p h c", h=HEADS),
                                        bc(m.ex_pair[:, at(j * HEADS, HEADS)], HW), ALU.mult).then_inc(scaled_a, 1)
                    dve.wait_ge(summed, j + 1 + U)
                    dve.wait_ge(added, j + DEPTH)
                    acc = m.acc[:, at(tile), 0:out_w].rearrange("p o w -> p (o w)")
                    v.tensor_tensor(acc, acc, psum[:, u % DEPTH, 0:out_w], ALU.add).then_inc(added, 1)
                    build(j + DEPTH, (u + DEPTH) % U)
                    if gathers and u % HALF == HALF - 1:
                        v.tensor_copy(m.stage[:, u - HALF + 1:u + 1], index[:, at(j + 1 + HALF, HALF)]).then_inc(staged, 1)

        @block.tensor
        def _(pe):
            with pe.Fori(0, ITERS) as i:
                for u in range(U):
                    j = i * U + u
                    if mode == "plain":
                        pe.wait_ge(fetched[u], i * 16 + 16)
                    else:
                        pe.wait_ge(scaled_a, j + 1)
                    pe.wait_ge(hot, j + 1)
                    pe.wait_ge(added, j + 1)
                    nc.tensor.matmul(psum[:, u % DEPTH, 0:out_w], onehot[:, u, :], scaled[:, u, 0:out_w],
                                     start=True, stop=True).then_inc(summed, 1)
                    pe.wait_ge(summed, j + 1 + U)
                    pe.sem_inc(freed, 1)


def gat_max(nc, m):
    with phase(nc) as (sb, ps, sem, block_):
        ring = sb("ring", [P, U, GROW])
        onehot = sb("onehot", [P, U, P])
        mask = sb("mask", [P, U, P])
        masked = sb("masked", [P, 2, HEADS, P])
        part = sb("part", [P, 2, HEADS])
        flipped = ps("flipped", [P, DEPTH, 512])
        spread = ps("spread", [P, DEPTH, HEADS, P])
        fetched = [sem(f"fetched{u}", True) for u in range(U)]
        stored = [sem(f"stored{u}") for u in range(U)]
        staged, freed, hot, flip, spr, mask_ok, mskd, red, kept, noted = (
            sem(n) for n in ("staged", "freed", "hot", "flip", "spr", "mask_ok", "mskd", "red", "kept", "noted"))
        block = block_()

        @block.gpsimd
        def _(pool):
            gather_rows(nc, pool, m, m.gat_dram, GROW, ring, staged, fetched, freed)

        @block.sync
        def _(sp):
            with sp.Fori(0, ITERS) as i:
                for u in range(U):
                    j = i * U + u
                    sp.wait_ge(fetched[u], i * 16 + 16)
                    sp.nop(nofuse=True)
                    sp.dma_start(m.rows_dram[at(j * P, P), :], ring[:, u, :]).then_inc(stored[u], 16)
                    if u:
                        sp.wait_ge(stored[u - 1], i * 16 + 16)
                        sp.nop(nofuse=True)
                        sp.wait_ge(spr, j)
                        sp.nop(nofuse=True)
                        sp.wait_ge(noted, j)
                        sp.nop(nofuse=True)
                        sp.sem_inc(freed, 1)
                sp.wait_ge(stored[U - 1], i * 16 + 16)
                sp.nop(nofuse=True)
                sp.wait_ge(spr, i * U + U)
                sp.nop(nofuse=True)
                sp.wait_ge(noted, i * U + U)
                sp.nop(nofuse=True)
                sp.sem_inc(freed, 1)

        @block.scalar
        def _(act):
            with act.Fori(0, ITERS) as i:
                for u in range(U):
                    j = i * U + u
                    act.wait_ge(flip, j + 1)
                    act.wait_ge(mskd, j + 1)
                    act.nop(nofuse=True)
                    nc.scalar.activation(mask[:, u, :], flipped[:, u % DEPTH, 0:P], ACT.Copy, scale=BIG, bias=-BIG).then_inc(mask_ok, 1)
                    act.wait_ge(fetched[u], i * 16 + 16)
                    act.nop(nofuse=True)
                    nc.scalar.activation(m.as_pair[:, at(j * HEADS, HEADS)], ring[:, u, GW:GROW], ACT.Copy).then_inc(noted, 1)

        @block.vector
        def _(dve):
            v = nc.vector

            def build(j, u):
                v.tensor_scalar(onehot[:, u, :], m.iota[:, :], m.loc_pair[:, at(j)], None, ALU.is_equal).then_inc(hot, 1)

            for k in range(2):
                v.tensor_copy(m.stage[:, k * HALF:(k + 1) * HALF], m.src_pair[:, k * HALF:(k + 1) * HALF]).then_inc(staged, 1)
            v.sem_inc(freed, U)
            v.sem_inc(mskd, U)
            v.sem_inc(kept, 2)
            for u in range(DEPTH):
                build(u, u)
            with dve.Fori(0, ITERS) as i:
                for u in range(U):
                    j = i * U + u
                    tile = dve.value_load(m.tile_row[0:1, at(j)], min_val=0, max_val=NT - 1)
                    dve.wait_ge(spr, j + 1)
                    dve.wait_ge(mask_ok, j + 1)
                    v.tensor_tensor(masked[:, u % 2, :, :], spread[:, u % DEPTH, :, :], mid(mask[:, u, :], HEADS), ALU.add).then_inc(mskd, 1)
                    build(j + DEPTH, (u + DEPTH) % U)
                    dve.wait_ge(mskd, j + 1 + U)
                    v.tensor_reduce(part[:, u % 2, :], masked[:, u % 2, :, :], AX.X, ALU.max).then_inc(red, 1)
                    dve.wait_ge(red, j + 1)
                    dve.wait_ge(kept, j + 2)
                    top = m.top[:, at(tile), :].rearrange("p o h -> p (o h)")
                    v.tensor_tensor(top, top, part[:, u % 2, :], ALU.max).then_inc(kept, 1)
                    if u % HALF == HALF - 1:
                        v.tensor_copy(m.stage[:, u - HALF + 1:u + 1], m.src_pair[:, at(j + 1 + HALF, HALF)]).then_inc(staged, 1)

        @block.tensor
        def _(pe):
            with pe.Fori(0, ITERS) as i:
                for u in range(U):
                    j = i * U + u
                    pe.wait_ge(hot, j + 1)
                    pe.wait_ge(mskd, j + 1 + U - DEPTH)
                    nc.tensor.transpose(flipped[:, u % DEPTH, 0:P], onehot[:, u, :], m.ident[:, :]).then_inc(flip, 1)
                    pe.wait_ge(fetched[u], i * 16 + 16)
                    for h in range(HEADS):
                        last = nc.tensor.matmul(spread[:, u % DEPTH, h, :], ring[:, u, GW + h:GW + h + 1].to_broadcast([P, P]),
                                                m.ident[:, :], start=True, stop=True)
                    last.then_inc(spr, 1)


def gat_expand(nc, m):
    with phase(nc) as (sb, ps, sem, block_):
        onehot, turned = sb("onehot", [P, U, P]), sb("turned", [P, U, P])
        flipped = ps("flipped", [P, DEPTH, 512])
        got = ps("got", [P, DEPTH, 512])
        hot, flip, turn, exp_, noted = (sem(n) for n in ("hot", "flip", "turn", "exp", "noted"))
        block = block_()

        @block.vector
        def _(dve):
            dve.sem_inc(exp_, U)
            with dve.Fori(0, ITERS) as i:
                for u in range(U):
                    dve.wait_ge(exp_, i * U + u + 1)
                    nc.vector.tensor_scalar(onehot[:, u, :], m.iota[:, :], m.loc_pair[:, at(i * U + u)], None, ALU.is_equal).then_inc(hot, 1)

        @block.scalar
        def _(act):
            act.sem_inc(noted, DEPTH)
            with act.Fori(0, ITERS) as i:
                for u in range(U):
                    j = i * U + u
                    act.wait_ge(flip, j + 1)
                    act.nop(nofuse=True)
                    nc.scalar.activation(turned[:, u, :], flipped[:, u % DEPTH, 0:P], ACT.Copy).then_inc(turn, 1)
                    act.wait_ge(exp_, j + 1 + U)
                    act.nop(nofuse=True)
                    nc.scalar.activation(m.am_pair[:, at(j * 2 * HEADS, 2 * HEADS)], got[:, u % DEPTH, 0:2 * HEADS], ACT.Copy).then_inc(noted, 1)

        @block.tensor
        def _(pe):
            with pe.Fori(0, ITERS) as i:
                for u in range(U):
                    j = i * U + u
                    tile = pe.value_load(m.tile_row[0:1, at(j)], min_val=0, max_val=NT - 1)
                    pe.wait_ge(hot, j + 1)
                    pe.wait_ge(noted, j + 1)
                    nc.tensor.transpose(flipped[:, u % DEPTH, 0:P], onehot[:, u, :], m.ident[:, :]).then_inc(flip, 1)
                    pe.wait_ge(turn, j + 1)
                    nc.tensor.matmul(got[:, u % DEPTH, 0:2 * HEADS], turned[:, u, :],
                                     m.am[:, at(tile), :].rearrange("p o h -> p (o h)"), start=True, stop=True).then_inc(exp_, 1)


def flip_nodes(nc, m, src, dst):
    with phase(nc) as (sb, ps, sem, block_):
        psum = ps("flip", [P, 2, 4, P])
        flipped, taken = sem("flipped"), sem("taken")
        block = block_()
        groups = [range(t, min(t + 4, NT)) for t in range(0, NT, 4)]

        @block.tensor
        def _(pe):
            for g, tiles in enumerate(groups):
                if g >= 2:
                    pe.wait_ge(taken, g - 1)
                for k, t in enumerate(tiles):
                    last = nc.tensor.transpose(psum[:, g % 2, k, :], src[:, t, 0:D], m.ident[:, :])
                last.then_inc(flipped, 1)

        @block.scalar
        def _(act):
            for g, tiles in enumerate(groups):
                act.wait_ge(flipped, g + 1)
                n = len(tiles)
                nc.scalar.activation(dst[:, tiles[0] * P:(tiles[0] + n) * P].rearrange("p (k e) -> p k e", k=n),
                                     psum[:, g % 2, 0:n, :], ACT.Copy).then_inc(taken, 1)


def project(nc, m, weight, out, scale=None):
    with phase(nc) as (sb, ps, sem, block_):
        w = sb("w", [P, D])
        psum = ps("proj", [P, 4, 512])
        w_in, done, taken = sem("w_in"), sem("done"), sem("taken")
        block = block_()

        @block.sync
        def _(sp):
            sp.dma_start(w[:, :], weight).then_inc(w_in, 16)

        @block.tensor
        def _(pe):
            pe.wait_ge(w_in, 16)
            for t in range(NT):
                if t >= 4:
                    pe.wait_ge(taken, t - 3)
                nc.tensor.matmul(psum[:, t % 4, 0:D], m.hT[:, t * P:(t + 1) * P], w[:, :], start=True, stop=True).then_inc(done, 1)

        @block.scalar
        def _(act):
            for t in range(NT):
                act.wait_ge(done, t + 1)
                kw = {} if scale is None else {"scale": scale[:, t:t + 1]}
                nc.scalar.activation(out[:, t, 0:D], psum[:, t % 4, 0:D], ACT.Copy, **kw).then_inc(taken, 1)


def store_table(nc, table, rows):
    with phase(nc) as (sb, ps, sem, block_):
        out = sem("out")
        block = block_()

        @block.sync
        def _(sp):
            sp.dma_start(table.rearrange("(t p) w -> p t w", p=P), rows).then_inc(out, 16)
            sp.wait_ge(out, 16)


def row_of(v):
    return v.unsqueeze(0).to_broadcast([P, v.shape[0]])


def l0_finish(nc, m):
    with phase(nc) as (sb, ps, sem, block_):
        pos, safe = sb("pos", [P, NT]), sb("safe", [P, NT])
        d_, ready, root = sem("d"), sem("ready"), sem("root")
        block = block_()

        @block.vector
        def _(dve):
            v = nc.vector
            step = Chain(dve, d_)
            step(v.tensor_copy(m.dinv[:, :], m.acc[:, :, D]))
            step(v.tensor_scalar(m.cnt_inv[:, :], m.acc[:, :, D + 1], 1.0, None, ALU.max))
            step(v.reciprocal(m.cnt_inv[:, :], m.cnt_inv[:, :]))
            step(v.tensor_scalar(pos[:, :], m.dinv[:, :], 0.0, None, ALU.is_gt))
            step(v.tensor_tensor(safe[:, :], m.dinv[:, :], pos[:, :], ALU.mult))
            step(v.tensor_tensor(safe[:, :], safe[:, :], pos[:, :], ALU.subtract))
            v.tensor_scalar(safe[:, :], safe[:, :], 1.0, None, ALU.add).then_inc(ready, 1)
            dve.wait_ge(root, 1)
            step(v.reciprocal(safe[:, :], safe[:, :]))
            step(v.tensor_tensor(m.dinv[:, :], safe[:, :], pos[:, :], ALU.mult))
            step(v.scalar_tensor_tensor(m.x[:, :, :], m.h[:, :, :], m.eps1[:, 0:1], m.x[:, :, :], ALU.mult, ALU.add))
            step(v.tensor_tensor(m.x[:, :, :], m.x[:, :, :], m.acc[:, :, 0:D], ALU.add))

        @block.scalar
        def _(act):
            act.wait_ge(ready, 1)
            nc.scalar.activation(safe[:, :], safe[:, :], ACT.Sqrt).then_inc(root, 1)


def clear_acc(nc, m):
    with phase(nc) as (sb, ps, sem, block_):
        block = block_()

        @block.vector
        def _(dve):
            nc.vector.memset(m.acc[:, :, :], 0.0)


def gat_layer(nc, m, weight, att_src, att_dst, bias):
    flip_nodes(nc, m, m.h, m.hT)
    rows = m.acc2
    with phase(nc) as (sb0, ps0, sem0, block0):
        hw = sb0("hw", [P, NT, D])
        project(nc, m, weight, hw)
        with phase(nc) as (sb, ps, sem, block_):
            att = [sb(f"att{k}", [P, D]) for k in range(2)]
            prod = sb("prod", [P, NT, D])
            att_in, d_ = sem("att_in"), sem("d")
            block = block_()

            @block.sync
            def _(sp):
                for k, v in enumerate((att_src, att_dst)):
                    sp.dma_start(att[k][:, :], row_of(v.rearrange("h c -> (h c)"))).then_inc(att_in, 16)

            @block.vector
            def _(dve):
                v = nc.vector
                step = Chain(dve, d_)
                dve.wait_ge(att_in, 32)
                for k, o in enumerate((m.a_src, m.a_dst)):
                    step(v.tensor_tensor(prod[:, :, :], hw[:, :, :], mid(att[k][:, :], NT), ALU.mult))
                    step(v.tensor_reduce(o[:, :, :], prod[:, :, :].rearrange("p t (h c) -> p t h c", h=HEADS), AX.X, ALU.add))
                step(v.tensor_copy(m.top[:, :, :], m.a_src[:, :, :]))
                step(v.tensor_copy(rows[:, :, GW:GROW], m.a_src[:, :, :]))
                for h in range(HEADS):
                    step(v.tensor_copy(rows[:, :, h * HW:h * HW + HC], hw[:, :, h * HC:(h + 1) * HC]))
                    step(v.memset(rows[:, :, h * HW + HC:(h + 1) * HW], 1.0))
    store_table(nc, m.gat_dram, rows[:, :, 0:GROW])
    gat_max(nc, m)
    with phase(nc) as (sb, ps, sem, block_):
        tmp, own = sb("tmp", [P, NT, HEADS]), sb("own", [P, NT, HEADS])
        d_, ready, exped = sem("d"), sem("ready"), sem("exped")
        block = block_()

        @block.vector
        def _(dve):
            v = nc.vector
            step = Chain(dve, d_)
            step(v.tensor_copy(m.am[:, :, 0:HEADS], m.a_dst[:, :, :]))
            step(v.tensor_tensor(tmp[:, :, :], m.top[:, :, :], m.a_dst[:, :, :], ALU.add))
            step(v.scalar_tensor_tensor(m.am[:, :, HEADS:], tmp[:, :, :], 0.2, tmp[:, :, :], ALU.mult, ALU.max))
            step(v.tensor_tensor(tmp[:, :, :], m.a_src[:, :, :], m.a_dst[:, :, :], ALU.add))
            step(v.scalar_tensor_tensor(own[:, :, :], tmp[:, :, :], 0.2, tmp[:, :, :], ALU.mult, ALU.max))
            v.tensor_tensor(own[:, :, :], own[:, :, :], m.am[:, :, HEADS:], ALU.subtract).then_inc(ready, 1)
            dve.wait_ge(exped, 1)
            for h in range(HEADS):
                cols = slice(h * HW, (h + 1) * HW)
                step(v.tensor_tensor(m.acc[:, :, cols], rows[:, :, cols], bc(tmp[:, :, h], HW), ALU.mult))

        @block.scalar
        def _(act):
            act.wait_ge(ready, 1)
            nc.scalar.activation(tmp[:, :, :], own[:, :, :], ACT.Exp).then_inc(exped, 1)
    gat_expand(nc, m)
    with phase(nc) as (sb, ps, sem, block_):
        d_, ready, exped = sem("d"), sem("ready"), sem("exped")
        block = block_()
        n = NPAIRS_PAD
        asp = m.as_pair[:, 0:n * HEADS].rearrange("p (j h) -> p j h", h=HEADS)
        exp_ = m.ex_pair[:, 0:n * HEADS].rearrange("p (j h) -> p j h", h=HEADS)
        amp = m.am_pair[:, 0:n * 2 * HEADS].rearrange("p (j h) -> p j h", h=2 * HEADS)

        @block.vector
        def _(dve):
            v = nc.vector
            step = Chain(dve, d_)
            step(v.tensor_tensor(asp, asp, amp[:, :, 0:HEADS], ALU.add))
            step(v.scalar_tensor_tensor(exp_, asp, 0.2, asp, ALU.mult, ALU.max))
            step(v.tensor_tensor(exp_, exp_, amp[:, :, HEADS:], ALU.subtract))
            v.tensor_scalar(exp_, exp_, 0.0, None, ALU.min).then_inc(ready, 1)

        @block.scalar
        def _(act):
            act.wait_ge(ready, 1)
            nc.scalar.activation(exp_, exp_, ACT.Exp).then_inc(exped, 1)
    edge_sum(nc, m, m.rows_dram, GROW, mode="heads")
    with phase(nc) as (sb, ps, sem, block_):
        b_row, neg = sb("b_row", [P, D]), sb("neg", [P, NT, D])
        b_in, d_, ready, exped = sem("b_in"), sem("d"), sem("ready"), sem("exped")
        block = block_()

        @block.sync
        def _(sp):
            sp.dma_start(b_row[:, :], row_of(bias)).then_inc(b_in, 16)

        @block.vector
        def _(dve):
            v = nc.vector
            step = Chain(dve, d_)
            for h in range(HEADS):
                den = m.acc[:, :, h * HW + HC]
                step(v.reciprocal(den, den))
                step(v.tensor_tensor(m.h[:, :, h * HC:(h + 1) * HC], m.acc[:, :, h * HW:h * HW + HC], bc(den, HC), ALU.mult))
            dve.wait_ge(b_in, 16)
            step(v.tensor_tensor(m.h[:, :, :], m.h[:, :, :], mid(b_row[:, :], NT), ALU.add))
            v.tensor_scalar(neg[:, :, :], m.h[:, :, :], 0.0, None, ALU.min).then_inc(ready, 1)
            dve.wait_ge(exped, 1)
            step(v.tensor_scalar(neg[:, :, :], neg[:, :, :], -1.0, None, ALU.add))
            step(v.scalar_tensor_tensor(m.h[:, :, :], m.h[:, :, :], 0.0, neg[:, :, :], ALU.max, ALU.add))

        @block.scalar
        def _(act):
            act.wait_ge(ready, 1)
            nc.scalar.activation(neg[:, :, :], neg[:, :, :], ACT.Exp).then_inc(exped, 1)


NPAIRS_PAD = ITERS * U


def add_to_x(nc, m, src):
    with phase(nc) as (sb, ps, sem, block_):
        block = block_()

        @block.vector
        def _(dve):
            nc.vector.tensor_tensor(m.x[:, :, :], m.x[:, :, :], src, ALU.add)


def gcn_layer(nc, m, l, weight, b, gamma, beta):
    project(nc, m, weight, m.acc2, scale=m.dinv)
    store_table(nc, m.gcn_dram[l], m.acc2[:, :, 0:D])
    clear_acc(nc, m)
    edge_sum(nc, m, m.gcn_dram[l], D, index=m.src_pair, onehot_weight=m.w1)
    with phase(nc) as (sb, ps, sem, block_):
        d_ = sem("d")
        block = block_()

        @block.vector
        def _(dve):
            nc.vector.tensor_tensor(m.acc[:, :, 0:D], m.acc[:, :, 0:D], bc(m.dinv[:, :], D), ALU.mult).then_inc(d_, 1)
    flip_nodes(nc, m, m.acc, m.hT)
    with phase(nc) as (sb, ps, sem, block_):
        par = sb("par", [P, 3])
        pieces = [(s, min(s + 512, N_NODES)) for s in range(0, N_NODES, 512)]
        stats, mv = sb("stats", [P, len(pieces), 6]), sb("mv", [P, 2])
        scale, shift = sb("scale", [P, 1]), sb("shift", [P, 1])
        p_in, d_, var_ready, root = sem("p_in"), sem("d"), sem("var_ready"), sem("root")
        block = block_()

        @block.sync
        def _(sp):
            with nc.allow_non_contiguous_dma(reason="a number a partition"):
                for k, v in enumerate((b, gamma, beta)):
                    sp.dma_start(par[:, k:k + 1], v.unsqueeze(1)).then_inc(p_in, 16)

        @block.vector
        def _(dve):
            v = nc.vector
            step = Chain(dve, d_)
            dve.wait_ge(p_in, 48)
            if l == 0:
                step(v.tensor_scalar(m.lastT[:, :], m.hT[:, :], par[:, 0:1], None, ALU.add))
            else:
                step(v.scalar_tensor_tensor(m.lastT[:, :], m.hT[:, :], par[:, 0:1], m.lastT[:, :], ALU.add, ALU.add))
            for k, (s, e) in enumerate(pieces):
                step(v.bn_stats(stats[:, k, :], m.lastT[:, s:e]))
            step(v.bn_aggr(mv[:, :], stats[:, :, :].rearrange("p k s -> p (k s)")))
            v.tensor_scalar(scale[:, :], mv[:, 1:2], EPS, None, ALU.add).then_inc(var_ready, 1)
            dve.wait_ge(root, 1)
            step(v.reciprocal(scale[:, :], scale[:, :]))
            step(v.tensor_tensor(scale[:, :], scale[:, :], par[:, 1:2], ALU.mult))
            step(v.tensor_scalar(m.hT[:, :], m.lastT[:, :], mv[:, 0:1], scale[:, 0:1], ALU.subtract, ALU.mult))
            step(v.tensor_scalar(m.hT[:, :], m.hT[:, :], par[:, 2:3], 0.0, ALU.add, ALU.max))

        @block.scalar
        def _(act):
            act.wait_ge(var_ready, 1)
            nc.scalar.activation(scale[:, :], scale[:, :], ACT.Sqrt).then_inc(root, 1)


def rgcn_table(nc, m, rel_weights):
    with phase(nc) as (sb, ps, sem, block_):
        w = sb("w", [P, N_RELS, D])
        rows = sb("rows", [P, 2, N_RELS, D])
        psum = ps("rel", [P, 2, 4, 512])
        w_in, done, taken = sem("w_in"), sem("done"), sem("taken")
        out = [sem("out0"), sem("out1")]
        block = block_()
        table = m.rel_dram.rearrange("(r t p) f -> t p r f", r=N_RELS, p=P)

        @block.sync
        def _(sp):
            sp.dma_start(w[:, :, :], rel_weights.rearrange("r i h -> i r h")).then_inc(w_in, 16)
            for t in range(NT):
                sp.wait_ge(taken, 4 * (t + 1))
                sp.dma_start(table[t], rows[:, t % 2, :, :]).then_inc(out[t % 2], 16)
            for k in range(2):
                sp.wait_ge(out[k], 16 * ((NT + 1 - k) // 2))

        @block.tensor
        def _(pe):
            pe.wait_ge(w_in, 16)
            for t in range(NT):
                for g in range(4):
                    if t >= 2:
                        pe.wait_ge(taken, 4 * (t - 2) + g + 1)
                    nc.tensor.matmul(psum[:, t % 2, g, :], m.hT[:, t * P:(t + 1) * P],
                                     w[:, 4 * g:4 * g + 4, :].rearrange("p r f -> p (r f)"), start=True, stop=True).then_inc(done, 1)

        @block.scalar
        def _(act):
            for t in range(NT):
                if t >= 2:
                    act.wait_ge(out[t % 2], 16 * (t // 2))
                for g in range(4):
                    act.wait_ge(done, 4 * t + g + 1)
                    nc.scalar.activation(rows[:, t % 2, 4 * g:4 * g + 4, :].rearrange("p r f -> p (r f)"),
                                         psum[:, t % 2, g, :], ACT.Copy).then_inc(taken, 1)


def rgcn_finish(nc, m, b_lin, out_dram):
    with phase(nc) as (sb, ps, sem, block_):
        b_row = sb("b_row", [P, D])
        b_in, d_, ready, tanhed, final, out = (sem(n) for n in ("b_in", "d", "ready", "tanhed", "final", "out"))
        block = block_()

        @block.sync
        def _(sp):
            sp.dma_start(b_row[:, :], row_of(b_lin)).then_inc(b_in, 16)
            sp.wait_ge(final, 1)
            sp.dma_start(out_dram[0:(NT - 1) * P, :].rearrange("(t p) f -> p t f", p=P), m.x[:, 0:NT - 1, :]).then_inc(out, 16)
            sp.dma_start(out_dram[(NT - 1) * P:, :], m.x[0:LAST_ROWS, NT - 1, :]).then_inc(out, 16)
            sp.wait_ge(out, 32)

        @block.vector
        def _(dve):
            v = nc.vector
            step = Chain(dve, d_)
            step(v.tensor_tensor(m.acc[:, :, 0:D], m.acc[:, :, 0:D], bc(m.cnt_inv[:, :], D), ALU.mult))
            step(v.tensor_tensor(m.acc[:, :, 0:D], m.acc[:, :, 0:D], m.acc2[:, :, 0:D], ALU.add))
            dve.wait_ge(b_in, 16)
            v.tensor_tensor(m.acc[:, :, 0:D], m.acc[:, :, 0:D], mid(b_row[:, :], NT), ALU.add).then_inc(ready, 1)
            dve.wait_ge(tanhed, 1)
            v.tensor_tensor(m.x[:, :, :], m.x[:, :, :], m.acc[:, :, 0:D], ALU.add).then_inc(final, 1)

        @block.scalar
        def _(act):
            act.wait_ge(ready, 1)
            nc.scalar.activation(m.acc[:, :, 0:D], m.acc[:, :, 0:D], ACT.Tanh).then_inc(tanhed, 1)


class Memory:
    pass


def gnn_kernel(nc, a, out_dram, stop=99):
    m = Memory()
    with ExitStack() as ctx:
        def sb(name, shape, dt=FP32):
            return ctx.enter_context(nc.sbuf_tensor(name, shape, dt))

        m.iota, m.rev, m.ident = sb("iota", [P, P]), sb("rev", [P, P]), sb("ident", [P, P])
        m.pcol, m.revcol = sb("pcol", [P, 1]), sb("revcol", [P, U])
        m.beta, m.eps1 = sb("beta", [P, 1]), sb("eps1", [P, 1])
        m.x, m.h = sb("x", [P, NT, D]), sb("h", [P, NT, D])
        m.acc, m.acc2 = sb("acc", [P, NT, GROW]), sb("acc2", [P, NT, GROW])
        m.dinv, m.cnt_inv = sb("dinv", [P, NT]), sb("cnt_inv", [P, NT])
        m.src_pair, m.rel_pair = sb("src_pair", [P, NPP], I32), sb("rel_pair", [P, NPP], I32)
        m.loc_pair, m.w1 = sb("loc_pair", [P, NPP]), sb("w1", [P, NPP, 2])
        m.tile_row = sb("tile_row", [1, NPP], I32)
        m.stage = sb("stage", [P, U], I32)
        def dram(name, shape, dt=FP32):
            return nc.dram_tensor(name, shape, dt, kind="Internal").ap()

        m.rec_dram, m.src_dram, m.ev_dram = dram("rec_dram", [NPP, 4 * P]), dram("src_dram", [NPP * P]), dram("ev_dram", [NPP * P])
        m.l0_dram, m.gat_dram = dram("l0_dram", [NPAD, L0_ROW]), dram("gat_dram", [NPAD, GROW])
        m.rows_dram, m.rel_dram = dram("rows_dram", [NPAIRS_PAD * P, GROW]), dram("rel_dram", [N_RELS * NPAD, D])
        m.gcn_dram = [dram(f"gcn_dram{l}", [NPAD, D]) for l in range(3)]
        m.tile_dram = dram("tile_dram", [NPP], I32)

        with ExitStack() as early:
            def sb0(name, shape):
                return early.enter_context(nc.sbuf_tensor(name, shape, FP32))

            m.src_col, m.ev_col, m.hi_col, m.lo_col = (sb0(n, [P, NPP]) for n in ("src_col", "ev_col", "hi_col", "lo_col"))
            m.ev_pair = sb0("ev_pair", [P, NPP])
            m.seg_max, m.seg_sum = sb0("seg_max", [P, NT]), sb0("seg_sum", [P, NT])
            setup(nc, a, m)
            source_softmax(nc, m)
            layernorm_relu(nc, m, m.h)
            l0_table(nc, m)
            clear_acc(nc, m)
            edge_sum(nc, m, m.l0_dram, L0_ROW, index=m.src_pair, mode="source")
            l0_finish(nc, m)

        m.hT = sb("hT", [P, NPAD])
        if stop > 1:
            with ExitStack() as middle:
                def sb1(name, shape):
                    return middle.enter_context(nc.sbuf_tensor(name, shape, FP32))

                m.a_src, m.a_dst, m.top = (sb1(n, [P, NT, HEADS]) for n in ("a_src", "a_dst", "top"))
                m.am = sb1("am", [P, NT, 2 * HEADS])
                m.as_pair, m.ex_pair = sb1("as_pair", [P, NPP * HEADS]), sb1("ex_pair", [P, NPP * HEADS])
                m.am_pair = sb1("am_pair", [P, NPP * 2 * HEADS])
                layernorm_relu(nc, m, m.h)
                gat_layer(nc, m, a["L1_gnn_W1"], a["L1_gnn_att_src1"], a["L1_gnn_att_dst1"], a["L1_gnn_b1"])
                gat_layer(nc, m, a["L1_gnn_W2"], a["L1_gnn_att_src2"], a["L1_gnn_att_dst2"], a["L1_gnn_b2"])
                add_to_x(nc, m, m.h[:, :, :])

        if stop > 2:
            with ExitStack() as late:
                m.lastT = late.enter_context(nc.sbuf_tensor("lastT", [P, NPAD], FP32))
                layernorm_relu(nc, m, m.h)
                flip_nodes(nc, m, m.h, m.hT)
                for l in range(3):
                    gcn_layer(nc, m, l, a["L2_gnn_W"][l], a["L2_gnn_b"][l], a["L2_gnn_gamma"][l], a["L2_gnn_beta"][l])
                flip_nodes(nc, m, m.hT[:, :].rearrange("p (t n) -> p t n", t=NT), m.h[:, :, :].rearrange("p t f -> p (t f)"))
                add_to_x(nc, m, m.h[:, :, :])

        layernorm_relu(nc, m, m.h)
        flip_nodes(nc, m, m.h, m.hT)
        rgcn_table(nc, m, a["L3_gnn_rel_weights"])
        project(nc, m, a["L3_gnn_w_lin"], m.acc2)
        clear_acc(nc, m)
        if stop > 3:
            edge_sum(nc, m, m.rel_dram, D, index=m.rel_pair)
        rgcn_finish(nc, m, a["L3_gnn_b_lin"], out_dram)


_INS = ['x', 'src', 'dst', 'edge_type_16', 'edge_weight', 'L0_gnn_beta', 'L0_gnn_eps', 'L1_gnn_W1', 'L1_gnn_att_src1',
        'L1_gnn_att_dst1', 'L1_gnn_b1', 'L1_gnn_W2', 'L1_gnn_att_src2', 'L1_gnn_att_dst2', 'L1_gnn_b2', 'L2_gnn_W',
        'L2_gnn_b', 'L2_gnn_gamma', 'L2_gnn_beta', 'L3_gnn_rel_weights', 'L3_gnn_w_lin', 'L3_gnn_b_lin']


def kernel(**inputs):
    import numpy as _np
    import concourse.bacc as _bacc
    from concourse import mybir as _mybir
    from concourse.bass_utils import run_bass_kernel_spmd as _run

    nc = _bacc.Bacc("TRN2", target_bir_lowering=False, num_devices=1)
    arrays, args = {}, {}
    for name in _INS:
        v = _np.ascontiguousarray(inputs[name])
        arrays[f"in_{name}"] = v
        args[name] = nc.dram_tensor(f"in_{name}", v.shape, _mybir.dt.from_np(v.dtype), kind="ExternalInput").ap()
    out = nc.dram_tensor("out_x", (N_NODES, D), FP32, kind="ExternalOutput").ap()
    gnn_kernel(nc, args, out)
    r = _run(nc, [arrays], core_ids=[0])
    return r.results[0]["out_x"]
```

```python
from contextlib import ExitStack, contextmanager

import concourse.bass as bass
from concourse import mybir

FP32 = mybir.dt.float32
I32 = mybir.dt.int32
BF16 = mybir.dt.bfloat16
ALU = mybir.AluOpType
ACT = mybir.ActivationFunctionType
AX = mybir.AxisListType

P = 128
N_NODES, D = 3125, 128
N_EDGES = 100000
NT = -(-N_NODES // P)
NPAD = NT * P
LAST_ROWS = N_NODES - (NT - 1) * P
NC_ = -(-N_EDGES // P)
FULL_CHUNKS = N_EDGES // P
TAIL = N_EDGES - FULL_CHUNKS * P
CB = -(-NC_ // P)
NPAIRS = NC_ + NT - 1
G = 4
R = 4
U = R * G
B = 8
ITERS = -(-NPAIRS // U)
NPP = CB * P
NPAIRS_PAD = ITERS * U
HEADS, HC = 4, 32
GROW = D + HEADS
GROW3 = GROW + 3 * HEADS
L0_ROW = D + 2
N_RELS = 16
EPS = 1e-5
BIG = 2.0 ** 100
PAD_NODE = NPAD - 1
FAR = 1 << 20


class Chain:

    def __init__(self, eng, sem, base=0):
        self.eng, self.sem, self.n, self.base = eng, sem, 0, base

    def __call__(self, ins):
        self.n += 1
        ins.then_inc(self.sem, 1)
        self.eng.wait_ge(self.sem, self.base + self.n)


@contextmanager
def phase(nc):
    sems = []
    with ExitStack() as ctx:
        def give_back():
            for s in sems:
                nc.sync.sem_clear(s)
                nc.release_semaphore(s)

        ctx.callback(give_back)

        def sb(name, shape, dt=FP32):
            return ctx.enter_context(nc.sbuf_tensor(f"{name}_{nc.next_id()}", shape, dt))

        def ps(name, shape, dt=FP32):
            return ctx.enter_context(nc.psum_tensor(f"{name}_{nc.next_id()}", shape, dt))

        def sem(name, for_pool_dma=False):
            s = nc.alloc_semaphore(f"{name}_{nc.next_id()}")
            if not for_pool_dma:
                sems.append(s)
            return s

        yield sb, ps, sem, (lambda: ctx.enter_context(nc.Block()))


def bc(ap, n):
    return ap.unsqueeze(len(ap.shape)).to_broadcast([*ap.shape, n])


def mid(ap, n):
    return ap.unsqueeze(1).to_broadcast([ap.shape[0], n, ap.shape[1]])


def at(i, n=1):
    return bass.ds(i, n)


def setup(nc, a, m):
    with phase(nc) as (sb, ps, sem, block_):
        raw = [sb(f"raw{k}", [P, CB, P], I32) for k in range(3)]
        w_raw = sb("w_raw", [P, CB, P])
        rec = sb("rec", [P, CB, 4, P])
        ev = sb("ev", [P, CB, P])
        rec_pair = sb("rec_pair", [P, CB, 4 * P])
        ends = sb("ends", [1, NC_ - 1], I32)
        end_tile = sb("end_tile", [1, NC_ - 1], I32)
        keys = sb("keys", [1, NC_ - 1])
        chunk_no = sb("chunk_no", [1, NC_ - 1])
        keys_all = sb("keys_all", [P, NC_ - 1])
        below = sb("below", [P, NC_ - 1])
        jcol = sb("jcol", [P, CB])
        chunk_f = sb("chunk_f", [P, CB])
        chunk_i = sb("chunk_i", [P, CB], I32)
        tile_f = sb("tile_f", [P, CB])
        tile_128 = sb("tile_128", [P, CB])
        tile_cap = sb("tile_cap", [P, CB])
        tile_i = sb("tile_i", [P, CB], I32)
        tile_all_i, tile_all = sb("tile_all_i", [P, NPP], I32), sb("tile_all", [P, NPP])
        tile_first = sb("tile_first", [1, NPP])
        last_pair, last_pair_i = sb("last_pair", [P, 1]), sb("last_pair_i", [P, 1], I32)
        hi_i = sb("hi_i", [P, NPP], I32)
        psum = ps("tp", [P, 2, 4, P])
        made, loaded, ends_in, cleared = sem("made"), sem("loaded"), sem("ends_in"), sem("cleared")
        keyed, spread = sem("keyed"), sem("spread")
        chunks_known, recs_in, pairs_in = sem("chunks_known"), sem("recs_in", True), sem("pairs_in")
        rec_ready, tile_ready, tile_out, row_in = sem("rec_ready"), sem("tile_ready"), sem("tile_out"), sem("row_in")
        word = sb("word", [1, 1 + NPP // G])
        ends_known, rows_spread = sem("ends_known"), sem("rows_spread")
        stored, local, turned, taken, d_, b_in = sem("stored"), sem("local"), sem("turned"), sem("taken"), sem("d"), sem("b_in")
        block = block_()
        full = (CB - 1) * P * P
        rest = FULL_CHUNKS - (CB - 1) * P

        @block.gpsimd
        def _(pool):
            kw = dict(allow_small_or_imprecise_dtypes=True)
            nc.gpsimd.iota(m.iota[:, :], [[1, P]], 0, 0, **kw).then_inc(made, 1)
            nc.gpsimd.iota(m.pcol[:, :], [[0, 1]], 0, 1, **kw).then_inc(made, 1)
            nc.gpsimd.iota(m.rev[:, :], [[-1, P]], P, 0, **kw).then_inc(made, 1)
            nc.gpsimd.iota(m.revcol[:, :], [[0, B]], P, -1, **kw).then_inc(made, 1)
            nc.gpsimd.iota(jcol[:, :], [[P, CB]], 0, 1, **kw).then_inc(made, 1)
            nc.gpsimd.iota(chunk_no[:, :], [[1, NC_ - 1]], 0, 0, **kw).then_inc(made, 1)
            pool.wait_ge(keyed, 1)
            nc.gpsimd.partition_broadcast(keys_all[:, :], keys[:, :]).then_inc(spread, 1)
            pool.wait_ge(row_in, 16)
            nc.gpsimd.partition_broadcast(tile_all_i[:, :], m.tile_row[:, :]).then_inc(rows_spread, 1)
            pool.wait_ge(chunks_known, 1)
            pool.wait_ge(stored, 48)
            for b in range(CB):
                pool.indirect_dma_start(rec_pair[:, b, :], None, m.rec_dram[:, :],
                                        bass.IndirectOffsetOnAxis(ap=chunk_i[:, b:b + 1], axis=0)).then_inc(recs_in, 16)

        @block.sync
        def _(sp):
            with nc.allow_non_contiguous_dma(reason="the last destination of each chunk"):
                sp.dma_start(ends[:, :], a["dst"][0:(NC_ - 1) * P].rearrange("(o c e) -> o c e", o=1, e=P)[:, :, P - 1]).then_inc(ends_in, 16)
                sp.dma_start(m.beta[:, :], a["L0_gnn_beta"].rearrange("(o n) -> o n", o=1).to_broadcast([P, 1])).then_inc(b_in, 16)
                sp.dma_start(m.eps1[:, :], a["L0_gnn_eps"].rearrange("(o n) -> o n", o=1).to_broadcast([P, 1])).then_inc(b_in, 16)
            sp.wait_ge(cleared, 5)
            for name, tile in (("src", raw[0]), ("dst", raw[1]), ("edge_type_16", raw[2]), ("edge_weight", w_raw)):
                v = a[name]
                sp.dma_start(tile[:, 0:CB - 1, :], v[0:full].rearrange("(b c e) -> c b e", c=P, e=P)).then_inc(loaded, 16)
                sp.dma_start(tile[0:rest, CB - 1, :], v[full:FULL_CHUNKS * P].rearrange("(c e) -> c e", e=P)).then_inc(loaded, 16)
                sp.dma_start(tile[rest:rest + 1, CB - 1, 0:TAIL], v[FULL_CHUNKS * P:].rearrange("(c e) -> c e", c=1)).then_inc(loaded, 16)
            sp.dma_start(m.x[:, 0:NT - 1, :], a["x"][0:(NT - 1) * P, :].rearrange("(t p) f -> p t f", p=P)).then_inc(loaded, 16)
            sp.dma_start(m.x[0:LAST_ROWS, NT - 1, :], a["x"][(NT - 1) * P:, :]).then_inc(loaded, 16)
            sp.wait_ge(rec_ready, 1)
            sp.dma_start(m.rec_dram.rearrange("(b c) k -> c b k", c=P), rec[:, :, :, :].rearrange("p b k e -> p b (k e)")).then_inc(stored, 16)
            sp.dma_start(m.src_dram.rearrange("(b c e) -> c b e", c=P, e=P), rec[:, :, 0, :]).then_inc(stored, 16)
            sp.dma_start(m.ev_dram.rearrange("(b c e) -> c b e", c=P, e=P), ev[:, :, :]).then_inc(stored, 16)
            sp.wait_ge(tile_ready, 1)
            with nc.allow_non_contiguous_dma(reason="one number a pair"):
                sp.dma_start(m.tile_dram.rearrange("(b p) -> p b", p=P), tile_i[:, :]).then_inc(tile_out, 16)
            sp.wait_ge(tile_out, 16)
            sp.dma_start(m.tile_row[:, :], m.tile_dram.rearrange("(o j) -> o j", o=1)).then_inc(row_in, 16)
            sp.wait_ge(ends_known, 1)
            with nc.allow_non_contiguous_dma(reason="one number a tile"):
                sp.dma_start(m.end_dram.rearrange("(p o) -> p o", o=1), last_pair_i[:, :]).then_inc(tile_out, 16)
            sp.wait_ge(tile_out, 32)
            sp.dma_start(m.end_row[:, :], m.end_dram.rearrange("(o j) -> o j", o=1)).then_inc(row_in, 16)
            sp.wait_ge(row_in, 32)
            sp.wait_ge(stored, 48)

        @block.vector
        def _(dve):
            v = nc.vector
            step = Chain(dve, d_)
            v.memset(raw[0][:, CB - 1, :], PAD_NODE).then_inc(cleared, 1)
            v.memset(raw[1][:, CB - 1, :], FAR).then_inc(cleared, 1)
            v.memset(raw[2][:, CB - 1, :], 0).then_inc(cleared, 1)
            v.memset(w_raw[:, CB - 1, :], 0.0).then_inc(cleared, 1)
            v.memset(m.x[:, NT - 1, :], 0.0).then_inc(cleared, 1)
            v.memset(m.w1[:, :, 1:2], 1.0)
            dve.wait_ge(made, 6)
            v.tensor_scalar(m.ident[:, :], m.iota[:, :], m.pcol[:, 0:1], None, ALU.is_equal)
            dve.wait_ge(ends_in, 16)
            step(v.tensor_scalar(end_tile[:, :], ends[:, :], 7, None, ALU.arith_shift_right))
            step(v.tensor_copy(keys[:, :], end_tile[:, :]))
            v.tensor_tensor(keys[:, :], keys[:, :], chunk_no[:, :], ALU.add).then_inc(keyed, 1)
            dve.wait_ge(loaded, 16 * 14)
            dve.wait_ge(b_in, 32)
            step(v.tensor_scalar(m.eps1[:, :], m.eps1[:, :], 1.0, None, ALU.add))
            step(v.tensor_copy(rec[:, :, 0, :], raw[0][:, :, :]))
            step(v.tensor_copy(rec[:, :, 1, :], raw[1][:, :, :]))
            step(v.tensor_copy(rec[:, :, 2, :], w_raw[:, :, :]))
            step(v.tensor_copy(rec[:, :, 3, :], raw[2][:, :, :]))
            step(v.tensor_scalar(ev[:, :, :], w_raw[:, :, :], m.beta[:, 0:1], None, ALU.mult))
            v.scalar_tensor_tensor(rec[:, :, 3, :], rec[:, :, 3, :], float(NPAD), rec[:, :, 0, :], ALU.mult, ALU.add).then_inc(rec_ready, 1)
            dve.wait_ge(spread, 1)
            for b in range(CB):
                step(v.tensor_scalar(below[:, :], keys_all[:, :], jcol[:, b:b + 1], None, ALU.is_lt, ALU.add, accum_out=chunk_f[:, b:b + 1]))
            v.tensor_copy(chunk_i[:, :], chunk_f[:, :]).then_inc(chunks_known, 1)
            step(v.tensor_tensor(tile_f[:, :], jcol[:, :], chunk_f[:, :], ALU.subtract))
            step(v.tensor_scalar(tile_128[:, :], tile_f[:, :], float(P), None, ALU.mult))
            step(v.tensor_scalar(tile_cap[:, :], tile_f[:, :], float(NT - 1), None, ALU.min))
            v.tensor_copy(tile_i[:, :], tile_cap[:, :]).then_inc(tile_ready, 1)
            dve.wait_ge(rows_spread, 1)
            step(v.tensor_copy(tile_all[:, :], tile_all_i[:, :]))
            step(v.tensor_copy(tile_first[:, :], tile_all_i[0:1, :]))
            step(v.memset(m.fresh[:, 0:1], -BIG))
            step(v.tensor_tensor(m.fresh[:, 1:], tile_all[:, 1:], tile_all[:, 0:NPP - 1], ALU.is_gt))
            step(v.tensor_scalar(m.fresh[:, 1:], m.fresh[:, 1:], -BIG, None, ALU.mult))
            step(v.tensor_scalar(tile_all[:, 0:NPAIRS], tile_all[:, 0:NPAIRS], m.pcol[:, 0:1], None, ALU.is_le, ALU.add, accum_out=last_pair[:, :]))
            step(v.tensor_scalar(last_pair[:, :], last_pair[:, :], -1.0, None, ALU.add))
            v.tensor_copy(last_pair_i[:, :], last_pair[:, :]).then_inc(ends_known, 1)
            step(v.memset(word[:, :], 0.0))
            for k in range(G):
                step(v.scalar_tensor_tensor(word[:, 1:], tile_first[:, k::G], 32.0 ** k, word[:, 1:], ALU.mult, ALU.add))
            step(v.tensor_copy(m.word_row[:, :], word[:, :]))
            dve.wait_ge(recs_in, 16 * CB)
            for b in range(CB):
                last = v.tensor_scalar(rec_pair[:, b, P:2 * P], rec_pair[:, b, P:2 * P], tile_128[:, b:b + 1], None, ALU.subtract)
                step(last)
            v.nop().then_inc(local, 1)
            for b in range(CB):
                dve.wait_ge(turned, 2 * b + 1)
                q = psum[:, 0, :, :]
                cols = slice(b * P, b * P + P)
                step(v.tensor_copy(m.src_pair[:, cols], q[:, 0, :]))
                step(v.tensor_copy(m.loc_pair[:, cols], q[:, 1, :]))
                step(v.tensor_copy(m.w1[:, cols, 0], q[:, 2, :]))
                step(v.tensor_copy(m.rel_pair[:, cols], q[:, 3, :]))
                v.tensor_scalar(m.ev_pair[:, cols], q[:, 2, :], m.beta[:, 0:1], None, ALU.mult).then_inc(taken, 1)
                dve.wait_ge(turned, 2 * b + 2)
                step(v.tensor_copy(m.src_col[:, cols], psum[:, 1, 0, :]))
                v.tensor_copy(m.ev_col[:, cols], psum[:, 1, 1, :]).then_inc(taken, 1)
            step(v.tensor_copy(hi_i[:, :], m.src_col[:, :]))
            step(v.tensor_scalar(hi_i[:, :], hi_i[:, :], 7, None, ALU.arith_shift_right))
            step(v.tensor_copy(m.hi_col[:, :], hi_i[:, :]))
            step(v.scalar_tensor_tensor(m.lo_col[:, :], m.hi_col[:, :], -float(P), m.src_col[:, :], ALU.mult, ALU.add))

        @block.tensor
        def _(pe):
            pe.wait_ge(local, 1)
            pe.wait_ge(rec_ready, 1)
            for b in range(CB):
                if b:
                    pe.wait_ge(taken, 2 * b - 1)
                for k in range(4):
                    last = nc.tensor.transpose(psum[:, 0, k, :], rec_pair[:, b, k * P:(k + 1) * P], m.ident[:, :])
                last.then_inc(turned, 1)
                if b:
                    pe.wait_ge(taken, 2 * b)
                nc.tensor.transpose(psum[:, 1, 0, :], rec[:, b, 0, :], m.ident[:, :])
                nc.tensor.transpose(psum[:, 1, 1, :], ev[:, b, :], m.ident[:, :]).then_inc(turned, 1)


def source_softmax(nc, m):
    blocks = -(-NC_ // B)
    blocks += blocks % 2
    with phase(nc) as (sb, ps, sem, block_):
        rows = [[sb(f"rows{b}{k}", [P, B, P]) for k in range(2)] for b in range(2)]
        differ, masked, onehot = sb("differ", [P, B, P]), sb("masked", [P, B, P]), sb("onehot", [P, B, P])
        masked2 = sb("masked2", [P, B, P])
        mx, first, is_first, below, ex = (sb(n, [P, B]) for n in ("mx", "first", "is_first", "below", "ex"))
        hi1 = sb("hi1", [P, B, NT])
        moved = sb("moved", [P, B, 3 * NT])
        chunk_max = sb("chunk_max", [P, B, NT])
        block_max, new_max, block_sum = sb("block_max", [P, NT]), sb("new_max", [P, NT]), sb("block_sum", [P, NT])
        gap, shrink = sb("gap", [P, B + 1, NT]), sb("shrink", [P, B + 1, NT])
        scaled = sb("scaled", [P, B, NT])
        psum = ps("node", [P, B, P])
        row_in = [sem("row_in0"), sem("row_in1")]
        rows_free, d_, gap1, exp1, gap2, exp2, ready, summed = (sem(n) for n in ("rows_free", "d", "gap1", "exp1", "gap2", "exp2", "ready", "summed"))
        block = block_()
        K = 20

        @block.sync
        def _(sp):
            with sp.Fori(0, blocks // 2) as i:
                for b in range(2):
                    blk = i * 2 + b
                    sp.wait_ge(rows_free, blk + 1)
                    sp.nop(nofuse=True)
                    for k, dram in enumerate((m.src_dram, m.ev_dram)):
                        sp.dma_start(rows[b][k][:, :, :].rearrange("p u e -> p (u e)"),
                                     dram[at(blk * (B * P), B * P)].unsqueeze(0).to_broadcast([P, B * P])).then_inc(row_in[b], 16)

        @block.vector
        def _(dve):
            v = nc.vector
            v.memset(m.seg_sum[:, :], 0.0)
            v.memset(m.seg_max[:, :], -BIG).then_inc(d_, 1)
            v.sem_inc(rows_free, 2)
            with dve.Fori(0, blocks // 2) as i:
                for b in range(2):
                    blk = i * 2 + b
                    step = Chain(dve, d_, blk * K + 1)
                    cols = at(blk * B, B)
                    srow, erow = rows[b][0][:, :, :], rows[b][1][:, :, :]
                    dve.wait_ge(row_in[b], i * 32 + 32)
                    step(v.tensor_tensor(differ[:, :, :], srow, bc(m.src_col[:, cols], P), ALU.not_equal))
                    step(v.scalar_tensor_tensor(masked[:, :, :], differ[:, :, :], -BIG, erow, ALU.mult, ALU.add))
                    v.sem_inc(rows_free, 1)
                    step(v.tensor_reduce(mx[:, :], masked[:, :, :], AX.X, ALU.max))
                    v.tensor_tensor(below[:, :], m.ev_col[:, cols], mx[:, :], ALU.subtract).then_inc(gap1, 1)
                    step(v.scalar_tensor_tensor(masked2[:, :, :], differ[:, :, :], -BIG, mid(m.rev[:, :], B), ALU.mult, ALU.add))
                    step(v.tensor_reduce(first[:, :], masked2[:, :, :], AX.X, ALU.max))
                    step(v.tensor_tensor(is_first[:, :], first[:, :], m.revcol[:, :], ALU.is_equal))
                    step(v.tensor_tensor(onehot[:, :, :], mid(m.iota[:, :], B), bc(m.lo_col[:, cols], P), ALU.is_equal))
                    step(v.tensor_tensor(hi1[:, :, :], mid(m.iota[:, 0:NT], B), bc(m.hi_col[:, cols], NT), ALU.is_equal))
                    step(v.tensor_tensor(moved[:, :, 2 * NT:], hi1[:, :, :], bc(is_first[:, :], NT), ALU.mult))
                    step(v.tensor_tensor(moved[:, :, NT:2 * NT], moved[:, :, 2 * NT:], bc(mx[:, :], NT), ALU.mult))
                    dve.wait_ge(exp1, blk + 1)
                    v.tensor_tensor(moved[:, :, 0:NT], hi1[:, :, :], bc(ex[:, :], NT), ALU.mult).then_inc(ready, 1)
                    dve.wait_ge(summed, blk + 1)
                    step(v.tensor_scalar(chunk_max[:, :, :], psum[:, :, 2 * NT:3 * NT], 1.0, BIG, ALU.subtract, ALU.mult))
                    step(v.tensor_tensor(chunk_max[:, :, :], chunk_max[:, :, :], psum[:, :, NT:2 * NT], ALU.add))
                    step(v.tensor_reduce(block_max[:, :], chunk_max[:, :, :].rearrange("p u h -> p h u"), AX.X, ALU.max))
                    step(v.tensor_tensor(new_max[:, :], m.seg_max[:, :], block_max[:, :], ALU.max))
                    step(v.tensor_tensor(gap[:, 0:B, :], chunk_max[:, :, :], mid(new_max[:, :], B), ALU.subtract))
                    v.tensor_tensor(gap[:, B, :], m.seg_max[:, :], new_max[:, :], ALU.subtract).then_inc(gap2, 1)
                    dve.wait_ge(exp2, blk + 1)
                    step(v.tensor_copy(m.seg_max[:, :], new_max[:, :]))
                    step(v.tensor_tensor(scaled[:, :, :], shrink[:, 0:B, :], psum[:, :, 0:NT], ALU.mult))
                    step(v.tensor_reduce(block_sum[:, :], scaled[:, :, :].rearrange("p u h -> p h u"), AX.X, ALU.add))
                    step(v.tensor_tensor(m.seg_sum[:, :], m.seg_sum[:, :], shrink[:, B, :], ALU.mult))
                    step(v.tensor_tensor(m.seg_sum[:, :], m.seg_sum[:, :], block_sum[:, :], ALU.add))
                    assert step.n == K, step.n

        @block.scalar
        def _(act):
            with act.Fori(0, blocks // 2) as i:
                for b in range(2):
                    blk = i * 2 + b
                    act.wait_ge(gap1, blk + 1)
                    nc.scalar.activation(ex[:, :], below[:, :], ACT.Exp).then_inc(exp1, 1)
                    act.wait_ge(gap2, blk + 1)
                    nc.scalar.activation(shrink[:, :, :], gap[:, :, :], ACT.Exp).then_inc(exp2, 1)

        @block.tensor
        def _(pe):
            with pe.Fori(0, blocks // 2) as i:
                for b in range(2):
                    pe.wait_ge(ready, i * 2 + b + 1)
                    for u in range(B):
                        last = nc.tensor.matmul(psum[:, u, 0:3 * NT], onehot[:, u, :], moved[:, u, :], start=True, stop=True)
                    last.then_inc(summed, 1)


def layernorm_relu(nc, m, out):
    with phase(nc) as (sb, ps, sem, block_):
        total, var = sb("total", [P, NT]), sb("var", [P, NT])
        sq = sb("sq", [P, NT, D])
        d_, var_ready, root = sem("d"), sem("var_ready"), sem("root")
        block = block_()

        @block.vector
        def _(dve):
            v = nc.vector
            step = Chain(dve, d_)
            step(v.tensor_reduce(total[:, :], m.x[:, :, :], AX.X, ALU.add))
            step(v.tensor_scalar(total[:, :], total[:, :], 1.0 / D, None, ALU.mult))
            step(v.tensor_tensor(out[:, :, 0:D], m.x[:, :, :], bc(total[:, :], D), ALU.subtract))
            step(v.tensor_tensor(sq[:, :, :], out[:, :, 0:D], out[:, :, 0:D], ALU.mult))
            step(v.tensor_reduce(var[:, :], sq[:, :, :], AX.X, ALU.add))
            v.tensor_scalar(var[:, :], var[:, :], 1.0 / D, EPS, ALU.mult, ALU.add).then_inc(var_ready, 1)
            dve.wait_ge(root, 1)
            step(v.reciprocal(var[:, :], var[:, :]))
            step(v.tensor_tensor(out[:, :, 0:D], out[:, :, 0:D], bc(var[:, :], D), ALU.mult))
            step(v.tensor_scalar(out[:, :, 0:D], out[:, :, 0:D], 0.0, None, ALU.max))

        @block.scalar
        def _(act):
            act.wait_ge(var_ready, 1)
            nc.scalar.activation(var[:, :], var[:, :], ACT.Sqrt).then_inc(root, 1)


def l0_table(nc, m):
    with phase(nc) as (sb, ps, sem, block_):
        sq, rows = sb("sq", [P, NT, D]), sb("rows", [P, NT, L0_ROW])
        norm, den = sb("norm", [P, NT]), sb("den", [P, NT])
        d_, n2, root, ready, out = sem("d"), sem("n2"), sem("root"), sem("ready"), sem("out")
        block = block_()

        @block.vector
        def _(dve):
            v = nc.vector
            step = Chain(dve, d_)
            step(v.tensor_tensor(sq[:, :, :], m.h[:, :, :], m.h[:, :, :], ALU.mult))
            step(v.tensor_reduce(norm[:, :], sq[:, :, :], AX.X, ALU.add))
            v.tensor_scalar(norm[:, :], norm[:, :], 1e-24, None, ALU.max).then_inc(n2, 1)
            step(v.tensor_scalar(den[:, :], m.seg_sum[:, :], 0.5, None, ALU.max))
            dve.wait_ge(root, 1)
            step(v.tensor_tensor(den[:, :], den[:, :], norm[:, :], ALU.mult))
            step(v.reciprocal(den[:, :], den[:, :]))
            step(v.tensor_scalar(rows[:, :, D], m.seg_max[:, :], -1.0, None, ALU.mult))
            step(v.memset(rows[:, :, D + 1:], 0.0))
            v.tensor_tensor(rows[:, :, 0:D], m.h[:, :, :], bc(den[:, :], D), ALU.mult).then_inc(ready, 1)

        @block.scalar
        def _(act):
            act.wait_ge(n2, 1)
            nc.scalar.activation(norm[:, :], norm[:, :], ACT.Sqrt).then_inc(root, 1)

        @block.sync
        def _(sp):
            sp.wait_ge(ready, 1)
            sp.dma_start(m.l0_dram.rearrange("(t p) w -> p t w", p=P), rows[:, :, :]).then_inc(out, 16)
            sp.wait_ge(out, 16)


L0_ROW = D + 2

def tile_of(pe, word, k):
    return pe.snap((word >> (5 * k)) & 31 if k < G - 1 else word >> (5 * k), min_val=0, max_val=31)


def fetch_groups(nc, pool, m, table, ring, staged, fetched, ring_free):
    with pool.Fori(0, ITERS) as i:
        for g in range(R):
            pool.wait_ge(staged, i * R + g + 1)
            pool.nop(nofuse=True)
            pool.wait_ge(ring_free, i * R + g + 1)
            pool.nop(nofuse=True)
            for u in range(g * G, (g + 1) * G):
                pool.indirect_dma_start(ring[:, u, :], None, table[:, :],
                                        bass.IndirectOffsetOnAxis(ap=m.stage[:, u:u + 1], axis=0)).then_inc(fetched[g], 16)


def edge_sum(nc, m, table, index=None, weight=None, mode="plain"):
    with phase(nc) as (sb, ps, sem, block_):
        gathers = mode != "heads"
        width, extra = {"plain": (D, 0), "source": (L0_ROW, 2), "heads": (GROW, HEADS)}[mode]
        ring = sb("ring", [P, U, width])
        scaled = ring if mode == "plain" else sb("scaled", [P, U, D + extra])
        onehot = sb("onehot", [P, U, P])
        places, weights = sb("places", [P, U]), sb("weights", [P, U])
        p_src, ev = sb("p_src", [P, U]), sb("ev", [P, U])
        zeros = sb("zeros", [P, 512])
        total = ps("total", [P, 8 * 512])
        more = total[:, 7 * 512:]
        fetched = [sem(f"fetched{g}", gathers) for g in range(R)]
        cleared, staged, placed, termed, weighed, hot, summed, scaled_up, closed, d_ = (sem(n) for n in (
            "cleared", "staged", "placed", "termed", "weighed", "hot", "summed", "scaled_up", "closed", "d"))
        block = block_()

        if gathers:
            @block.gpsimd
            def _(pool):
                fetch_groups(nc, pool, m, table, ring, staged, fetched, summed if mode == "plain" else scaled_up)
        else:
            @block.sync
            def _(sp):
                with sp.Fori(0, ITERS) as i:
                    for g in range(R):
                        sp.wait_ge(scaled_up, i * R + g + 1)
                        sp.nop(nofuse=True)
                        sp.dma_start(ring[:, g * G:(g + 1) * G, :],
                                     table[at((i * R + g) * (G * P), G * P), :].rearrange("(u p) w -> p u w", p=P)).then_inc(fetched[g], 16)

        if mode != "plain":
            @block.scalar
            def _(act):
                with act.Fori(0, ITERS) as i:
                    for g in range(R):
                        slots = slice(g * G, (g + 1) * G)
                        if mode == "heads":
                            act.wait_ge(summed, i * R + g + 1)
                            act.nop(nofuse=True)
                            nc.scalar.activation(scaled[:, slots, D:], m.ex_pair[:, at((i * R + g) * (G * HEADS), G * HEADS)]
                                                 .rearrange("p (u h) -> p u h", h=HEADS), ACT.Copy).then_inc(termed, 1)
                            continue
                        nc.scalar.activation(ev[:, slots], m.ev_pair[:, at((i * R + g) * G, G)], ACT.Copy).then_inc(termed, 1)
                        act.wait_ge(termed, i * R + g + 1)
                        act.nop(nofuse=True)
                        act.wait_ge(fetched[g], i * 64 + 64)
                        act.nop(nofuse=True)
                        for u in range(g * G, (g + 1) * G):
                            last = nc.scalar.activation(p_src[:, u:u + 1], ev[:, u:u + 1], ACT.Exp, bias=ring[:, u, D:D + 1])
                        last.then_inc(weighed, 1)
                        act.wait_ge(summed, i * R + g + 1)
                        act.nop(nofuse=True)
                        nc.scalar.activation(scaled[:, slots, D:], m.w1[:, at((i * R + g) * G, G), :], ACT.Copy)
                        act.wait_ge(weighed, i * R + g + 1)
                        act.nop(nofuse=True)
                        for u in range(g * G, (g + 1) * G):
                            last = nc.scalar.activation(scaled[:, u, 0:D], ring[:, u, 0:D], ACT.Copy, scale=p_src[:, u:u + 1])
                        last.then_inc(scaled_up, 1)

        @block.vector
        def _(dve):
            v = nc.vector
            v.memset(zeros[:, :], 0.0).then_inc(cleared, 1)
            if gathers:
                for g in range(R):
                    v.tensor_copy(m.stage[:, g * G:(g + 1) * G], index[:, g * G:(g + 1) * G]).then_inc(staged, 1)
            v.sem_inc(summed, R)
            if mode != "plain":
                v.sem_inc(scaled_up, R)
            def build(gi, g):
                slots = slice(g * G, (g + 1) * G)
                dve.wait_ge(summed, gi + 1)
                n = 2 if weight is not None else 1
                v.tensor_copy(places[:, slots], m.loc_pair[:, at(gi * G, G)]).then_inc(placed, 1)
                if weight is not None:
                    v.tensor_copy(weights[:, slots], weight[:, at(gi * G, G), 0]).then_inc(placed, 1)
                dve.wait_ge(placed, gi * n + n)
                for u in range(g * G, (g + 1) * G):
                    last = v.tensor_scalar(onehot[:, u, :], m.iota[:, :], places[:, u:u + 1],
                                           None if weight is None else weights[:, u:u + 1],
                                           ALU.is_equal, ALU.bypass if weight is None else ALU.mult)
                last.then_inc(hot, 1)

            build(0, 0)
            with dve.Fori(0, ITERS) as i:
                for g in range(R):
                    gi = i * R + g
                    slots = slice(g * G, (g + 1) * G)
                    build(gi + 1, (g + 1) % R)
                    if gathers:
                        dve.wait_ge(fetched[g], i * 64 + 64)
                        v.tensor_copy(m.stage[:, slots], index[:, at((gi + R) * G, G)]).then_inc(staged, 1)
                    else:
                        dve.wait_ge(fetched[g], i * 16 + 16)
                        dve.wait_ge(termed, gi + 1)
                        v.tensor_tensor(scaled[:, slots, 0:D].rearrange("p u (h c) -> p u h c", h=HEADS),
                                        ring[:, slots, 0:D].rearrange("p u (h c) -> p u h c", h=HEADS),
                                        bc(scaled[:, slots, D:], HC), ALU.mult).then_inc(scaled_up, 1)
            step = Chain(dve, d_)
            dve.wait_ge(closed, 1)
            for b in range(7):
                tiles = slice(4 * b, min(4 * b + 4, NT))
                n = min(4 * b + 4, NT) - 4 * b
                step(v.tensor_copy(m.acc[:, tiles, 0:D], total[:, b * 512:b * 512 + n * D].rearrange("p (t f) -> p t f", f=D)))
            if extra:
                step(v.tensor_copy(m.acc[:, :, D:D + extra], total[:, 7 * 512:7 * 512 + NT * extra].rearrange("p (t f) -> p t f", f=extra)))

        @block.tensor
        def _(pe):
            pe.wait_ge(cleared, 1)
            for b in range(7):
                nc.tensor.matmul(total[:, b * 512:(b + 1) * 512], zeros[:, 0:P], zeros[:, :], start=True, stop=False)
            if extra:
                nc.tensor.matmul(more, zeros[:, 0:P], zeros[:, :], start=True, stop=False)
            with pe.Fori(0, ITERS) as i:
                for g in range(R):
                    gi = i * R + g
                    word = pe.value_load(m.word_row[0:1, at(gi + 1)])
                    if mode == "plain":
                        pe.wait_ge(fetched[g], i * 64 + 64)
                    else:
                        pe.wait_ge(scaled_up, gi + R + 1)
                    pe.nop(nofuse=True)
                    pe.wait_ge(hot, gi + 1)
                    pe.nop(nofuse=True)
                    for k in range(G):
                        u, tile = g * G + k, tile_of(pe, word, k)
                        last = nc.tensor.matmul(total[:, at(tile * D, D)], onehot[:, u, :], scaled[:, u, 0:D], start=False, stop=False, skip_group_check=True)
                        if extra:
                            last = nc.tensor.matmul(total[:, at(tile * extra + 7 * 512, extra)], onehot[:, u, :], scaled[:, u, D:], start=False, stop=False, skip_group_check=True)
                    last.then_inc(summed, 1)
            for b in range(7):
                last = nc.tensor.matmul(total[:, b * 512:(b + 1) * 512], zeros[:, 0:P], zeros[:, :], start=False, stop=True)
            if extra:
                last = nc.tensor.matmul(more, zeros[:, 0:P], zeros[:, :], start=False, stop=True)
            last.then_inc(closed, 1)


def gat_max(nc, m):
    with phase(nc) as (sb, ps, sem, block_):
        NTERM = 3 * HEADS
        ring = sb("ring", [P, U, GROW3])
        terms = sb("terms", [P, R, P], BF16)
        terms_t = sb("terms_t", [P, R, P], BF16)
        ident_b = sb("ident_b", [P, P], BF16)
        row_no, hit, which = sb("row_no", [P, G, HEADS]), sb("hit", [P, G, HEADS]), sb("which", [P, G, HEADS])
        pick = sb("pick", [P, G, HEADS, P], BF16)
        other = sb("other", [P, U, P], BF16)
        minus = sb("minus", [P, HEADS, P], BF16)
        places = sb("places", [P, U])
        part = sb("part", [P, G + NPAIRS_PAD, HEADS])
        upto = sb("upto", [P, HEADS, NPAIRS_PAD])
        spread = ps("spread", [P, 2, 2, HEADS * P])
        flipped = ps("flipped", [P, 2, 1024], BF16)
        fetched = [sem(f"fetched{g}", True) for g in range(R)]
        stored = [sem(f"stored{g}") for g in range(R)]
        staged, ring_free, placed, hot, spr, red, noted, flip, turned, made, counted, d_ = (
            sem(n) for n in ("staged", "ring_free", "placed", "hot", "spr", "red", "noted", "flip", "turned", "made", "counted", "d"))
        block = block_()

        @block.gpsimd
        def _(pool):
            nc.gpsimd.iota(row_no[:, :, :], [[-NTERM, G], [-1, HEADS]], 0, 1, allow_small_or_imprecise_dtypes=True).then_inc(counted, 1)
            fetch_groups(nc, pool, m, m.gat_dram, ring, staged, fetched, ring_free)

        @block.sync
        def _(sp):
            with sp.Fori(0, ITERS) as i:
                for g in range(R):
                    gi = i * R + g
                    sp.wait_ge(fetched[g], i * 64 + 64)
                    sp.nop(nofuse=True)
                    sp.dma_start(m.rows_dram[at(gi * (G * P), G * P), :].rearrange("(u p) w -> p u w", p=P),
                                 ring[:, g * G:(g + 1) * G, 0:GROW]).then_inc(stored[g], 16)
                    sp.wait_ge(noted, gi + 1)
                    sp.nop(nofuse=True)
                    sp.wait_ge(stored[g], i * 16 + 16)
                    sp.nop(nofuse=True)
                    sp.sem_inc(ring_free, 1)

        @block.scalar
        def _(act):
            act.wait_ge(made, 1)
            with act.Fori(0, ITERS) as i:
                for g in range(R):
                    gi = i * R + g
                    slots = slice(g * G, (g + 1) * G)
                    act.wait_ge(fetched[g], i * 64 + 64)
                    act.nop(nofuse=True)
                    nc.scalar.activation(m.as_pair[:, at(gi * (G * HEADS), G * HEADS)].rearrange("p (u h) -> p u h", h=HEADS),
                                         ring[:, slots, D:GROW], ACT.Copy)
                    nc.scalar.activation(terms[:, g, 0:G * NTERM].rearrange("p (u k) -> p u k", k=NTERM),
                                         ring[:, slots, GROW:], ACT.Copy).then_inc(noted, 1)
                    act.wait_ge(flip, gi + 1)
                    act.nop(nofuse=True)
                    nc.scalar.activation(terms_t[:, g, :], flipped[:, g % 2, 0:P], ACT.Copy).then_inc(turned, 1)

        @block.vector
        def _(dve):
            v = nc.vector
            step = Chain(dve, d_)
            step(v.tensor_copy(ident_b[:, :], m.ident[:, :]))
            step(v.memset(terms[:, :, :], 0.0))
            step(v.memset(terms_t[:, R - 1, :], 0.0))
            step(v.memset(other[:, U - G:, :], 0.0))
            for h in range(HEADS):
                step(v.tensor_scalar(minus[:, h, :], m.ident[:, :], -BIG, None, ALU.mult))
            dve.wait_ge(counted, 1)
            step(v.tensor_scalar(which[:, :, :], row_no[:, :, :], 0.0, None, ALU.is_equal))
            for k in (1, 2):
                step(v.tensor_scalar(hit[:, :, :], row_no[:, :, :], float(k * HEADS), None, ALU.is_equal))
                step(v.tensor_tensor(which[:, :, :], which[:, :, :], hit[:, :, :], ALU.add))
            step(v.tensor_copy(pick[:, :, :, :], bc(which[:, :, :], P)))
            v.sem_inc(made, 1)
            v.sem_inc(ring_free, R)
            v.sem_inc(red, 2)
            v.sem_inc(hot, 1)
            v.sem_inc(turned, 2)
            for g in range(R):
                v.tensor_copy(m.stage[:, g * G:(g + 1) * G], m.src_pair[:, g * G:(g + 1) * G]).then_inc(staged, 1)

            def maxima(first, unit, k):
                dve.wait_ge(spr, unit)
                v.tensor_reduce(part[:, first, :].rearrange("p u h -> p (u h)"),
                                spread[:, k, :, :].rearrange("p u (h e) -> p (u h) e", h=HEADS), AX.X, ALU.max).then_inc(red, 1)

            with dve.Fori(0, ITERS) as i:
                for g in range(R):
                    gi = i * R + g
                    slots = slice(g * G, (g + 1) * G)
                    v.tensor_copy(places[:, slots], m.loc_pair[:, at(gi * G, G)]).then_inc(placed, 1)
                    dve.wait_ge(placed, gi + 1)
                    for u in range(g * G, (g + 1) * G):
                        last = v.tensor_scalar(other[:, u, :], m.iota[:, :], places[:, u:u + 1], None, ALU.not_equal)
                    last.then_inc(hot, 1)
                    for k in range(2):
                        maxima(at(gi * G + 2 * k, 2), gi * 2 + k + 1, k)
                    dve.wait_ge(fetched[g], i * 64 + 64)
                    v.tensor_copy(m.stage[:, slots], m.src_pair[:, at((gi + R) * G, G)]).then_inc(staged, 1)
            for k in range(2):
                maxima(slice(NPAIRS_PAD + 2 * k, NPAIRS_PAD + 2 * k + 2), ITERS * R * 2 + k + 1, k)
            dve.wait_ge(red, 2 * (ITERS * R + 1) + 2)
            for h in range(HEADS):
                step(v.tensor_tensor_scan(upto[:, h, :], m.fresh[:, 0:NPAIRS_PAD], part[:, G:, h], -BIG, ALU.add, ALU.max))
            with dve.Fori(0, NT) as t:
                end = dve.value_load(m.end_row[0:1, at(t)], min_val=0, max_val=NPAIRS - 1)
                top = m.top[:, at(t), :].rearrange("p o h -> p (o h)")
                v.tensor_tensor(top, top, upto[:, :, at(end)].rearrange("p h o -> p (h o)"), ALU.max)

        @block.tensor
        def _(pe):
            def spread_pairs(gprev, n):
                pe.wait_ge(turned, n + 1)
                pe.wait_ge(hot, n)
                for k in range(2):
                    pe.wait_ge(red, 2 * n - 1 + k)
                    for w in range(2):
                        u = 2 * k + w
                        nc.tensor.matmul(spread[:, k, w, :], other[:, gprev * G + u, :], minus[:, :, :].rearrange("p h e -> p (h e)"), start=True, stop=False)
                        for h in range(HEADS):
                            last = nc.tensor.matmul(spread[:, k, w, h * P:(h + 1) * P], pick[:, u, h, :], terms_t[:, gprev, :],
                                                    start=False, stop=h == HEADS - 1)
                    last.then_inc(spr, 1)

            pe.wait_ge(made, 1)
            with pe.Fori(0, ITERS) as i:
                for g in range(R):
                    gi = i * R + g
                    pe.wait_ge(noted, gi + 1)
                    pe.wait_ge(turned, gi + 1)
                    nc.tensor.transpose(flipped[:, g % 2, 0:P], terms[:, g, :], ident_b[:, :]).then_inc(flip, 1)
                    spread_pairs((g - 1) % R, gi + 1)
            spread_pairs(R - 1, ITERS * R + 1)


def split3(dve, step, v, x, parts, rest, back):
    step(v.tensor_copy(rest, x))
    for k, part in enumerate(parts):
        step(v.tensor_copy(part, rest))
        step(v.tensor_copy(back, part))
        if k < 2:
            step(v.tensor_tensor(rest, rest, back, ALU.subtract))


def gat_expand(nc, m):
    with phase(nc) as (sb, ps, sem, block_):
        W = 2 * HEADS
        onehot, turned = sb("onehot", [P, U, P], BF16), sb("turned", [P, U, P], BF16)
        am3 = sb("am3", [P, 32, 3, W], BF16)
        rest, back = sb("rest", [P, NT, W]), sb("back", [P, NT, W])
        ident_b = sb("ident_b", [P, P], BF16)
        places = sb("places", [P, U])
        flipped = ps("flipped", [P, 2, 1024], BF16)
        got = ps("got", [P, 2, 512])
        placed, hot, flip, turn, expd, noted, made, d_ = (sem(n) for n in ("placed", "hot", "flip", "turn", "expd", "noted", "made", "d"))
        block = block_()

        @block.vector
        def _(dve):
            v = nc.vector
            step = Chain(dve, d_)
            step(v.tensor_copy(ident_b[:, :], m.ident[:, :]))
            step(v.memset(turned[:, U - G:, :], 0.0))
            split3(dve, step, v, m.am[:, :, :], [am3[:, 0:NT, k, :] for k in range(3)], rest[:, :, :], back[:, :, :])
            v.sem_inc(made, 1)
            v.sem_inc(turn, 2)
            v.sem_inc(noted, 2)

            def note(first, n, k):
                dve.wait_ge(expd, n)
                v.tensor_reduce(m.am_pair[:, first].rearrange("p (u w) -> p u w", w=W),
                                got[:, k, 0:G * 3 * W].rearrange("p (u k w) -> p u w k", k=3, w=W), AX.X, ALU.add).then_inc(noted, 1)

            def build(gi, g):
                slots = slice(g * G, (g + 1) * G)
                v.tensor_copy(places[:, slots], m.loc_pair[:, at(gi * G, G)]).then_inc(placed, 1)
                dve.wait_ge(placed, gi + 1)
                for u in range(g * G, (g + 1) * G):
                    last = v.tensor_scalar(onehot[:, u, :], m.iota[:, :], places[:, u:u + 1], None, ALU.is_equal)
                last.then_inc(hot, 1)

            build(0, 0)
            with dve.Fori(0, ITERS) as i:
                for g in range(R):
                    gi = i * R + g
                    build(gi + 1, (g + 1) % R)
                    note(at(gi * (G * W), G * W), gi + 1, (g - 1) % 2)
            note(slice(NPAIRS_PAD * W, (NPAIRS_PAD + G) * W), ITERS * R + 1, 1)

        @block.scalar
        def _(act):
            act.wait_ge(made, 1)
            with act.Fori(0, ITERS) as i:
                for g in range(R):
                    act.wait_ge(flip, i * R + g + 1)
                    act.nop(nofuse=True)
                    act.wait_ge(expd, i * R + g + 1)
                    act.nop(nofuse=True)
                    nc.scalar.activation(turned[:, g * G:(g + 1) * G, :].rearrange("p u e -> p (u e)"), flipped[:, g % 2, 0:G * P], ACT.Copy).then_inc(turn, 1)

        @block.tensor
        def _(pe):
            def expand(gprev, n):
                word = pe.value_load(m.word_row[0:1, at(n - 1)])
                pe.wait_ge(turn, n + 1)
                pe.nop(nofuse=True)
                pe.wait_ge(noted, n)
                pe.nop(nofuse=True)
                for k in range(G):
                    tile = tile_of(pe, word, k)
                    last = nc.tensor.matmul(got[:, gprev % 2, k * 3 * W:(k + 1) * 3 * W], turned[:, gprev * G + k, :],
                                            am3[:, at(tile), :, :].rearrange("p o k w -> p (o k w)"), start=True, stop=True)
                last.then_inc(expd, 1)

            pe.wait_ge(made, 1)
            with pe.Fori(0, ITERS) as i:
                for g in range(R):
                    gi = i * R + g
                    pe.wait_ge(hot, gi + 1)
                    pe.wait_ge(turn, gi + 1)
                    for u in range(g * G, (g + 1) * G):
                        last = nc.tensor.transpose(flipped[:, g % 2, (u - g * G) * P:(u - g * G + 1) * P], onehot[:, u, :], ident_b[:, :])
                    last.then_inc(flip, 1)
                    expand((g - 1) % R, gi + 1)
            expand(R - 1, ITERS * R + 1)


def flip_nodes(nc, m, src, dst):
    with phase(nc) as (sb, ps, sem, block_):
        psum = ps("flip", [P, 2, 4, P])
        flipped, taken = sem("flipped"), sem("taken")
        block = block_()
        groups = [range(t, min(t + 4, NT)) for t in range(0, NT, 4)]

        @block.tensor
        def _(pe):
            for g, tiles in enumerate(groups):
                if g >= 2:
                    pe.wait_ge(taken, g - 1)
                for k, t in enumerate(tiles):
                    last = nc.tensor.transpose(psum[:, g % 2, k, :], src[:, t, 0:D], m.ident[:, :])
                last.then_inc(flipped, 1)

        @block.scalar
        def _(act):
            for g, tiles in enumerate(groups):
                act.wait_ge(flipped, g + 1)
                n = len(tiles)
                nc.scalar.activation(dst[:, tiles[0] * P:(tiles[0] + n) * P].rearrange("p (k e) -> p k e", k=n),
                                     psum[:, g % 2, 0:n, :], ACT.Copy).then_inc(taken, 1)


def project(nc, m, weight, out, scale=None):
    with phase(nc) as (sb, ps, sem, block_):
        w = sb("w", [P, D])
        psum = ps("proj", [P, 4, 512])
        w_in, done, taken = sem("w_in"), sem("done"), sem("taken")
        block = block_()

        @block.sync
        def _(sp):
            sp.dma_start(w[:, :], weight).then_inc(w_in, 16)

        @block.tensor
        def _(pe):
            pe.wait_ge(w_in, 16)
            for t in range(NT):
                if t >= 4:
                    pe.wait_ge(taken, t - 3)
                nc.tensor.matmul(psum[:, t % 4, 0:D], m.hT[:, t * P:(t + 1) * P], w[:, :], start=True, stop=True).then_inc(done, 1)

        @block.scalar
        def _(act):
            for t in range(NT):
                act.wait_ge(done, t + 1)
                kw = {} if scale is None else {"scale": scale[:, t:t + 1]}
                nc.scalar.activation(out[:, t, 0:D], psum[:, t % 4, 0:D], ACT.Copy, **kw).then_inc(taken, 1)


def store_table(nc, table, rows):
    with phase(nc) as (sb, ps, sem, block_):
        out = sem("out")
        block = block_()

        @block.sync
        def _(sp):
            sp.dma_start(table.rearrange("(t p) w -> p t w", p=P), rows).then_inc(out, 16)
            sp.wait_ge(out, 16)


def row_of(v):
    return v.unsqueeze(0).to_broadcast([P, v.shape[0]])


def l0_finish(nc, m):
    with phase(nc) as (sb, ps, sem, block_):
        pos, safe = sb("pos", [P, NT]), sb("safe", [P, NT])
        d_, ready, root = sem("d"), sem("ready"), sem("root")
        block = block_()

        @block.vector
        def _(dve):
            v = nc.vector
            step = Chain(dve, d_)
            step(v.tensor_copy(m.dinv[:, :], m.acc[:, :, D]))
            step(v.tensor_scalar(m.cnt_inv[:, :], m.acc[:, :, D + 1], 1.0, None, ALU.max))
            step(v.reciprocal(m.cnt_inv[:, :], m.cnt_inv[:, :]))
            step(v.tensor_scalar(pos[:, :], m.dinv[:, :], 0.0, None, ALU.is_gt))
            step(v.tensor_tensor(safe[:, :], m.dinv[:, :], pos[:, :], ALU.mult))
            step(v.tensor_tensor(safe[:, :], safe[:, :], pos[:, :], ALU.subtract))
            v.tensor_scalar(safe[:, :], safe[:, :], 1.0, None, ALU.add).then_inc(ready, 1)
            dve.wait_ge(root, 1)
            step(v.reciprocal(safe[:, :], safe[:, :]))
            step(v.tensor_tensor(m.dinv[:, :], safe[:, :], pos[:, :], ALU.mult))
            step(v.scalar_tensor_tensor(m.x[:, :, :], m.h[:, :, :], m.eps1[:, 0:1], m.x[:, :, :], ALU.mult, ALU.add))
            step(v.tensor_tensor(m.x[:, :, :], m.x[:, :, :], m.acc[:, :, 0:D], ALU.add))

        @block.scalar
        def _(act):
            act.wait_ge(ready, 1)
            nc.scalar.activation(safe[:, :], safe[:, :], ACT.Sqrt).then_inc(root, 1)


def gat_layer(nc, m, weight, att_src, att_dst, bias):
    flip_nodes(nc, m, m.h, m.hT)
    rows = m.acc2
    with phase(nc) as (sb0, ps0, sem0, block0):
        hw = sb0("hw", [P, NT, D])
        project(nc, m, weight, hw)
        with phase(nc) as (sb, ps, sem, block_):
            att = [sb(f"att{k}", [P, D]) for k in range(2)]
            prod = sb("prod", [P, NT, D])
            parts = sb("parts", [P, NT, 3, HEADS], BF16)
            rest, back = sb("rest", [P, NT, HEADS]), sb("back", [P, NT, HEADS])
            att_in, d_ = sem("att_in"), sem("d")
            block = block_()

            @block.sync
            def _(sp):
                for k, v in enumerate((att_src, att_dst)):
                    sp.dma_start(att[k][:, :], row_of(v.rearrange("h c -> (h c)"))).then_inc(att_in, 16)

            @block.vector
            def _(dve):
                v = nc.vector
                step = Chain(dve, d_)
                dve.wait_ge(att_in, 32)
                for k, o in enumerate((m.a_src, m.a_dst)):
                    step(v.tensor_tensor(prod[:, :, :], hw[:, :, :], mid(att[k][:, :], NT), ALU.mult))
                    step(v.tensor_reduce(o[:, :, :], prod[:, :, :].rearrange("p t (h c) -> p t h c", h=HEADS), AX.X, ALU.add))
                step(v.tensor_copy(m.top[:, :, :], m.a_src[:, :, :]))
                step(v.tensor_copy(rows[:, :, D:GROW], m.a_src[:, :, :]))
                step(v.tensor_copy(rows[:, :, 0:D], hw[:, :, :]))
                split3(dve, step, v, m.a_src[:, :, :], [parts[:, :, k, :] for k in range(3)], rest[:, :, :], back[:, :, :])
                step(v.tensor_copy(rows[:, :, GROW:].rearrange("p t (k h) -> p t k h", k=3), parts[:, :, :, :]))
    store_table(nc, m.gat_dram, rows[:, :, :])
    gat_max(nc, m)
    with phase(nc) as (sb, ps, sem, block_):
        tmp, own = sb("tmp", [P, NT, HEADS]), sb("own", [P, NT, HEADS])
        d_, ready, exped = sem("d"), sem("ready"), sem("exped")
        block = block_()

        @block.vector
        def _(dve):
            v = nc.vector
            step = Chain(dve, d_)
            step(v.tensor_copy(m.am[:, :, 0:HEADS], m.a_dst[:, :, :]))
            step(v.tensor_tensor(tmp[:, :, :], m.top[:, :, :], m.a_dst[:, :, :], ALU.add))
            step(v.scalar_tensor_tensor(m.am[:, :, HEADS:], tmp[:, :, :], 0.2, tmp[:, :, :], ALU.mult, ALU.max))
            step(v.tensor_tensor(tmp[:, :, :], m.a_src[:, :, :], m.a_dst[:, :, :], ALU.add))
            step(v.scalar_tensor_tensor(own[:, :, :], tmp[:, :, :], 0.2, tmp[:, :, :], ALU.mult, ALU.max))
            v.tensor_tensor(own[:, :, :], own[:, :, :], m.am[:, :, HEADS:], ALU.subtract).then_inc(ready, 1)

        @block.scalar
        def _(act):
            act.wait_ge(ready, 1)
            nc.scalar.activation(m.own[:, :, :], own[:, :, :], ACT.Exp).then_inc(exped, 1)
    gat_expand(nc, m)
    with phase(nc) as (sb, ps, sem, block_):
        d_, ready, exped = sem("d"), sem("ready"), sem("exped")
        block = block_()
        n = NPAIRS_PAD
        asp = m.as_pair[:, 0:n * HEADS].rearrange("p (j h) -> p j h", h=HEADS)
        exp_ = m.ex_pair[:, 0:n * HEADS].rearrange("p (j h) -> p j h", h=HEADS)
        amp = m.am_pair[:, G * 2 * HEADS:(n + G) * 2 * HEADS].rearrange("p (j h) -> p j h", h=2 * HEADS)

        @block.vector
        def _(dve):
            v = nc.vector
            step = Chain(dve, d_)
            step(v.tensor_tensor(asp, asp, amp[:, :, 0:HEADS], ALU.add))
            step(v.scalar_tensor_tensor(exp_, asp, 0.2, asp, ALU.mult, ALU.max))
            step(v.tensor_tensor(exp_, exp_, amp[:, :, HEADS:], ALU.subtract))
            v.tensor_scalar(exp_, exp_, 0.0, None, ALU.min).then_inc(ready, 1)

        @block.scalar
        def _(act):
            act.wait_ge(ready, 1)
            nc.scalar.activation(exp_, exp_, ACT.Exp).then_inc(exped, 1)
    edge_sum(nc, m, m.rows_dram, mode="heads")
    with phase(nc) as (sb, ps, sem, block_):
        b_row, neg = sb("b_row", [P, D]), sb("neg", [P, NT, D])
        b_in, d_, ready, exped = sem("b_in"), sem("d"), sem("ready"), sem("exped")
        block = block_()

        @block.sync
        def _(sp):
            sp.dma_start(b_row[:, :], row_of(bias)).then_inc(b_in, 16)

        @block.vector
        def _(dve):
            v = nc.vector
            step = Chain(dve, d_)
            den = m.acc[:, :, D:GROW]
            step(v.tensor_tensor(den, den, m.own[:, :, :], ALU.add))
            step(v.reciprocal(den, den))
            for h in range(HEADS):
                cols = slice(h * HC, (h + 1) * HC)
                step(v.tensor_tensor(neg[:, :, cols], rows[:, :, cols], bc(m.own[:, :, h], HC), ALU.mult))
                step(v.tensor_tensor(neg[:, :, cols], neg[:, :, cols], m.acc[:, :, cols], ALU.add))
                step(v.tensor_tensor(m.h[:, :, cols], neg[:, :, cols], bc(m.acc[:, :, D + h], HC), ALU.mult))
            dve.wait_ge(b_in, 16)
            step(v.tensor_tensor(m.h[:, :, :], m.h[:, :, :], mid(b_row[:, :], NT), ALU.add))
            v.tensor_scalar(neg[:, :, :], m.h[:, :, :], 0.0, None, ALU.min).then_inc(ready, 1)
            dve.wait_ge(exped, 1)
            step(v.tensor_scalar(neg[:, :, :], neg[:, :, :], -1.0, None, ALU.add))
            step(v.scalar_tensor_tensor(m.h[:, :, :], m.h[:, :, :], 0.0, neg[:, :, :], ALU.max, ALU.add))

        @block.scalar
        def _(act):
            act.wait_ge(ready, 1)
            nc.scalar.activation(neg[:, :, :], neg[:, :, :], ACT.Exp).then_inc(exped, 1)


def add_to_x(nc, m, src):
    with phase(nc) as (sb, ps, sem, block_):
        block = block_()

        @block.vector
        def _(dve):
            nc.vector.tensor_tensor(m.x[:, :, :], m.x[:, :, :], src, ALU.add)


def gcn_layer(nc, m, l, weight, b, gamma, beta):
    project(nc, m, weight, m.acc2, scale=m.dinv)
    store_table(nc, m.gcn_dram[l], m.acc2[:, :, 0:D])
    edge_sum(nc, m, m.gcn_dram[l], index=m.src_pair, weight=m.w1)
    with phase(nc) as (sb, ps, sem, block_):
        d_ = sem("d")
        block = block_()

        @block.vector
        def _(dve):
            nc.vector.tensor_tensor(m.acc[:, :, 0:D], m.acc[:, :, 0:D], bc(m.dinv[:, :], D), ALU.mult).then_inc(d_, 1)
    flip_nodes(nc, m, m.acc, m.hT)
    with phase(nc) as (sb, ps, sem, block_):
        par = sb("par", [P, 3])
        pieces = [(s, min(s + 512, N_NODES)) for s in range(0, N_NODES, 512)]
        stats, mv = sb("stats", [P, len(pieces), 6]), sb("mv", [P, 2])
        scale, shift = sb("scale", [P, 1]), sb("shift", [P, 1])
        p_in, d_, var_ready, root = sem("p_in"), sem("d"), sem("var_ready"), sem("root")
        block = block_()

        @block.sync
        def _(sp):
            with nc.allow_non_contiguous_dma(reason="a number a partition"):
                for k, v in enumerate((b, gamma, beta)):
                    sp.dma_start(par[:, k:k + 1], v.unsqueeze(1)).then_inc(p_in, 16)

        @block.vector
        def _(dve):
            v = nc.vector
            step = Chain(dve, d_)
            dve.wait_ge(p_in, 48)
            if l == 0:
                step(v.tensor_scalar(m.lastT[:, :], m.hT[:, :], par[:, 0:1], None, ALU.add))
            else:
                step(v.scalar_tensor_tensor(m.lastT[:, :], m.hT[:, :], par[:, 0:1], m.lastT[:, :], ALU.add, ALU.add))
            for k, (s, e) in enumerate(pieces):
                step(v.bn_stats(stats[:, k, :], m.lastT[:, s:e]))
            step(v.bn_aggr(mv[:, :], stats[:, :, :].rearrange("p k s -> p (k s)")))
            v.tensor_scalar(scale[:, :], mv[:, 1:2], EPS, None, ALU.add).then_inc(var_ready, 1)
            dve.wait_ge(root, 1)
            step(v.reciprocal(scale[:, :], scale[:, :]))
            step(v.tensor_tensor(scale[:, :], scale[:, :], par[:, 1:2], ALU.mult))
            step(v.tensor_scalar(m.hT[:, :], m.lastT[:, :], mv[:, 0:1], scale[:, 0:1], ALU.subtract, ALU.mult))
            step(v.tensor_scalar(m.hT[:, :], m.hT[:, :], par[:, 2:3], 0.0, ALU.add, ALU.max))

        @block.scalar
        def _(act):
            act.wait_ge(var_ready, 1)
            nc.scalar.activation(scale[:, :], scale[:, :], ACT.Sqrt).then_inc(root, 1)


def rgcn_table(nc, m, rel_weights):
    with phase(nc) as (sb, ps, sem, block_):
        w = sb("w", [P, N_RELS, D])
        rows = sb("rows", [P, 2, N_RELS, D])
        psum = ps("rel", [P, 2, 4, 512])
        w_in, done, taken = sem("w_in"), sem("done"), sem("taken")
        out = [sem("out0"), sem("out1")]
        block = block_()
        table = m.rel_dram.rearrange("(r t p) f -> t p r f", r=N_RELS, p=P)

        @block.sync
        def _(sp):
            sp.dma_start(w[:, :, :], rel_weights.rearrange("r i h -> i r h")).then_inc(w_in, 16)
            for t in range(NT):
                sp.wait_ge(taken, 4 * (t + 1))
                sp.dma_start(table[t], rows[:, t % 2, :, :]).then_inc(out[t % 2], 16)
            for k in range(2):
                sp.wait_ge(out[k], 16 * ((NT + 1 - k) // 2))

        @block.tensor
        def _(pe):
            pe.wait_ge(w_in, 16)
            for t in range(NT):
                for g in range(4):
                    if t >= 2:
                        pe.wait_ge(taken, 4 * (t - 2) + g + 1)
                    nc.tensor.matmul(psum[:, t % 2, g, :], m.hT[:, t * P:(t + 1) * P],
                                     w[:, 4 * g:4 * g + 4, :].rearrange("p r f -> p (r f)"), start=True, stop=True).then_inc(done, 1)

        @block.scalar
        def _(act):
            for t in range(NT):
                if t >= 2:
                    act.wait_ge(out[t % 2], 16 * (t // 2))
                for g in range(4):
                    act.wait_ge(done, 4 * t + g + 1)
                    nc.scalar.activation(rows[:, t % 2, 4 * g:4 * g + 4, :].rearrange("p r f -> p (r f)"),
                                         psum[:, t % 2, g, :], ACT.Copy).then_inc(taken, 1)


def rgcn_finish(nc, m, b_lin, out_dram):
    with phase(nc) as (sb, ps, sem, block_):
        b_row = sb("b_row", [P, D])
        b_in, d_, ready, tanhed, final, out = (sem(n) for n in ("b_in", "d", "ready", "tanhed", "final", "out"))
        block = block_()

        @block.sync
        def _(sp):
            sp.dma_start(b_row[:, :], row_of(b_lin)).then_inc(b_in, 16)
            sp.wait_ge(final, 1)
            sp.dma_start(out_dram[0:(NT - 1) * P, :].rearrange("(t p) f -> p t f", p=P), m.x[:, 0:NT - 1, :]).then_inc(out, 16)
            sp.dma_start(out_dram[(NT - 1) * P:, :], m.x[0:LAST_ROWS, NT - 1, :]).then_inc(out, 16)
            sp.wait_ge(out, 32)

        @block.vector
        def _(dve):
            v = nc.vector
            step = Chain(dve, d_)
            step(v.tensor_tensor(m.acc[:, :, 0:D], m.acc[:, :, 0:D], bc(m.cnt_inv[:, :], D), ALU.mult))
            step(v.tensor_tensor(m.acc[:, :, 0:D], m.acc[:, :, 0:D], m.acc2[:, :, 0:D], ALU.add))
            dve.wait_ge(b_in, 16)
            v.tensor_tensor(m.acc[:, :, 0:D], m.acc[:, :, 0:D], mid(b_row[:, :], NT), ALU.add).then_inc(ready, 1)
            dve.wait_ge(tanhed, 1)
            v.tensor_tensor(m.x[:, :, :], m.x[:, :, :], m.acc[:, :, 0:D], ALU.add).then_inc(final, 1)

        @block.scalar
        def _(act):
            act.wait_ge(ready, 1)
            nc.scalar.activation(m.acc[:, :, 0:D], m.acc[:, :, 0:D], ACT.Tanh).then_inc(tanhed, 1)


class Memory:
    pass


def gnn_kernel(nc, a, out_dram, stop=99):
    m = Memory()
    with ExitStack() as ctx:
        def sb(name, shape, dt=FP32):
            return ctx.enter_context(nc.sbuf_tensor(name, shape, dt))

        m.iota, m.rev, m.ident = sb("iota", [P, P]), sb("rev", [P, P]), sb("ident", [P, P])
        m.pcol, m.revcol = sb("pcol", [P, 1]), sb("revcol", [P, B])
        m.beta, m.eps1 = sb("beta", [P, 1]), sb("eps1", [P, 1])
        m.x, m.h = sb("x", [P, NT, D]), sb("h", [P, NT, D])
        m.acc, m.acc2 = sb("acc", [P, NT, GROW]), sb("acc2", [P, NT, GROW3])
        m.dinv, m.cnt_inv = sb("dinv", [P, NT]), sb("cnt_inv", [P, NT])
        m.src_pair, m.rel_pair = sb("src_pair", [P, NPP], I32), sb("rel_pair", [P, NPP], I32)
        m.loc_pair, m.w1 = sb("loc_pair", [P, NPP]), sb("w1", [P, NPP, 2])
        m.tile_row = sb("tile_row", [1, NPP], I32)
        m.fresh = sb("fresh", [P, NPP])
        m.end_row = sb("end_row", [1, P], I32)
        m.word_row = sb("word_row", [1, 1 + NPP // G], I32)
        m.stage = sb("stage", [P, U], I32)
        def dram(name, shape, dt=FP32):
            return nc.dram_tensor(name, shape, dt, kind="Internal").ap()

        m.rec_dram, m.src_dram, m.ev_dram = dram("rec_dram", [NPP, 4 * P]), dram("src_dram", [NPP * P]), dram("ev_dram", [NPP * P])
        m.l0_dram, m.gat_dram = dram("l0_dram", [NPAD, L0_ROW]), dram("gat_dram", [NPAD, GROW3])
        m.rows_dram, m.rel_dram = dram("rows_dram", [NPAIRS_PAD * P, GROW]), dram("rel_dram", [N_RELS * NPAD, D])
        m.gcn_dram = [dram(f"gcn_dram{l}", [NPAD, D]) for l in range(3)]
        m.tile_dram, m.end_dram = dram("tile_dram", [NPP], I32), dram("end_dram", [P], I32)

        with ExitStack() as early:
            def sb0(name, shape):
                return early.enter_context(nc.sbuf_tensor(name, shape, FP32))

            m.src_col, m.ev_col, m.hi_col, m.lo_col = (sb0(n, [P, NPP]) for n in ("src_col", "ev_col", "hi_col", "lo_col"))
            m.ev_pair = sb0("ev_pair", [P, NPP])
            m.seg_max, m.seg_sum = sb0("seg_max", [P, NT]), sb0("seg_sum", [P, NT])
            setup(nc, a, m)
            source_softmax(nc, m)
            layernorm_relu(nc, m, m.h)
            l0_table(nc, m)
            edge_sum(nc, m, m.l0_dram, index=m.src_pair, mode="source")
            l0_finish(nc, m)

        m.hT = sb("hT", [P, NPAD])
        if stop > 1:
            with ExitStack() as middle:
                def sb1(name, shape):
                    return middle.enter_context(nc.sbuf_tensor(name, shape, FP32))

                m.a_src, m.a_dst, m.top, m.own = (sb1(n, [P, NT, HEADS]) for n in ("a_src", "a_dst", "top", "own"))
                m.am = sb1("am", [P, NT, 2 * HEADS])
                m.as_pair, m.ex_pair = sb1("as_pair", [P, NPP * HEADS]), sb1("ex_pair", [P, NPP * HEADS])
                m.am_pair = sb1("am_pair", [P, (G + NPAIRS_PAD) * 2 * HEADS])
                layernorm_relu(nc, m, m.h)
                gat_layer(nc, m, a["L1_gnn_W1"], a["L1_gnn_att_src1"], a["L1_gnn_att_dst1"], a["L1_gnn_b1"])
                gat_layer(nc, m, a["L1_gnn_W2"], a["L1_gnn_att_src2"], a["L1_gnn_att_dst2"], a["L1_gnn_b2"])
                add_to_x(nc, m, m.h[:, :, :])

        if stop > 2:
            with ExitStack() as late:
                m.lastT = late.enter_context(nc.sbuf_tensor("lastT", [P, NPAD], FP32))
                layernorm_relu(nc, m, m.h)
                flip_nodes(nc, m, m.h, m.hT)
                for l in range(3):
                    gcn_layer(nc, m, l, a["L2_gnn_W"][l], a["L2_gnn_b"][l], a["L2_gnn_gamma"][l], a["L2_gnn_beta"][l])
                flip_nodes(nc, m, m.hT[:, :].rearrange("p (t n) -> p t n", t=NT), m.h[:, :, :].rearrange("p t f -> p (t f)"))
                add_to_x(nc, m, m.h[:, :, :])

        layernorm_relu(nc, m, m.h)
        flip_nodes(nc, m, m.h, m.hT)
        rgcn_table(nc, m, a["L3_gnn_rel_weights"])
        project(nc, m, a["L3_gnn_w_lin"], m.acc2)
        edge_sum(nc, m, m.rel_dram, index=m.rel_pair)
        rgcn_finish(nc, m, a["L3_gnn_b_lin"], out_dram)


_INS = ['x', 'src', 'dst', 'edge_type_16', 'edge_weight', 'L0_gnn_beta', 'L0_gnn_eps', 'L1_gnn_W1', 'L1_gnn_att_src1',
        'L1_gnn_att_dst1', 'L1_gnn_b1', 'L1_gnn_W2', 'L1_gnn_att_src2', 'L1_gnn_att_dst2', 'L1_gnn_b2', 'L2_gnn_W',
        'L2_gnn_b', 'L2_gnn_gamma', 'L2_gnn_beta', 'L3_gnn_rel_weights', 'L3_gnn_w_lin', 'L3_gnn_b_lin']


def kernel(**inputs):
    import numpy as _np
    import concourse.bacc as _bacc
    from concourse import mybir as _mybir
    from concourse.bass_utils import run_bass_kernel_spmd as _run

    nc = _bacc.Bacc("TRN2", target_bir_lowering=False, num_devices=1)
    arrays, args = {}, {}
    for name in _INS:
        v = _np.ascontiguousarray(inputs[name])
        arrays[f"in_{name}"] = v
        args[name] = nc.dram_tensor(f"in_{name}", v.shape, _mybir.dt.from_np(v.dtype), kind="ExternalInput").ap()
    out = nc.dram_tensor("out_x", (N_NODES, D), FP32, kind="ExternalOutput").ap()
    gnn_kernel(nc, args, out)
    r = _run(nc, [arrays], core_ids=[0])
    return r.results[0]["out_x"]
```

```python
from contextlib import ExitStack, contextmanager

import concourse.bass as bass
from concourse import mybir

FP32 = mybir.dt.float32
I32 = mybir.dt.int32
BF16 = mybir.dt.bfloat16
ALU = mybir.AluOpType
ACT = mybir.ActivationFunctionType
AX = mybir.AxisListType

P = 128
N_NODES, D = 3125, 128
N_EDGES = 100000
NT = -(-N_NODES // P)
NPAD = NT * P
LAST_ROWS = N_NODES - (NT - 1) * P
NC_ = -(-N_EDGES // P)
FULL_CHUNKS = N_EDGES // P
TAIL = N_EDGES - FULL_CHUNKS * P
CB = -(-NC_ // P)
NPAIRS = NC_ + NT - 1
G = 4
R = 4
U = R * G
B = 8
BITS = 12
BIT = 2.0 ** 50
ITERS = -(-NPAIRS // U)
NPP = CB * P
NPAIRS_PAD = ITERS * U
HEADS, HC = 4, 32
GROW = D + HEADS
GROW3 = GROW + 3 * HEADS
L0_ROW = D + 2
N_RELS = 16
EPS = 1e-5
BIG = 2.0 ** 100
PAD_NODE = NPAD - 1
FAR = 1 << 20


class Chain:

    def __init__(self, eng, sem, base=0):
        self.eng, self.sem, self.n, self.base = eng, sem, 0, base

    def __call__(self, ins):
        self.n += 1
        ins.then_inc(self.sem, 1)
        self.eng.wait_ge(self.sem, self.base + self.n)


@contextmanager
def phase(nc):
    sems = []
    with ExitStack() as ctx:
        def give_back():
            for s in sems:
                nc.sync.sem_clear(s)
                nc.release_semaphore(s)

        ctx.callback(give_back)

        def sb(name, shape, dt=FP32):
            return ctx.enter_context(nc.sbuf_tensor(f"{name}_{nc.next_id()}", shape, dt))

        def ps(name, shape, dt=FP32):
            return ctx.enter_context(nc.psum_tensor(f"{name}_{nc.next_id()}", shape, dt))

        def sem(name, for_pool_dma=False):
            s = nc.alloc_semaphore(f"{name}_{nc.next_id()}")
            if not for_pool_dma:
                sems.append(s)
            return s

        yield sb, ps, sem, (lambda: ctx.enter_context(nc.Block()))


def bc(ap, n):
    return ap.unsqueeze(len(ap.shape)).to_broadcast([*ap.shape, n])


def mid(ap, n):
    return ap.unsqueeze(1).to_broadcast([ap.shape[0], n, ap.shape[1]])


def at(i, n=1):
    return bass.ds(i, n)


def setup(nc, a, m):
    with phase(nc) as (sb, ps, sem, block_):
        raw = [sb(f"raw{k}", [P, CB, P], I32) for k in range(3)]
        w_raw = sb("w_raw", [P, CB, P])
        rec = sb("rec", [P, CB, 4, P])
        ev = sb("ev", [P, CB, P])
        bit, bits = sb("bit", [P, CB, P], I32), sb("bits", [P, BITS, CB, P], BF16)
        values = sb("values", [P, 3, CB, P], BF16)
        rec_pair = sb("rec_pair", [P, CB, 4 * P])
        ends = sb("ends", [1, NC_ - 1], I32)
        end_tile = sb("end_tile", [1, NC_ - 1], I32)
        keys = sb("keys", [1, NC_ - 1])
        chunk_no = sb("chunk_no", [1, NC_ - 1])
        keys_all = sb("keys_all", [P, NC_ - 1])
        below = sb("below", [P, NC_ - 1])
        jcol = sb("jcol", [P, CB])
        chunk_f = sb("chunk_f", [P, CB])
        chunk_i = sb("chunk_i", [P, CB], I32)
        tile_f = sb("tile_f", [P, CB])
        tile_128 = sb("tile_128", [P, CB])
        tile_cap = sb("tile_cap", [P, CB])
        tile_i = sb("tile_i", [P, CB], I32)
        tile_all_i, tile_all = sb("tile_all_i", [P, NPP], I32), sb("tile_all", [P, NPP])
        tile_first = sb("tile_first", [1, NPP])
        last_pair, last_pair_i = sb("last_pair", [P, 1]), sb("last_pair_i", [P, 1], I32)
        hi_i = sb("hi_i", [P, NPP], I32)
        psum = ps("tp", [P, 2, 4, P])
        made, loaded, ends_in, cleared = sem("made"), sem("loaded"), sem("ends_in"), sem("cleared")
        keyed, spread, coded = sem("keyed"), sem("spread"), sem("coded")
        chunks_known, recs_in = sem("chunks_known"), sem("recs_in", True)
        rec_ready, tile_ready, tile_out, row_in = sem("rec_ready"), sem("tile_ready"), sem("tile_out"), sem("row_in")
        word = sb("word", [1, 1 + NPP // G])
        ends_known, rows_spread = sem("ends_known"), sem("rows_spread")
        stored, local, turned, taken, d_, b_in = sem("stored"), sem("local"), sem("turned"), sem("taken"), sem("d"), sem("b_in")
        block = block_()
        full = (CB - 1) * P * P
        rest = FULL_CHUNKS - (CB - 1) * P

        @block.gpsimd
        def _(pool):
            kw = dict(allow_small_or_imprecise_dtypes=True)
            nc.gpsimd.iota(m.iota[:, :], [[1, P]], 0, 0, **kw).then_inc(made, 1)
            nc.gpsimd.iota(m.pcol[:, :], [[0, 1]], 0, 1, **kw).then_inc(made, 1)
            nc.gpsimd.iota(jcol[:, :], [[P, CB]], 0, 1, **kw).then_inc(made, 1)
            nc.gpsimd.iota(chunk_no[:, :], [[1, NC_ - 1]], 0, 0, **kw).then_inc(made, 1)
            pool.wait_ge(keyed, 1)
            nc.gpsimd.partition_broadcast(keys_all[:, :], keys[:, :]).then_inc(spread, 1)
            pool.wait_ge(row_in, 16)
            nc.gpsimd.partition_broadcast(tile_all_i[:, :], m.tile_row[:, :]).then_inc(rows_spread, 1)
            pool.wait_ge(chunks_known, 1)
            pool.wait_ge(stored, 16)
            for b in range(CB):
                pool.indirect_dma_start(rec_pair[:, b, :], None, m.rec_dram[:, :],
                                        bass.IndirectOffsetOnAxis(ap=chunk_i[:, b:b + 1], axis=0)).then_inc(recs_in, 16)

        @block.sync
        def _(sp):
            with nc.allow_non_contiguous_dma(reason="the last destination of each chunk"):
                sp.dma_start(ends[:, :], a["dst"][0:(NC_ - 1) * P].rearrange("(o c e) -> o c e", o=1, e=P)[:, :, P - 1]).then_inc(ends_in, 16)
                sp.dma_start(m.beta[:, :], a["L0_gnn_beta"].rearrange("(o n) -> o n", o=1).to_broadcast([P, 1])).then_inc(b_in, 16)
                sp.dma_start(m.eps1[:, :], a["L0_gnn_eps"].rearrange("(o n) -> o n", o=1).to_broadcast([P, 1])).then_inc(b_in, 16)
            sp.wait_ge(cleared, 5)
            for name, tile in (("src", raw[0]), ("dst", raw[1]), ("edge_type_16", raw[2]), ("edge_weight", w_raw)):
                v = a[name]
                sp.dma_start(tile[:, 0:CB - 1, :], v[0:full].rearrange("(b c e) -> c b e", c=P, e=P)).then_inc(loaded, 16)
                sp.dma_start(tile[0:rest, CB - 1, :], v[full:FULL_CHUNKS * P].rearrange("(c e) -> c e", e=P)).then_inc(loaded, 16)
                sp.dma_start(tile[rest:rest + 1, CB - 1, 0:TAIL], v[FULL_CHUNKS * P:].rearrange("(c e) -> c e", c=1)).then_inc(loaded, 16)
            sp.dma_start(m.x[:, 0:NT - 1, :], a["x"][0:(NT - 1) * P, :].rearrange("(t p) f -> p t f", p=P)).then_inc(loaded, 16)
            sp.dma_start(m.x[0:LAST_ROWS, NT - 1, :], a["x"][(NT - 1) * P:, :]).then_inc(loaded, 16)
            sp.wait_ge(rec_ready, 1)
            sp.dma_start(m.rec_dram.rearrange("(b c) k -> c b k", c=P), rec[:, :, :, :].rearrange("p b k e -> p b (k e)")).then_inc(stored, 16)
            sp.wait_ge(tile_ready, 1)
            with nc.allow_non_contiguous_dma(reason="one number a pair"):
                sp.dma_start(m.tile_dram.rearrange("(b p) -> p b", p=P), tile_i[:, :]).then_inc(tile_out, 16)
            sp.wait_ge(tile_out, 16)
            sp.dma_start(m.tile_row[:, :], m.tile_dram.rearrange("(o j) -> o j", o=1)).then_inc(row_in, 16)
            sp.wait_ge(ends_known, 1)
            with nc.allow_non_contiguous_dma(reason="one number a tile"):
                sp.dma_start(m.end_dram.rearrange("(p o) -> p o", o=1), last_pair_i[:, :]).then_inc(tile_out, 16)
            sp.wait_ge(tile_out, 32)
            sp.dma_start(m.end_row[:, :], m.end_dram.rearrange("(o j) -> o j", o=1)).then_inc(row_in, 16)
            sp.wait_ge(coded, 1)
            for dram, tile, n in ((m.bits_dram, bits, BITS), (m.values_dram, values, 3)):
                for k in range(n):
                    sp.dma_start(dram[k, :].rearrange("(b c e) -> c b e", c=P, e=P), tile[:, k, :, :]).then_inc(stored, 16)
            sp.wait_ge(row_in, 32)
            sp.wait_ge(stored, 16 * (1 + BITS + 3))

        @block.vector
        def _(dve):
            v = nc.vector
            step = Chain(dve, d_)
            v.memset(raw[0][:, CB - 1, :], PAD_NODE).then_inc(cleared, 1)
            v.memset(raw[1][:, CB - 1, :], FAR).then_inc(cleared, 1)
            v.memset(raw[2][:, CB - 1, :], 0).then_inc(cleared, 1)
            v.memset(w_raw[:, CB - 1, :], 0.0).then_inc(cleared, 1)
            v.memset(m.x[:, NT - 1, :], 0.0).then_inc(cleared, 1)
            v.memset(m.w1[:, :, 1:2], 1.0)
            dve.wait_ge(made, 4)
            v.tensor_scalar(m.ident[:, :], m.iota[:, :], m.pcol[:, 0:1], None, ALU.is_equal)
            dve.wait_ge(ends_in, 16)
            step(v.tensor_scalar(end_tile[:, :], ends[:, :], 7, None, ALU.arith_shift_right))
            step(v.tensor_copy(keys[:, :], end_tile[:, :]))
            v.tensor_tensor(keys[:, :], keys[:, :], chunk_no[:, :], ALU.add).then_inc(keyed, 1)
            dve.wait_ge(loaded, 16 * 14)
            dve.wait_ge(b_in, 32)
            step(v.tensor_scalar(m.eps1[:, :], m.eps1[:, :], 1.0, None, ALU.add))
            step(v.tensor_copy(rec[:, :, 0, :], raw[0][:, :, :]))
            step(v.tensor_copy(rec[:, :, 1, :], raw[1][:, :, :]))
            step(v.tensor_copy(rec[:, :, 2, :], w_raw[:, :, :]))
            step(v.tensor_copy(rec[:, :, 3, :], raw[2][:, :, :]))
            step(v.tensor_scalar(ev[:, :, :], w_raw[:, :, :], m.beta[:, 0:1], None, ALU.mult))
            v.scalar_tensor_tensor(rec[:, :, 3, :], rec[:, :, 3, :], float(NPAD), rec[:, :, 0, :], ALU.mult, ALU.add).then_inc(rec_ready, 1)
            dve.wait_ge(spread, 1)
            for b in range(CB):
                step(v.tensor_scalar(below[:, :], keys_all[:, :], jcol[:, b:b + 1], None, ALU.is_lt, ALU.add, accum_out=chunk_f[:, b:b + 1]))
            v.tensor_copy(chunk_i[:, :], chunk_f[:, :]).then_inc(chunks_known, 1)
            step(v.tensor_tensor(tile_f[:, :], jcol[:, :], chunk_f[:, :], ALU.subtract))
            step(v.tensor_scalar(tile_128[:, :], tile_f[:, :], float(P), None, ALU.mult))
            step(v.tensor_scalar(tile_cap[:, :], tile_f[:, :], float(NT - 1), None, ALU.min))
            v.tensor_copy(tile_i[:, :], tile_cap[:, :]).then_inc(tile_ready, 1)
            dve.wait_ge(rows_spread, 1)
            step(v.tensor_copy(tile_all[:, :], tile_all_i[:, :]))
            step(v.tensor_copy(tile_first[:, :], tile_all_i[0:1, :]))
            step(v.memset(m.fresh[:, 0:1], -BIG))
            step(v.tensor_tensor(m.fresh[:, 1:], tile_all[:, 1:], tile_all[:, 0:NPP - 1], ALU.is_gt))
            step(v.tensor_scalar(m.fresh[:, 1:], m.fresh[:, 1:], -BIG, None, ALU.mult))
            step(v.tensor_scalar(tile_all[:, 0:NPAIRS], tile_all[:, 0:NPAIRS], m.pcol[:, 0:1], None, ALU.is_le, ALU.add, accum_out=last_pair[:, :]))
            step(v.tensor_scalar(last_pair[:, :], last_pair[:, :], -1.0, None, ALU.add))
            v.tensor_copy(last_pair_i[:, :], last_pair[:, :]).then_inc(ends_known, 1)
            step(v.memset(word[:, :], 0.0))
            for k in range(G):
                step(v.scalar_tensor_tensor(word[:, 1:], tile_first[:, k::G], P * 32.0 ** k, word[:, 1:], ALU.mult, ALU.add))
            step(v.tensor_copy(m.word_row[:, :], word[:, :]))
            for k in range(BITS):
                step(v.tensor_scalar(bit[:, :, :], raw[0][:, :, :], k, 1, ALU.arith_shift_right, ALU.bitwise_and))
                step(v.tensor_scalar(bits[:, k, :, :], bit[:, :, :], 2 * BIT, -BIT, ALU.mult, ALU.add))
            split3(dve, step, v, ev[:, :, :], [values[:, k, :, :] for k in range(3)], m.acc[:, 0:CB, 0:P], m.acc2[:, 0:CB, 0:P])
            v.nop().then_inc(coded, 1)
            dve.wait_ge(recs_in, 16 * CB)
            for b in range(CB):
                last = v.tensor_scalar(rec_pair[:, b, P:2 * P], rec_pair[:, b, P:2 * P], tile_128[:, b:b + 1], None, ALU.subtract)
                step(last)
            v.nop().then_inc(local, 1)
            for b in range(CB):
                dve.wait_ge(turned, 2 * b + 1)
                q = psum[:, 0, :, :]
                cols = slice(b * P, b * P + P)
                step(v.tensor_copy(m.src_pair[:, cols], q[:, 0, :]))
                step(v.tensor_copy(m.loc_pair[:, cols], q[:, 1, :]))
                step(v.tensor_copy(m.w1[:, cols, 0], q[:, 2, :]))
                step(v.tensor_copy(m.rel_pair[:, cols], q[:, 3, :]))
                v.tensor_scalar(m.ev_pair[:, cols], q[:, 2, :], m.beta[:, 0:1], None, ALU.mult).then_inc(taken, 1)
                dve.wait_ge(turned, 2 * b + 2)
                step(v.tensor_copy(m.src_col[:, cols], psum[:, 1, 0, :]))
                v.tensor_copy(m.ev_col[:, cols], psum[:, 1, 1, :]).then_inc(taken, 1)
            step(v.tensor_copy(hi_i[:, :], m.src_col[:, :]))
            step(v.tensor_scalar(hi_i[:, :], hi_i[:, :], 7, None, ALU.arith_shift_right))
            step(v.tensor_copy(m.hi_col[:, :], hi_i[:, :]))
            step(v.scalar_tensor_tensor(m.lo_col[:, :], m.hi_col[:, :], -float(P), m.src_col[:, :], ALU.mult, ALU.add))

        @block.tensor
        def _(pe):
            pe.wait_ge(local, 1)
            pe.wait_ge(rec_ready, 1)
            for b in range(CB):
                if b:
                    pe.wait_ge(taken, 2 * b - 1)
                for k in range(4):
                    last = nc.tensor.transpose(psum[:, 0, k, :], rec_pair[:, b, k * P:(k + 1) * P], m.ident[:, :])
                last.then_inc(turned, 1)
                if b:
                    pe.wait_ge(taken, 2 * b)
                nc.tensor.transpose(psum[:, 1, 0, :], rec[:, b, 0, :], m.ident[:, :])
                nc.tensor.transpose(psum[:, 1, 1, :], ev[:, b, :], m.ident[:, :]).then_inc(turned, 1)


def source_softmax(nc, m):
    blocks = -(-NC_ // B)
    blocks += blocks % 2
    assert (blocks + 3) * B <= NPP
    W2 = 2 * NT
    with phase(nc) as (sb, ps, sem, block_):
        left, right = ([sb(f"{n}{b}", [1 + BITS, B * P], BF16) for b in range(2)] for n in ("left", "right"))
        values = [sb(f"values{b}", [3, B * P], BF16) for b in range(2)]
        ones3 = sb("ones3", [3, P], BF16)
        unit = sb("unit", [P, 1])
        onehot = sb("onehot", [P, 2, B, P])
        same = sb("same", [P, 2, B, P], BF16)
        mx, below, ex, mates, per_mate, share = (sb(n, [P, 2, B]) for n in ("mx", "below", "ex", "mates", "per_mate", "share"))
        hi1 = sb("hi1", [P, 2, B, NT])
        moved = sb("moved", [P, 2, B, 3 * NT])
        chunk_max = sb("chunk_max", [P, B, NT])
        block_max, new_max, block_sum = sb("block_max", [P, NT]), sb("new_max", [P, NT]), sb("block_sum", [P, NT])
        gap, shrink = sb("gap", [P, B + 1, NT]), sb("shrink", [P, B + 1, NT])
        scaled = sb("scaled", [P, B, NT])
        alike = ps("alike", [P, 2, B, P])
        psum = ps("node", [P, 2, B, P])
        bits_in = [sem("bits_in0"), sem("bits_in1")]
        made, laid, peaked, gap1, exp1, shared, ready, summed, gap2, exp2, d_ = (sem(n) for n in (
            "made", "laid", "peaked", "gap1", "exp1", "shared", "ready", "summed", "gap2", "exp2", "d"))
        block = block_()
        K = 9

        @block.sync
        def _(sp):
            def load(blk, b):
                for tile in (left[b], right[b]):
                    sp.dma_start(tile[1:, :], m.bits_dram[:, at(blk * (B * P), B * P)]).then_inc(bits_in[b], 16)
                sp.dma_start(values[b][:, :], m.values_dram[:, at(blk * (B * P), B * P)]).then_inc(bits_in[b], 16)

            load(0, 0)
            load(1, 1)
            sp.wait_ge(laid, 1)
            load(2, 0)
            with sp.Fori(0, blocks // 2) as i:
                for b in range(2):
                    blk = i * 2 + b
                    sp.wait_ge(laid, blk + 2)
                    sp.nop(nofuse=True)
                    load(blk + 3, 1 - b)

        @block.vector
        def _(dve):
            v = nc.vector
            for b in range(2):
                v.memset(left[b][0:1, :], BIT)
                v.memset(right[b][0:1, :], -BITS * BIT)
            v.memset(unit[:, :], 1.0)
            v.memset(ones3[:, :], 1.0).then_inc(made, 1)
            v.memset(m.seg_sum[:, :], 0.0)
            v.memset(m.seg_max[:, :], -BIG).then_inc(d_, 1)

            def place(n, b):
                v.tensor_tensor(onehot[:, b, :, :], mid(m.iota[:, :], B), bc(m.lo_col[:, at(n * B, B)], P), ALU.is_equal)

            def begin(n, b):
                cols = at(n * B, B)
                v.tensor_tensor(hi1[:, b, :, :], mid(m.iota[:, 0:NT], B), bc(m.hi_col[:, cols], NT), ALU.is_equal)
                dve.wait_ge(laid, n + 1)
                v.tensor_reduce(mx[:, b, :], alike[:, b, :, :], AX.X, ALU.max).then_inc(peaked, 1)
                dve.wait_ge(peaked, n + 1)
                v.tensor_tensor(below[:, b, :], m.ev_col[:, cols], mx[:, b, :], ALU.subtract).then_inc(gap1, 1)

            def complete(n, b):
                dve.wait_ge(exp1, n + 1)
                v.reciprocal(per_mate[:, b, :], mates[:, b, :]).then_inc(shared, 1)
                v.tensor_copy(moved[:, b, :, W2:], hi1[:, b, :, :])
                dve.wait_ge(shared, n * 2 + 1)
                v.tensor_tensor(share[:, b, :], mx[:, b, :], per_mate[:, b, :], ALU.mult).then_inc(shared, 1)
                v.tensor_tensor(moved[:, b, :, 0:NT], hi1[:, b, :, :], bc(ex[:, b, :], NT), ALU.mult)
                dve.wait_ge(shared, n * 2 + 2)
                v.tensor_tensor(moved[:, b, :, NT:W2], hi1[:, b, :, :], bc(share[:, b, :], NT), ALU.mult).then_inc(ready, 1)

            place(0, 0)
            begin(0, 0)
            complete(0, 0)
            place(1, 1)
            begin(1, 1)
            with dve.Fori(0, blocks // 2) as i:
                for b in range(2):
                    blk = i * 2 + b
                    step = Chain(dve, d_, blk * K + 1)
                    got = psum[:, b, :, :]
                    begin(blk + 2, b)
                    complete(blk + 1, 1 - b)
                    dve.wait_ge(summed, blk + 1)
                    step(v.tensor_scalar(chunk_max[:, :, :], got[:, :, W2:W2 + NT], 1.0, -1.0, ALU.min, ALU.add))
                    step(v.scalar_tensor_tensor(chunk_max[:, :, :], chunk_max[:, :, :], BIG, got[:, :, NT:W2], ALU.mult, ALU.add))
                    step(v.tensor_reduce(block_max[:, :], chunk_max[:, :, :].rearrange("p u h -> p h u"), AX.X, ALU.max))
                    step(v.tensor_tensor(new_max[:, :], m.seg_max[:, :], block_max[:, :], ALU.max))
                    v.tensor_tensor(gap[:, 0:B, :], chunk_max[:, :, :], mid(new_max[:, :], B), ALU.subtract)
                    v.tensor_tensor(gap[:, B, :], m.seg_max[:, :], new_max[:, :], ALU.subtract).then_inc(gap2, 1)
                    place(blk + 2, b)
                    dve.wait_ge(exp2, blk + 1)
                    step(v.tensor_copy(m.seg_max[:, :], new_max[:, :]))
                    step(v.tensor_tensor(scaled[:, :, :], shrink[:, 0:B, :], got[:, :, 0:NT], ALU.mult))
                    step(v.tensor_reduce(block_sum[:, :], scaled[:, :, :].rearrange("p u h -> p h u"), AX.X, ALU.add))
                    step(v.tensor_tensor(m.seg_sum[:, :], m.seg_sum[:, :], shrink[:, B, :], ALU.mult))
                    step(v.tensor_tensor(m.seg_sum[:, :], m.seg_sum[:, :], block_sum[:, :], ALU.add))
                    assert step.n == K

        @block.scalar
        def _(act):
            def weigh(n, b):
                act.wait_ge(gap1, n + 1)
                act.nop(nofuse=True)
                for u in range(B):
                    nc.scalar.activation(same[:, b, u, :], alike[:, b, u, :], ACT.Relu, bias=unit[:, 0:1], scale=1 / (2 * BIG), accum_out=mates[:, b, u:u + 1])
                nc.scalar.activation(ex[:, b, :], below[:, b, :], ACT.Exp).then_inc(exp1, 1)

            act.wait_ge(made, 1)
            weigh(0, 0)
            weigh(1, 1)
            with act.Fori(0, blocks // 2) as i:
                for b in range(2):
                    blk = i * 2 + b
                    weigh(blk + 2, b)
                    act.wait_ge(gap2, blk + 1)
                    act.nop(nofuse=True)
                    nc.scalar.activation(shrink[:, :, :], gap[:, :, :], ACT.Exp).then_inc(exp2, 1)

        @block.tensor
        def _(pe):
            def lay(b, loads):
                pe.wait_ge(bits_in[b], loads)
                for half in range(2):
                    cols = slice(half * 512, (half + 1) * 512)
                    out = alike[:, b, half * 4:half * 4 + 4, :].rearrange("p u e -> p (u e)")
                    nc.tensor.matmul(out, ones3[:, :], values[b][:, cols], start=True, stop=False, skip_group_check=True)
                    for u in range(half * 4, half * 4 + 4):
                        c = slice(u * P, (u + 1) * P)
                        last = nc.tensor.matmul(alike[:, b, u, :], left[b][:, c], right[b][:, c], start=False, stop=True, skip_group_check=True)
                last.then_inc(laid, 1)

            def move(n, b):
                pe.wait_ge(ready, n + 1)
                for u in range(B):
                    last = nc.tensor.matmul(psum[:, b, u, 0:3 * NT], onehot[:, b, u, :], moved[:, b, u, :], start=True, stop=True)
                last.then_inc(summed, 1)

            pe.wait_ge(made, 1)
            lay(0, 48)
            lay(1, 48)
            pe.wait_ge(exp1, 1)
            lay(0, 96)
            move(0, 0)
            with pe.Fori(0, blocks // 2) as i:
                for b in range(2):
                    blk = i * 2 + b
                    pe.wait_ge(exp1, blk + 2)
                    lay(1 - b, (i + b) * 48 + 96)
                    move(blk + 1, 1 - b)


def layernorm_relu(nc, m, out):
    with phase(nc) as (sb, ps, sem, block_):
        total, var = sb("total", [P, NT]), sb("var", [P, NT])
        sq = sb("sq", [P, NT, D])
        d_, var_ready, root = sem("d"), sem("var_ready"), sem("root")
        block = block_()

        @block.vector
        def _(dve):
            v = nc.vector
            step = Chain(dve, d_)
            step(v.tensor_reduce(total[:, :], m.x[:, :, :], AX.X, ALU.add))
            step(v.tensor_scalar(total[:, :], total[:, :], 1.0 / D, None, ALU.mult))
            step(v.tensor_tensor(out[:, :, 0:D], m.x[:, :, :], bc(total[:, :], D), ALU.subtract))
            step(v.tensor_tensor(sq[:, :, :], out[:, :, 0:D], out[:, :, 0:D], ALU.mult))
            step(v.tensor_reduce(var[:, :], sq[:, :, :], AX.X, ALU.add))
            v.tensor_scalar(var[:, :], var[:, :], 1.0 / D, EPS, ALU.mult, ALU.add).then_inc(var_ready, 1)
            dve.wait_ge(root, 1)
            step(v.reciprocal(var[:, :], var[:, :]))
            step(v.tensor_tensor(out[:, :, 0:D], out[:, :, 0:D], bc(var[:, :], D), ALU.mult))
            step(v.tensor_scalar(out[:, :, 0:D], out[:, :, 0:D], 0.0, None, ALU.max))

        @block.scalar
        def _(act):
            act.wait_ge(var_ready, 1)
            nc.scalar.activation(var[:, :], var[:, :], ACT.Sqrt).then_inc(root, 1)


def l0_table(nc, m):
    with phase(nc) as (sb, ps, sem, block_):
        sq, rows = sb("sq", [P, NT, D]), sb("rows", [P, NT, L0_ROW])
        norm, den = sb("norm", [P, NT]), sb("den", [P, NT])
        d_, n2, root, ready, out = sem("d"), sem("n2"), sem("root"), sem("ready"), sem("out")
        block = block_()

        @block.vector
        def _(dve):
            v = nc.vector
            step = Chain(dve, d_)
            step(v.tensor_tensor(sq[:, :, :], m.h[:, :, :], m.h[:, :, :], ALU.mult))
            step(v.tensor_reduce(norm[:, :], sq[:, :, :], AX.X, ALU.add))
            v.tensor_scalar(norm[:, :], norm[:, :], 1e-24, None, ALU.max).then_inc(n2, 1)
            step(v.tensor_scalar(den[:, :], m.seg_sum[:, :], 0.5, None, ALU.max))
            dve.wait_ge(root, 1)
            step(v.tensor_tensor(den[:, :], den[:, :], norm[:, :], ALU.mult))
            step(v.reciprocal(den[:, :], den[:, :]))
            step(v.tensor_scalar(rows[:, :, D], m.seg_max[:, :], -1.0, None, ALU.mult))
            step(v.memset(rows[:, :, D + 1:], 0.0))
            v.tensor_tensor(rows[:, :, 0:D], m.h[:, :, :], bc(den[:, :], D), ALU.mult).then_inc(ready, 1)

        @block.scalar
        def _(act):
            act.wait_ge(n2, 1)
            nc.scalar.activation(norm[:, :], norm[:, :], ACT.Sqrt).then_inc(root, 1)

        @block.sync
        def _(sp):
            sp.wait_ge(ready, 1)
            sp.dma_start(m.l0_dram.rearrange("(t p) w -> p t w", p=P), rows[:, :, :]).then_inc(out, 16)
            sp.wait_ge(out, 16)


L0_ROW = D + 2

def tile_times(pe, word, k, scale):
    down = P.bit_length() - scale.bit_length()
    return pe.snap((word >> (5 * k + down)) & (31 * scale), min_val=0, max_val=31 * scale)


def fetch_groups(nc, pool, m, table, ring, staged, fetched, ring_free):
    with pool.Fori(0, ITERS) as i:
        for g in range(R):
            pool.wait_ge(staged, i * R + g + 1)
            pool.nop(nofuse=True)
            pool.wait_ge(ring_free, i * R + g + 1)
            pool.nop(nofuse=True)
            for u in range(g * G, (g + 1) * G):
                pool.indirect_dma_start(ring[:, u, :], None, table[:, :],
                                        bass.IndirectOffsetOnAxis(ap=m.stage[:, u:u + 1], axis=0)).then_inc(fetched[g], 16)


def edge_sum(nc, m, table, index=None, weight=None, mode="plain"):
    with phase(nc) as (sb, ps, sem, block_):
        gathers = mode != "heads"
        width, extra = {"plain": (D, 0), "source": (L0_ROW, 2), "heads": (GROW, 3 * HEADS)}[mode]
        ring = sb("ring", [P, U, width])
        scaled = ring if mode == "plain" else sb("scaled", [P, U, D + (HEADS if mode == "heads" else extra)])
        if mode == "heads":
            onehot_b, parts = sb("onehot_b", [P, U, P], BF16), sb("parts", [P, U, extra], BF16)
        onehot = sb("onehot", [P, U, P])
        places, weights = sb("places", [P, U]), sb("weights", [P, U])
        p_src, ev = sb("p_src", [P, U]), sb("ev", [P, U])
        zeros = sb("zeros", [P, 512])
        total = ps("total", [P, 8 * 512])
        more = total[:, 7 * 512:]
        room = 16 if mode == "heads" else 2
        narrower = D.bit_length() - room.bit_length()
        fetched = [sem(f"fetched{g}", gathers) for g in range(R)]
        cleared, staged, placed, termed, weighed, hot, summed, scaled_up, closed, d_ = (sem(n) for n in (
            "cleared", "staged", "placed", "termed", "weighed", "hot", "summed", "scaled_up", "closed", "d"))
        block = block_()

        if gathers:
            @block.gpsimd
            def _(pool):
                fetch_groups(nc, pool, m, table, ring, staged, fetched, summed if mode == "plain" else scaled_up)
        else:
            @block.sync
            def _(sp):
                with sp.Fori(0, ITERS) as i:
                    for g in range(R):
                        sp.wait_ge(scaled_up, i * R + g + 1)
                        sp.nop(nofuse=True)
                        sp.dma_start(ring[:, g * G:(g + 1) * G, :],
                                     table[at((i * R + g) * (G * P), G * P), :].rearrange("(u p) w -> p u w", p=P)).then_inc(fetched[g], 16)

        if mode != "plain":
            @block.scalar
            def _(act):
                with act.Fori(0, ITERS) as i:
                    for g in range(R):
                        slots = slice(g * G, (g + 1) * G)
                        if mode == "heads":
                            act.wait_ge(summed, i * R + g + 1)
                            act.nop(nofuse=True)
                            nc.scalar.activation(parts[:, slots, :], m.ex_parts[:, at((i * R + g) * G, G), :], ACT.Copy)
                            nc.scalar.activation(scaled[:, slots, D:], m.ex_pair[:, at((i * R + g) * (G * HEADS), G * HEADS)]
                                                 .rearrange("p (u h) -> p u h", h=HEADS), ACT.Copy).then_inc(termed, 1)
                            continue
                        nc.scalar.activation(ev[:, slots], m.ev_pair[:, at((i * R + g) * G, G)], ACT.Copy).then_inc(termed, 1)
                        act.wait_ge(termed, i * R + g + 1)
                        act.nop(nofuse=True)
                        act.wait_ge(fetched[g], i * 64 + 64)
                        act.nop(nofuse=True)
                        for u in range(g * G, (g + 1) * G):
                            last = nc.scalar.activation(p_src[:, u:u + 1], ev[:, u:u + 1], ACT.Exp, bias=ring[:, u, D:D + 1])
                        last.then_inc(weighed, 1)
                        act.wait_ge(summed, i * R + g + 1)
                        act.nop(nofuse=True)
                        nc.scalar.activation(scaled[:, slots, D:], m.w1[:, at((i * R + g) * G, G), :], ACT.Copy)
                        act.wait_ge(weighed, i * R + g + 1)
                        act.nop(nofuse=True)
                        for u in range(g * G, (g + 1) * G):
                            last = nc.scalar.activation(scaled[:, u, 0:D], ring[:, u, 0:D], ACT.Copy, scale=p_src[:, u:u + 1])
                        last.then_inc(scaled_up, 1)

        @block.vector
        def _(dve):
            v = nc.vector
            v.memset(zeros[:, :], 0.0).then_inc(cleared, 1)
            if gathers:
                for g in range(R):
                    v.tensor_copy(m.stage[:, g * G:(g + 1) * G], index[:, g * G:(g + 1) * G]).then_inc(staged, 1)
            v.sem_inc(summed, R)
            if mode != "plain":
                v.sem_inc(scaled_up, R)

            def build(gi, g):
                slots = slice(g * G, (g + 1) * G)
                dve.wait_ge(summed, gi + 1)
                n = 2 if weight is not None else 1
                v.tensor_copy(places[:, slots], m.loc_pair[:, at(gi * G, G)]).then_inc(placed, 1)
                if weight is not None:
                    v.tensor_copy(weights[:, slots], weight[:, at(gi * G, G), 0]).then_inc(placed, 1)
                dve.wait_ge(placed, gi * n + n)
                for u in range(g * G, (g + 1) * G):
                    last = v.tensor_scalar(onehot[:, u, :], m.iota[:, :], places[:, u:u + 1],
                                           None if weight is None else weights[:, u:u + 1],
                                           ALU.is_equal, ALU.bypass if weight is None else ALU.mult)
                last.then_inc(hot, 1)
                if mode == "heads":
                    for u in range(g * G, (g + 1) * G):
                        v.tensor_scalar(onehot_b[:, u, :], m.iota[:, :], places[:, u:u + 1], None, ALU.is_equal)

            build(0, 0)
            with dve.Fori(0, ITERS) as i:
                for g in range(R):
                    gi = i * R + g
                    slots = slice(g * G, (g + 1) * G)
                    build(gi + 1, (g + 1) % R)
                    if gathers:
                        dve.wait_ge(fetched[g], i * 64 + 64)
                        v.tensor_copy(m.stage[:, slots], index[:, at((gi + R) * G, G)]).then_inc(staged, 1)
                    else:
                        dve.wait_ge(fetched[g], i * 16 + 16)
                        dve.wait_ge(termed, gi + 1)
                        v.tensor_tensor(scaled[:, slots, 0:D].rearrange("p u (h c) -> p u h c", h=HEADS),
                                        ring[:, slots, 0:D].rearrange("p u (h c) -> p u h c", h=HEADS),
                                        bc(scaled[:, slots, D:], HC), ALU.mult).then_inc(scaled_up, 1)
            step = Chain(dve, d_)
            dve.wait_ge(closed, 1)
            for b in range(7):
                tiles = slice(4 * b, min(4 * b + 4, NT))
                n = min(4 * b + 4, NT) - 4 * b
                step(v.tensor_copy(m.acc[:, tiles, 0:D], total[:, b * 512:b * 512 + n * D].rearrange("p (t f) -> p t f", f=D)))
            if mode == "heads":
                step(v.tensor_reduce(m.acc[:, :, D:GROW], more[:, 0:NT * room].rearrange("p (t k h) -> p t h k", k=room // HEADS, h=HEADS)[:, :, :, 0:3], AX.X, ALU.add))
            elif extra:
                step(v.tensor_copy(m.acc[:, :, D:D + extra], more[:, 0:NT * room].rearrange("p (t f) -> p t f", f=room)))

        @block.tensor
        def _(pe):
            pe.wait_ge(cleared, 1)
            for b in range(7):
                nc.tensor.matmul(total[:, b * 512:(b + 1) * 512], zeros[:, 0:P], zeros[:, :], start=True, stop=False)
            if extra:
                nc.tensor.matmul(more, zeros[:, 0:P], zeros[:, :], start=True, stop=False)
            with pe.Fori(0, ITERS) as i:
                for g in range(R):
                    gi = i * R + g
                    word = pe.value_load(m.word_row[0:1, at(gi + 1)])
                    if mode == "plain":
                        pe.wait_ge(fetched[g], i * 64 + 64)
                    else:
                        pe.wait_ge(scaled_up, gi + R + 1)
                    pe.nop(nofuse=True)
                    if mode != "heads":
                        pe.wait_ge(hot, gi + 1)
                        pe.nop(nofuse=True)
                    for k in range(G):
                        u, col = g * G + k, tile_times(pe, word, k, D)
                        last = nc.tensor.matmul(total[:, at(col, D)], onehot[:, u, :], scaled[:, u, 0:D], start=False, stop=False, skip_group_check=True)
                        if extra:
                            left, right = (onehot_b[:, u, :], parts[:, u, :]) if mode == "heads" else (onehot[:, u, :], scaled[:, u, D:])
                            last = nc.tensor.matmul(more[:, at(col >> narrower, extra)], left, right, start=False, stop=False, skip_group_check=True)
                    last.then_inc(summed, 1)
            for b in range(7):
                last = nc.tensor.matmul(total[:, b * 512:(b + 1) * 512], zeros[:, 0:P], zeros[:, :], start=False, stop=True)
            if extra:
                last = nc.tensor.matmul(more, zeros[:, 0:P], zeros[:, :], start=False, stop=True)
            last.then_inc(closed, 1)


def gat_max(nc, m):
    with phase(nc) as (sb, ps, sem, block_):
        NTERM = 3 * HEADS
        ring = sb("ring", [P, U, GROW3])
        terms = sb("terms", [P, R, P], BF16)
        terms_t = sb("terms_t", [P, R, P], BF16)
        ident_b = sb("ident_b", [P, P], BF16)
        row_no, hit, which = sb("row_no", [P, G, HEADS]), sb("hit", [P, G, HEADS]), sb("which", [P, G, HEADS])
        pick = sb("pick", [P, G, HEADS, P], BF16)
        other = sb("other", [P, U, P], BF16)
        minus = sb("minus", [P, HEADS, P], BF16)
        places = sb("places", [P, U])
        part = sb("part", [P, G + NPAIRS_PAD, HEADS])
        upto = sb("upto", [P, HEADS, NPAIRS_PAD])
        spread = ps("spread", [P, 2, 2, HEADS * P])
        flipped = ps("flipped", [P, 2, 1024], BF16)
        fetched = [sem(f"fetched{g}", True) for g in range(R)]
        stored = [sem(f"stored{g}") for g in range(R)]
        staged, ring_free, placed, hot, spr, red, noted, flip, turned, made, counted, d_ = (
            sem(n) for n in ("staged", "ring_free", "placed", "hot", "spr", "red", "noted", "flip", "turned", "made", "counted", "d"))
        block = block_()

        @block.gpsimd
        def _(pool):
            nc.gpsimd.iota(row_no[:, :, :], [[-NTERM, G], [-1, HEADS]], 0, 1, allow_small_or_imprecise_dtypes=True).then_inc(counted, 1)
            fetch_groups(nc, pool, m, m.gat_dram, ring, staged, fetched, ring_free)

        @block.sync
        def _(sp):
            with sp.Fori(0, ITERS) as i:
                for g in range(R):
                    gi = i * R + g
                    sp.wait_ge(fetched[g], i * 64 + 64)
                    sp.nop(nofuse=True)
                    sp.dma_start(m.rows_dram[at(gi * (G * P), G * P), :].rearrange("(u p) w -> p u w", p=P),
                                 ring[:, g * G:(g + 1) * G, 0:GROW]).then_inc(stored[g], 16)
                    sp.wait_ge(noted, gi + 1)
                    sp.nop(nofuse=True)
                    sp.wait_ge(stored[g], i * 16 + 16)
                    sp.nop(nofuse=True)
                    sp.sem_inc(ring_free, 1)

        @block.scalar
        def _(act):
            act.wait_ge(made, 1)
            with act.Fori(0, ITERS) as i:
                for g in range(R):
                    gi = i * R + g
                    slots = slice(g * G, (g + 1) * G)
                    act.wait_ge(fetched[g], i * 64 + 64)
                    act.nop(nofuse=True)
                    nc.scalar.activation(m.as_pair[:, at(gi * (G * HEADS), G * HEADS)].rearrange("p (u h) -> p u h", h=HEADS),
                                         ring[:, slots, D:GROW], ACT.Copy)
                    nc.scalar.activation(terms[:, g, 0:G * NTERM].rearrange("p (u k) -> p u k", k=NTERM),
                                         ring[:, slots, GROW:], ACT.Copy).then_inc(noted, 1)
                    act.wait_ge(flip, gi + 1)
                    act.nop(nofuse=True)
                    nc.scalar.activation(terms_t[:, g, :], flipped[:, g % 2, 0:P], ACT.Copy).then_inc(turned, 1)

        @block.vector
        def _(dve):
            v = nc.vector
            step = Chain(dve, d_)
            step(v.tensor_copy(ident_b[:, :], m.ident[:, :]))
            step(v.memset(terms[:, :, :], 0.0))
            step(v.memset(terms_t[:, R - 1, :], 0.0))
            step(v.memset(other[:, U - G:, :], 0.0))
            for h in range(HEADS):
                step(v.tensor_scalar(minus[:, h, :], m.ident[:, :], -BIG, None, ALU.mult))
            dve.wait_ge(counted, 1)
            step(v.tensor_scalar(which[:, :, :], row_no[:, :, :], 0.0, None, ALU.is_equal))
            for k in (1, 2):
                step(v.tensor_scalar(hit[:, :, :], row_no[:, :, :], float(k * HEADS), None, ALU.is_equal))
                step(v.tensor_tensor(which[:, :, :], which[:, :, :], hit[:, :, :], ALU.add))
            step(v.tensor_copy(pick[:, :, :, :], bc(which[:, :, :], P)))
            v.sem_inc(made, 1)
            v.sem_inc(ring_free, R)
            v.sem_inc(red, 2)
            v.sem_inc(hot, 1)
            v.sem_inc(turned, 2)
            for g in range(R):
                v.tensor_copy(m.stage[:, g * G:(g + 1) * G], m.src_pair[:, g * G:(g + 1) * G]).then_inc(staged, 1)

            def maxima(first, unit, k):
                dve.wait_ge(spr, unit)
                v.tensor_reduce(part[:, first, :].rearrange("p u h -> p (u h)"),
                                spread[:, k, :, :].rearrange("p u (h e) -> p (u h) e", h=HEADS), AX.X, ALU.max).then_inc(red, 1)

            with dve.Fori(0, ITERS) as i:
                for g in range(R):
                    gi = i * R + g
                    slots = slice(g * G, (g + 1) * G)
                    v.tensor_copy(places[:, slots], m.loc_pair[:, at(gi * G, G)]).then_inc(placed, 1)
                    dve.wait_ge(placed, gi + 1)
                    for u in range(g * G, (g + 1) * G):
                        last = v.tensor_scalar(other[:, u, :], m.iota[:, :], places[:, u:u + 1], None, ALU.not_equal)
                    last.then_inc(hot, 1)
                    for k in range(2):
                        maxima(at(gi * G + 2 * k, 2), gi * 2 + k + 1, k)
                    dve.wait_ge(fetched[g], i * 64 + 64)
                    v.tensor_copy(m.stage[:, slots], m.src_pair[:, at((gi + R) * G, G)]).then_inc(staged, 1)
            for k in range(2):
                maxima(slice(NPAIRS_PAD + 2 * k, NPAIRS_PAD + 2 * k + 2), ITERS * R * 2 + k + 1, k)
            dve.wait_ge(red, 2 * (ITERS * R + 1) + 2)
            for h in range(HEADS):
                step(v.tensor_tensor_scan(upto[:, h, :], m.fresh[:, 0:NPAIRS_PAD], part[:, G:, h], -BIG, ALU.add, ALU.max))
            with dve.Fori(0, NT) as t:
                end = dve.value_load(m.end_row[0:1, at(t)], min_val=0, max_val=NPAIRS - 1)
                top = m.top[:, at(t), :].rearrange("p o h -> p (o h)")
                v.tensor_tensor(top, top, upto[:, :, at(end)].rearrange("p h o -> p (h o)"), ALU.max)

        @block.tensor
        def _(pe):
            def spread_pairs(gprev, n):
                pe.wait_ge(turned, n + 1)
                pe.wait_ge(hot, n)
                for k in range(2):
                    pe.wait_ge(red, 2 * n - 1 + k)
                    for w in range(2):
                        u = 2 * k + w
                        nc.tensor.matmul(spread[:, k, w, :], other[:, gprev * G + u, :], minus[:, :, :].rearrange("p h e -> p (h e)"), start=True, stop=False)
                        for h in range(HEADS):
                            last = nc.tensor.matmul(spread[:, k, w, h * P:(h + 1) * P], pick[:, u, h, :], terms_t[:, gprev, :],
                                                    start=False, stop=h == HEADS - 1)
                    last.then_inc(spr, 1)

            pe.wait_ge(made, 1)
            with pe.Fori(0, ITERS) as i:
                for g in range(R):
                    gi = i * R + g
                    pe.wait_ge(noted, gi + 1)
                    pe.wait_ge(turned, gi + 1)
                    nc.tensor.transpose(flipped[:, g % 2, 0:P], terms[:, g, :], ident_b[:, :]).then_inc(flip, 1)
                    spread_pairs((g - 1) % R, gi + 1)
            spread_pairs(R - 1, ITERS * R + 1)


def split3(dve, step, v, x, parts, rest, back):
    step(v.tensor_copy(rest, x))
    for k, part in enumerate(parts):
        step(v.tensor_copy(part, rest))
        step(v.tensor_copy(back, part))
        if k < 2:
            step(v.tensor_tensor(rest, rest, back, ALU.subtract))


def gat_expand(nc, m):
    with phase(nc) as (sb, ps, sem, block_):
        W = 2 * HEADS
        onehot, turned = sb("onehot", [P, U, P], BF16), sb("turned", [P, U, P], BF16)
        am3 = sb("am3", [P, 32, 4, W], BF16)
        rest, back = sb("rest", [P, NT, W]), sb("back", [P, NT, W])
        ident_b = sb("ident_b", [P, P], BF16)
        places = sb("places", [P, U])
        flipped = ps("flipped", [P, 2, 1024], BF16)
        got = ps("got", [P, 2, 512])
        placed, hot, flip, turn, expd, noted, made, d_ = (sem(n) for n in ("placed", "hot", "flip", "turn", "expd", "noted", "made", "d"))
        block = block_()

        @block.vector
        def _(dve):
            v = nc.vector
            step = Chain(dve, d_)
            step(v.tensor_copy(ident_b[:, :], m.ident[:, :]))
            step(v.memset(turned[:, U - G:, :], 0.0))
            split3(dve, step, v, m.am[:, :, :], [am3[:, 0:NT, k, :] for k in range(3)], rest[:, :, :], back[:, :, :])
            v.sem_inc(made, 1)
            v.sem_inc(turn, 2)
            v.sem_inc(noted, 2)

            def note(first, n, k):
                dve.wait_ge(expd, n)
                v.tensor_reduce(m.am_pair[:, first].rearrange("p (u w) -> p u w", w=W),
                                got[:, k, 0:G * 3 * W].rearrange("p (u k w) -> p u w k", k=3, w=W), AX.X, ALU.add).then_inc(noted, 1)

            def build(gi, g):
                slots = slice(g * G, (g + 1) * G)
                v.tensor_copy(places[:, slots], m.loc_pair[:, at(gi * G, G)]).then_inc(placed, 1)
                dve.wait_ge(placed, gi + 1)
                for u in range(g * G, (g + 1) * G):
                    last = v.tensor_scalar(onehot[:, u, :], m.iota[:, :], places[:, u:u + 1], None, ALU.is_equal)
                last.then_inc(hot, 1)

            build(0, 0)
            with dve.Fori(0, ITERS) as i:
                for g in range(R):
                    gi = i * R + g
                    build(gi + 1, (g + 1) % R)
                    note(at(gi * (G * W), G * W), gi + 1, (g - 1) % 2)
            note(slice(NPAIRS_PAD * W, (NPAIRS_PAD + G) * W), ITERS * R + 1, 1)

        @block.scalar
        def _(act):
            act.wait_ge(made, 1)
            with act.Fori(0, ITERS) as i:
                for g in range(R):
                    act.wait_ge(flip, i * R + g + 1)
                    act.nop(nofuse=True)
                    act.wait_ge(expd, i * R + g + 1)
                    act.nop(nofuse=True)
                    nc.scalar.activation(turned[:, g * G:(g + 1) * G, :].rearrange("p u e -> p (u e)"), flipped[:, g % 2, 0:G * P], ACT.Copy).then_inc(turn, 1)

        @block.tensor
        def _(pe):
            def expand(gprev, n):
                word = pe.value_load(m.word_row[0:1, at(n - 1)])
                pe.wait_ge(turn, n + 1)
                pe.nop(nofuse=True)
                for k in range(G):
                    col = tile_times(pe, word, k, 4 * W)
                    last = nc.tensor.matmul(got[:, gprev % 2, k * 3 * W:(k + 1) * 3 * W], turned[:, gprev * G + k, :],
                                            am3[:, :, :, :].rearrange("p t k w -> p (t k w)")[:, at(col, 3 * W)], start=True, stop=True)
                last.then_inc(expd, 1)

            pe.wait_ge(made, 1)
            with pe.Fori(0, ITERS) as i:
                for g in range(R):
                    gi = i * R + g
                    pe.wait_ge(hot, gi + 1)
                    for u in range(g * G, (g + 1) * G):
                        last = nc.tensor.transpose(flipped[:, g % 2, (u - g * G) * P:(u - g * G + 1) * P], onehot[:, u, :], ident_b[:, :])
                    last.then_inc(flip, 1)
                    expand((g - 1) % R, gi + 1)
            pe.wait_ge(noted, ITERS * R + 1)
            expand(R - 1, ITERS * R + 1)


def flip_nodes(nc, m, src, dst):
    with phase(nc) as (sb, ps, sem, block_):
        psum = ps("flip", [P, 2, 4, P])
        flipped, taken = sem("flipped"), sem("taken")
        block = block_()
        groups = [range(t, min(t + 4, NT)) for t in range(0, NT, 4)]

        @block.tensor
        def _(pe):
            for g, tiles in enumerate(groups):
                if g >= 2:
                    pe.wait_ge(taken, g - 1)
                for k, t in enumerate(tiles):
                    last = nc.tensor.transpose(psum[:, g % 2, k, :], src[:, t, 0:D], m.ident[:, :])
                last.then_inc(flipped, 1)

        @block.scalar
        def _(act):
            for g, tiles in enumerate(groups):
                act.wait_ge(flipped, g + 1)
                n = len(tiles)
                nc.scalar.activation(dst[:, tiles[0] * P:(tiles[0] + n) * P].rearrange("p (k e) -> p k e", k=n),
                                     psum[:, g % 2, 0:n, :], ACT.Copy).then_inc(taken, 1)


def project(nc, m, weight, out, scale=None):
    with phase(nc) as (sb, ps, sem, block_):
        w = sb("w", [P, D])
        psum = ps("proj", [P, 4, 512])
        w_in, done, taken = sem("w_in"), sem("done"), sem("taken")
        block = block_()

        @block.sync
        def _(sp):
            sp.dma_start(w[:, :], weight).then_inc(w_in, 16)

        @block.tensor
        def _(pe):
            pe.wait_ge(w_in, 16)
            for t in range(NT):
                if t >= 4:
                    pe.wait_ge(taken, t - 3)
                nc.tensor.matmul(psum[:, t % 4, 0:D], m.hT[:, t * P:(t + 1) * P], w[:, :], start=True, stop=True).then_inc(done, 1)

        @block.scalar
        def _(act):
            for t in range(NT):
                act.wait_ge(done, t + 1)
                kw = {} if scale is None else {"scale": scale[:, t:t + 1]}
                nc.scalar.activation(out[:, t, 0:D], psum[:, t % 4, 0:D], ACT.Copy, **kw).then_inc(taken, 1)


def store_table(nc, table, rows):
    with phase(nc) as (sb, ps, sem, block_):
        out = sem("out")
        block = block_()

        @block.sync
        def _(sp):
            sp.dma_start(table.rearrange("(t p) w -> p t w", p=P), rows).then_inc(out, 16)
            sp.wait_ge(out, 16)


def row_of(v):
    return v.unsqueeze(0).to_broadcast([P, v.shape[0]])


def l0_finish(nc, m):
    with phase(nc) as (sb, ps, sem, block_):
        pos, safe = sb("pos", [P, NT]), sb("safe", [P, NT])
        d_, ready, root = sem("d"), sem("ready"), sem("root")
        block = block_()

        @block.vector
        def _(dve):
            v = nc.vector
            step = Chain(dve, d_)
            step(v.tensor_copy(m.dinv[:, :], m.acc[:, :, D]))
            step(v.tensor_scalar(m.cnt_inv[:, :], m.acc[:, :, D + 1], 1.0, None, ALU.max))
            step(v.reciprocal(m.cnt_inv[:, :], m.cnt_inv[:, :]))
            step(v.tensor_scalar(pos[:, :], m.dinv[:, :], 0.0, None, ALU.is_gt))
            step(v.tensor_tensor(safe[:, :], m.dinv[:, :], pos[:, :], ALU.mult))
            step(v.tensor_tensor(safe[:, :], safe[:, :], pos[:, :], ALU.subtract))
            v.tensor_scalar(safe[:, :], safe[:, :], 1.0, None, ALU.add).then_inc(ready, 1)
            dve.wait_ge(root, 1)
            step(v.reciprocal(safe[:, :], safe[:, :]))
            step(v.tensor_tensor(m.dinv[:, :], safe[:, :], pos[:, :], ALU.mult))
            step(v.scalar_tensor_tensor(m.x[:, :, :], m.h[:, :, :], m.eps1[:, 0:1], m.x[:, :, :], ALU.mult, ALU.add))
            step(v.tensor_tensor(m.x[:, :, :], m.x[:, :, :], m.acc[:, :, 0:D], ALU.add))

        @block.scalar
        def _(act):
            act.wait_ge(ready, 1)
            nc.scalar.activation(safe[:, :], safe[:, :], ACT.Sqrt).then_inc(root, 1)


def gat_layer(nc, m, weight, att_src, att_dst, bias):
    flip_nodes(nc, m, m.h, m.hT)
    rows = m.acc2
    with phase(nc) as (sb0, ps0, sem0, block0):
        hw = sb0("hw", [P, NT, D])
        project(nc, m, weight, hw)
        with phase(nc) as (sb, ps, sem, block_):
            att = [sb(f"att{k}", [P, D]) for k in range(2)]
            prod = sb("prod", [P, NT, D])
            parts = sb("parts", [P, NT, 3, HEADS], BF16)
            rest, back = sb("rest", [P, NT, HEADS]), sb("back", [P, NT, HEADS])
            att_in, d_ = sem("att_in"), sem("d")
            block = block_()

            @block.sync
            def _(sp):
                for k, v in enumerate((att_src, att_dst)):
                    sp.dma_start(att[k][:, :], row_of(v.rearrange("h c -> (h c)"))).then_inc(att_in, 16)

            @block.vector
            def _(dve):
                v = nc.vector
                step = Chain(dve, d_)
                dve.wait_ge(att_in, 32)
                for k, o in enumerate((m.a_src, m.a_dst)):
                    step(v.tensor_tensor(prod[:, :, :], hw[:, :, :], mid(att[k][:, :], NT), ALU.mult))
                    step(v.tensor_reduce(o[:, :, :], prod[:, :, :].rearrange("p t (h c) -> p t h c", h=HEADS), AX.X, ALU.add))
                step(v.tensor_copy(m.top[:, :, :], m.a_src[:, :, :]))
                step(v.tensor_copy(rows[:, :, D:GROW], m.a_src[:, :, :]))
                step(v.tensor_copy(rows[:, :, 0:D], hw[:, :, :]))
                split3(dve, step, v, m.a_src[:, :, :], [parts[:, :, k, :] for k in range(3)], rest[:, :, :], back[:, :, :])
                step(v.tensor_copy(rows[:, :, GROW:].rearrange("p t (k h) -> p t k h", k=3), parts[:, :, :, :]))
    store_table(nc, m.gat_dram, rows[:, :, :])
    gat_max(nc, m)
    with phase(nc) as (sb, ps, sem, block_):
        tmp, own = sb("tmp", [P, NT, HEADS]), sb("own", [P, NT, HEADS])
        d_, ready, exped = sem("d"), sem("ready"), sem("exped")
        block = block_()

        @block.vector
        def _(dve):
            v = nc.vector
            step = Chain(dve, d_)
            step(v.tensor_copy(m.am[:, :, 0:HEADS], m.a_dst[:, :, :]))
            step(v.tensor_tensor(tmp[:, :, :], m.top[:, :, :], m.a_dst[:, :, :], ALU.add))
            step(v.scalar_tensor_tensor(m.am[:, :, HEADS:], tmp[:, :, :], 0.2, tmp[:, :, :], ALU.mult, ALU.max))
            step(v.tensor_tensor(tmp[:, :, :], m.a_src[:, :, :], m.a_dst[:, :, :], ALU.add))
            step(v.scalar_tensor_tensor(own[:, :, :], tmp[:, :, :], 0.2, tmp[:, :, :], ALU.mult, ALU.max))
            v.tensor_tensor(own[:, :, :], own[:, :, :], m.am[:, :, HEADS:], ALU.subtract).then_inc(ready, 1)

        @block.scalar
        def _(act):
            act.wait_ge(ready, 1)
            nc.scalar.activation(m.own[:, :, :], own[:, :, :], ACT.Exp).then_inc(exped, 1)
    gat_expand(nc, m)
    with nc.sbuf_tensor(f"ex_parts_{nc.next_id()}", [P, NPAIRS_PAD, 3 * HEADS], BF16) as m.ex_parts:
        with phase(nc) as (sb, ps, sem, block_):
            d_, ready, exped = sem("d"), sem("ready"), sem("exped")
            block = block_()
            n = NPAIRS_PAD
            asp = m.as_pair[:, 0:n * HEADS].rearrange("p (j h) -> p j h", h=HEADS)
            exp_ = m.ex_pair[:, 0:n * HEADS].rearrange("p (j h) -> p j h", h=HEADS)
            amp = m.am_pair[:, G * 2 * HEADS:(n + G) * 2 * HEADS].rearrange("p (j h) -> p j h", h=2 * HEADS)

            @block.vector
            def _(dve):
                v = nc.vector
                step = Chain(dve, d_)
                step(v.tensor_tensor(asp, asp, amp[:, :, 0:HEADS], ALU.add))
                step(v.scalar_tensor_tensor(exp_, asp, 0.2, asp, ALU.mult, ALU.max))
                step(v.tensor_tensor(exp_, exp_, amp[:, :, HEADS:], ALU.subtract))
                v.tensor_scalar(exp_, exp_, 0.0, None, ALU.min).then_inc(ready, 1)
                dve.wait_ge(exped, 1)
                rest = m.am_pair[:, 0:n * HEADS].rearrange("p (j h) -> p j h", h=HEADS)
                step(v.tensor_copy(m.ex_parts[:, :, 0:HEADS], exp_))
                step(v.tensor_tensor(rest, exp_, m.ex_parts[:, :, 0:HEADS], ALU.subtract))
                step(v.tensor_copy(m.ex_parts[:, :, HEADS:2 * HEADS], rest))
                step(v.tensor_tensor(rest, rest, m.ex_parts[:, :, HEADS:2 * HEADS], ALU.subtract))
                step(v.tensor_copy(m.ex_parts[:, :, 2 * HEADS:], rest))

            @block.scalar
            def _(act):
                act.wait_ge(ready, 1)
                nc.scalar.activation(exp_, exp_, ACT.Exp).then_inc(exped, 1)
        edge_sum(nc, m, m.rows_dram, mode="heads")
    with phase(nc) as (sb, ps, sem, block_):
        b_row, neg = sb("b_row", [P, D]), sb("neg", [P, NT, D])
        b_in, d_, ready, exped = sem("b_in"), sem("d"), sem("ready"), sem("exped")
        block = block_()

        @block.sync
        def _(sp):
            sp.dma_start(b_row[:, :], row_of(bias)).then_inc(b_in, 16)

        @block.vector
        def _(dve):
            v = nc.vector
            step = Chain(dve, d_)
            den = m.acc[:, :, D:GROW]
            step(v.tensor_tensor(den, den, m.own[:, :, :], ALU.add))
            step(v.reciprocal(den, den))
            for h in range(HEADS):
                cols = slice(h * HC, (h + 1) * HC)
                step(v.tensor_tensor(neg[:, :, cols], rows[:, :, cols], bc(m.own[:, :, h], HC), ALU.mult))
                step(v.tensor_tensor(neg[:, :, cols], neg[:, :, cols], m.acc[:, :, cols], ALU.add))
                step(v.tensor_tensor(m.h[:, :, cols], neg[:, :, cols], bc(m.acc[:, :, D + h], HC), ALU.mult))
            dve.wait_ge(b_in, 16)
            step(v.tensor_tensor(m.h[:, :, :], m.h[:, :, :], mid(b_row[:, :], NT), ALU.add))
            v.tensor_scalar(neg[:, :, :], m.h[:, :, :], 0.0, None, ALU.min).then_inc(ready, 1)
            dve.wait_ge(exped, 1)
            step(v.tensor_scalar(neg[:, :, :], neg[:, :, :], -1.0, None, ALU.add))
            step(v.scalar_tensor_tensor(m.h[:, :, :], m.h[:, :, :], 0.0, neg[:, :, :], ALU.max, ALU.add))

        @block.scalar
        def _(act):
            act.wait_ge(ready, 1)
            nc.scalar.activation(neg[:, :, :], neg[:, :, :], ACT.Exp).then_inc(exped, 1)


def add_to_x(nc, m, src):
    with phase(nc) as (sb, ps, sem, block_):
        block = block_()

        @block.vector
        def _(dve):
            nc.vector.tensor_tensor(m.x[:, :, :], m.x[:, :, :], src, ALU.add)


def gcn_layer(nc, m, l, weight, b, gamma, beta):
    project(nc, m, weight, m.acc2, scale=m.dinv)
    store_table(nc, m.gcn_dram[l], m.acc2[:, :, 0:D])
    edge_sum(nc, m, m.gcn_dram[l], index=m.src_pair, weight=m.w1)
    with phase(nc) as (sb, ps, sem, block_):
        d_ = sem("d")
        block = block_()

        @block.vector
        def _(dve):
            nc.vector.tensor_tensor(m.acc[:, :, 0:D], m.acc[:, :, 0:D], bc(m.dinv[:, :], D), ALU.mult).then_inc(d_, 1)
    flip_nodes(nc, m, m.acc, m.hT)
    with phase(nc) as (sb, ps, sem, block_):
        par = sb("par", [P, 3])
        pieces = [(s, min(s + 512, N_NODES)) for s in range(0, N_NODES, 512)]
        stats, mv = sb("stats", [P, len(pieces), 6]), sb("mv", [P, 2])
        scale = sb("scale", [P, 1])
        p_in, d_, var_ready, root = sem("p_in"), sem("d"), sem("var_ready"), sem("root")
        block = block_()

        @block.sync
        def _(sp):
            with nc.allow_non_contiguous_dma(reason="a number a partition"):
                for k, v in enumerate((b, gamma, beta)):
                    sp.dma_start(par[:, k:k + 1], v.unsqueeze(1)).then_inc(p_in, 16)

        @block.vector
        def _(dve):
            v = nc.vector
            step = Chain(dve, d_)
            dve.wait_ge(p_in, 48)
            if l == 0:
                step(v.tensor_scalar(m.lastT[:, :], m.hT[:, :], par[:, 0:1], None, ALU.add))
            else:
                step(v.scalar_tensor_tensor(m.lastT[:, :], m.hT[:, :], par[:, 0:1], m.lastT[:, :], ALU.add, ALU.add))
            for k, (s, e) in enumerate(pieces):
                step(v.bn_stats(stats[:, k, :], m.lastT[:, s:e]))
            step(v.bn_aggr(mv[:, :], stats[:, :, :].rearrange("p k s -> p (k s)")))
            v.tensor_scalar(scale[:, :], mv[:, 1:2], EPS, None, ALU.add).then_inc(var_ready, 1)
            dve.wait_ge(root, 1)
            step(v.reciprocal(scale[:, :], scale[:, :]))
            step(v.tensor_tensor(scale[:, :], scale[:, :], par[:, 1:2], ALU.mult))
            step(v.tensor_scalar(m.hT[:, :], m.lastT[:, :], mv[:, 0:1], scale[:, 0:1], ALU.subtract, ALU.mult))
            step(v.tensor_scalar(m.hT[:, :], m.hT[:, :], par[:, 2:3], 0.0, ALU.add, ALU.max))

        @block.scalar
        def _(act):
            act.wait_ge(var_ready, 1)
            nc.scalar.activation(scale[:, :], scale[:, :], ACT.Sqrt).then_inc(root, 1)


def rgcn_table(nc, m, rel_weights):
    with phase(nc) as (sb, ps, sem, block_):
        w = sb("w", [P, N_RELS, D])
        rows = sb("rows", [P, 2, N_RELS, D])
        psum = ps("rel", [P, 2, 4, 512])
        w_in, done, taken = sem("w_in"), sem("done"), sem("taken")
        out = [sem("out0"), sem("out1")]
        block = block_()
        table = m.rel_dram.rearrange("(r t p) f -> t p r f", r=N_RELS, p=P)

        @block.sync
        def _(sp):
            sp.dma_start(w[:, :, :], rel_weights.rearrange("r i h -> i r h")).then_inc(w_in, 16)
            for t in range(NT):
                sp.wait_ge(taken, 4 * (t + 1))
                sp.dma_start(table[t], rows[:, t % 2, :, :]).then_inc(out[t % 2], 16)
            for k in range(2):
                sp.wait_ge(out[k], 16 * ((NT + 1 - k) // 2))

        @block.tensor
        def _(pe):
            pe.wait_ge(w_in, 16)
            for t in range(NT):
                for g in range(4):
                    if t >= 2:
                        pe.wait_ge(taken, 4 * (t - 2) + g + 1)
                    nc.tensor.matmul(psum[:, t % 2, g, :], m.hT[:, t * P:(t + 1) * P],
                                     w[:, 4 * g:4 * g + 4, :].rearrange("p r f -> p (r f)"), start=True, stop=True).then_inc(done, 1)

        @block.scalar
        def _(act):
            for t in range(NT):
                if t >= 2:
                    act.wait_ge(out[t % 2], 16 * (t // 2))
                for g in range(4):
                    act.wait_ge(done, 4 * t + g + 1)
                    nc.scalar.activation(rows[:, t % 2, 4 * g:4 * g + 4, :].rearrange("p r f -> p (r f)"),
                                         psum[:, t % 2, g, :], ACT.Copy).then_inc(taken, 1)


def rgcn_finish(nc, m, b_lin, out_dram):
    with phase(nc) as (sb, ps, sem, block_):
        b_row = sb("b_row", [P, D])
        b_in, d_, ready, tanhed, final, out = (sem(n) for n in ("b_in", "d", "ready", "tanhed", "final", "out"))
        block = block_()

        @block.sync
        def _(sp):
            sp.dma_start(b_row[:, :], row_of(b_lin)).then_inc(b_in, 16)
            sp.wait_ge(final, 1)
            sp.dma_start(out_dram[0:(NT - 1) * P, :].rearrange("(t p) f -> p t f", p=P), m.x[:, 0:NT - 1, :]).then_inc(out, 16)
            sp.dma_start(out_dram[(NT - 1) * P:, :], m.x[0:LAST_ROWS, NT - 1, :]).then_inc(out, 16)
            sp.wait_ge(out, 32)

        @block.vector
        def _(dve):
            v = nc.vector
            step = Chain(dve, d_)
            step(v.tensor_tensor(m.acc[:, :, 0:D], m.acc[:, :, 0:D], bc(m.cnt_inv[:, :], D), ALU.mult))
            step(v.tensor_tensor(m.acc[:, :, 0:D], m.acc[:, :, 0:D], m.acc2[:, :, 0:D], ALU.add))
            dve.wait_ge(b_in, 16)
            v.tensor_tensor(m.acc[:, :, 0:D], m.acc[:, :, 0:D], mid(b_row[:, :], NT), ALU.add).then_inc(ready, 1)
            dve.wait_ge(tanhed, 1)
            v.tensor_tensor(m.x[:, :, :], m.x[:, :, :], m.acc[:, :, 0:D], ALU.add).then_inc(final, 1)

        @block.scalar
        def _(act):
            act.wait_ge(ready, 1)
            nc.scalar.activation(m.acc[:, :, 0:D], m.acc[:, :, 0:D], ACT.Tanh).then_inc(tanhed, 1)


class Memory:
    pass


def gnn_kernel(nc, a, out_dram):
    m = Memory()
    with ExitStack() as ctx:
        def sb(name, shape, dt=FP32):
            return ctx.enter_context(nc.sbuf_tensor(name, shape, dt))

        m.iota, m.ident = sb("iota", [P, P]), sb("ident", [P, P])
        m.pcol = sb("pcol", [P, 1])
        m.beta, m.eps1 = sb("beta", [P, 1]), sb("eps1", [P, 1])
        m.x, m.h = sb("x", [P, NT, D]), sb("h", [P, NT, D])
        m.acc, m.acc2 = sb("acc", [P, NT, GROW]), sb("acc2", [P, NT, GROW3])
        m.dinv, m.cnt_inv = sb("dinv", [P, NT]), sb("cnt_inv", [P, NT])
        m.src_pair, m.rel_pair = sb("src_pair", [P, NPP], I32), sb("rel_pair", [P, NPP], I32)
        m.loc_pair, m.w1 = sb("loc_pair", [P, NPP]), sb("w1", [P, NPP, 2])
        m.tile_row = sb("tile_row", [1, NPP], I32)
        m.fresh = sb("fresh", [P, NPP])
        m.end_row = sb("end_row", [1, P], I32)
        m.word_row = sb("word_row", [1, 1 + NPP // G], I32)
        m.stage = sb("stage", [P, U], I32)

        def dram(name, shape, dt=FP32):
            return nc.dram_tensor(name, shape, dt, kind="Internal").ap()

        m.rec_dram = dram("rec_dram", [NPP, 4 * P])
        m.bits_dram, m.values_dram = dram("bits_dram", [BITS, NPP * P], BF16), dram("values_dram", [3, NPP * P], BF16)
        m.l0_dram, m.gat_dram = dram("l0_dram", [NPAD, L0_ROW]), dram("gat_dram", [NPAD, GROW3])
        m.rows_dram, m.rel_dram = dram("rows_dram", [NPAIRS_PAD * P, GROW]), dram("rel_dram", [N_RELS * NPAD, D])
        m.gcn_dram = [dram(f"gcn_dram{l}", [NPAD, D]) for l in range(3)]
        m.tile_dram, m.end_dram = dram("tile_dram", [NPP], I32), dram("end_dram", [P], I32)

        with ExitStack() as early:
            def sb0(name, shape):
                return early.enter_context(nc.sbuf_tensor(name, shape, FP32))

            m.src_col, m.ev_col, m.hi_col, m.lo_col = (sb0(n, [P, NPP]) for n in ("src_col", "ev_col", "hi_col", "lo_col"))
            m.ev_pair = sb0("ev_pair", [P, NPP])
            m.seg_max, m.seg_sum = sb0("seg_max", [P, NT]), sb0("seg_sum", [P, NT])
            setup(nc, a, m)
            source_softmax(nc, m)
            layernorm_relu(nc, m, m.h)
            l0_table(nc, m)
            edge_sum(nc, m, m.l0_dram, index=m.src_pair, mode="source")
            l0_finish(nc, m)

        m.hT = sb("hT", [P, NPAD])
        with ExitStack() as middle:
            def sb1(name, shape):
                return middle.enter_context(nc.sbuf_tensor(name, shape, FP32))

            m.a_src, m.a_dst, m.top, m.own = (sb1(n, [P, NT, HEADS]) for n in ("a_src", "a_dst", "top", "own"))
            m.am = sb1("am", [P, NT, 2 * HEADS])
            m.as_pair, m.ex_pair = sb1("as_pair", [P, NPP * HEADS]), sb1("ex_pair", [P, NPP * HEADS])
            m.am_pair = sb1("am_pair", [P, (G + NPAIRS_PAD) * 2 * HEADS])
            layernorm_relu(nc, m, m.h)
            gat_layer(nc, m, a["L1_gnn_W1"], a["L1_gnn_att_src1"], a["L1_gnn_att_dst1"], a["L1_gnn_b1"])
            gat_layer(nc, m, a["L1_gnn_W2"], a["L1_gnn_att_src2"], a["L1_gnn_att_dst2"], a["L1_gnn_b2"])
            add_to_x(nc, m, m.h[:, :, :])

        with ExitStack() as late:
            m.lastT = late.enter_context(nc.sbuf_tensor("lastT", [P, NPAD], FP32))
            layernorm_relu(nc, m, m.h)
            flip_nodes(nc, m, m.h, m.hT)
            for l in range(3):
                gcn_layer(nc, m, l, a["L2_gnn_W"][l], a["L2_gnn_b"][l], a["L2_gnn_gamma"][l], a["L2_gnn_beta"][l])
            flip_nodes(nc, m, m.hT[:, :].rearrange("p (t n) -> p t n", t=NT), m.h[:, :, :].rearrange("p t f -> p (t f)"))
            add_to_x(nc, m, m.h[:, :, :])

        layernorm_relu(nc, m, m.h)
        flip_nodes(nc, m, m.h, m.hT)
        rgcn_table(nc, m, a["L3_gnn_rel_weights"])
        project(nc, m, a["L3_gnn_w_lin"], m.acc2)
        edge_sum(nc, m, m.rel_dram, index=m.rel_pair)
        rgcn_finish(nc, m, a["L3_gnn_b_lin"], out_dram)


_INS = ['x', 'src', 'dst', 'edge_type_16', 'edge_weight', 'L0_gnn_beta', 'L0_gnn_eps', 'L1_gnn_W1', 'L1_gnn_att_src1',
        'L1_gnn_att_dst1', 'L1_gnn_b1', 'L1_gnn_W2', 'L1_gnn_att_src2', 'L1_gnn_att_dst2', 'L1_gnn_b2', 'L2_gnn_W',
        'L2_gnn_b', 'L2_gnn_gamma', 'L2_gnn_beta', 'L3_gnn_rel_weights', 'L3_gnn_w_lin', 'L3_gnn_b_lin']


def kernel(**inputs):
    import numpy as _np
    import concourse.bacc as _bacc
    from concourse import mybir as _mybir
    from concourse.bass_utils import run_bass_kernel_spmd as _run

    nc = _bacc.Bacc("TRN2", target_bir_lowering=False, num_devices=1)
    arrays, args = {}, {}
    for name in _INS:
        v = _np.ascontiguousarray(inputs[name])
        arrays[f"in_{name}"] = v
        args[name] = nc.dram_tensor(f"in_{name}", v.shape, _mybir.dt.from_np(v.dtype), kind="ExternalInput").ap()
    out = nc.dram_tensor("out_x", (N_NODES, D), FP32, kind="ExternalOutput").ap()
    gnn_kernel(nc, args, out)
    r = _run(nc, [arrays], core_ids=[0])
    return r.results[0]["out_x"]
```
